# Optimizing a Trainium2 kernel written in Bass

```python
import numpy as np
import jax
import jax.numpy as jnp

def _softmax(x, axis=-1):
    return jax.nn.softmax(x, axis=axis)
def _gelu(x):
    return jax.nn.gelu(x, approximate=True)
def _silu(x):
    return jax.nn.silu(x)
def _sigmoid(x):
    return jax.nn.sigmoid(x)
def _layernorm(x, axis=-1, eps=1e-5):
    m = jnp.mean(x, axis=axis, keepdims=True)
    v = jnp.var(x, axis=axis, keepdims=True)
    return (x - m) / jnp.sqrt(v + eps)
def _scatter_add(tgt, idx, src, axis=0):
    return tgt.at[idx].add(src)
def _segment_sum(src, seg, n):
    return jax.ops.segment_sum(src, seg, n)

kernel_name = 'mk_conv_attn_hybrid_d2_conv_nhwc256_d38311'

def setup_inputs(seed: int = 0):
    np.random.seed(seed)
    _w = jnp.asarray
    def _rec_inputs():
        import jax
        import jax.numpy as jnp
        _gk = jax.random.key(seed)
        x = -0.000929 + 1 * jax.random.normal(jax.random.fold_in(_gk, 1), (4, 32, 32, 256), jnp.float32)
        return x
    x = _rec_inputs()
    def _L0_conv_setup():
        import jax, jax.numpy as jnp
        import numpy as np
        KSIZE = 7
        HEADS = 8
        DIM = 256
        HID = int(DIM * 4.0)
        LEVELS = 8

        def _ln(x, w, b, eps=1e-05):
            m = x.mean(-1, keepdims=True)
            v = ((x - m) ** 2).mean(-1, keepdims=True)
            return (x - m) * jax.lax.rsqrt(v + eps) * w + b

        def _na2d(x, qkv_w, qkv_b, rpb, proj_w, proj_b, num_heads=HEADS, k=KSIZE):
            B, H, W, C = x.shape
            hd = C // num_heads
            qkv = (x @ qkv_w.T + qkv_b).reshape(B, H, W, 3, num_heads, hd)
            q, kk, v = (qkv[..., 0, :, :], qkv[..., 1, :, :], qkv[..., 2, :, :])
            start_h = jnp.clip(jnp.arange(H) - k // 2, 0, H - k)
            start_w = jnp.clip(jnp.arange(W) - k // 2, 0, W - k)
            idx_h = start_h[:, None] + jnp.arange(k)
            idx_w = start_w[:, None] + jnp.arange(k)
            Kn = jnp.take(jnp.take(kk, idx_h, axis=1), idx_w, axis=3)
            Kn = Kn.transpose(0, 1, 3, 5, 2, 4, 6)
            Vn = jnp.take(jnp.take(v, idx_h, axis=1), idx_w, axis=3)
            Vn = Vn.transpose(0, 1, 3, 5, 2, 4, 6)
            scale = hd ** (-0.5)
            attn = jnp.einsum('bijhd,bijhkld->bijhkl', q * scale, Kn)
            bidx_h = idx_h - jnp.arange(H)[:, None] + (k - 1)
            bidx_w = idx_w - jnp.arange(W)[:, None] + (k - 1)
            bias = rpb[:, bidx_h]
            bias = bias[..., bidx_w]
            bias = bias.transpose(1, 3, 0, 2, 4)
            attn = attn + bias[None]
            a = jax.nn.softmax(attn.reshape(B, H, W, num_heads, k * k), axis=-1)
            a = a.reshape(attn.shape)
            out = jnp.einsum('bijhkl,bijhkld->bijhd', a, Vn).reshape(B, H, W, C)
            return out @ proj_w.T + proj_b
        key = jax.random.key(seed)
        ks = jax.random.split(key, 12)
        B, H, W, C = (4, 32, 32, DIM)
        s = 0.02
        return {'x': jax.random.normal(ks[0], (B, H, W, C), jnp.float32), 'norm1_w': jnp.ones((C,), jnp.float32), 'norm1_b': jnp.zeros((C,), jnp.float32), 'qkv_w': jax.random.normal(ks[1], (3 * C, C), jnp.float32) * s, 'qkv_b': jnp.zeros((3 * C,), jnp.float32), 'rpb': jax.random.normal(ks[2], (HEADS, 2 * KSIZE - 1, 2 * KSIZE - 1), jnp.float32) * s, 'proj_w': jax.random.normal(ks[3], (C, C), jnp.float32) * s, 'proj_b': jnp.zeros((C,), jnp.float32), 'norm2_w': jnp.ones((C,), jnp.float32), 'norm2_b': jnp.zeros((C,), jnp.float32), 'fc1_w': jax.random.normal(ks[4], (HID, C), jnp.float32) * s, 'fc1_b': jnp.zeros((HID,), jnp.float32), 'fc2_w': jax.random.normal(ks[5], (C, HID), jnp.float32) * s, 'fc2_b': jnp.zeros((C,), jnp.float32), 'gamma_1': jnp.ones((LEVELS, C), jnp.float32), 'gamma_2': jnp.ones((LEVELS, C), jnp.float32), 'quality': 5}
    _L0_conv_all = _L0_conv_setup()
    _L0_conv_in = {k: v for k, v in _L0_conv_all.items() if k in ('norm1_w', 'norm1_b', 'qkv_w', 'qkv_b', 'rpb', 'proj_w', 'proj_b', 'norm2_w', 'norm2_b', 'fc1_w', 'fc1_b', 'fc2_w', 'fc2_b', 'gamma_1', 'gamma_2', )}
    del _L0_conv_all

    def _L1_attn_setup():
        import jax, jax.numpy as jnp
        import numpy as np
        H = 8
        LN_EPS = 1e-05
        key = jax.random.key(seed)
        ks = jax.random.split(key, 12)
        B, N, D = (1, 4096, 256)
        E = 65536
        x = jax.random.normal(ks[0], (B, N, D), dtype=jnp.float32)
        src = jax.random.randint(ks[1], (E,), 0, N)
        dst = jax.random.randint(ks[2], (E,), 0, N)
        loop = jnp.arange(N)
        edge_index = jnp.stack([jnp.concatenate([src, loop]), jnp.concatenate([dst, loop])]).astype(jnp.int64)
        s = 1.0 / np.sqrt(D)
        Wq = jax.random.normal(ks[3], (D, D), dtype=jnp.float32) * s
        Wk = jax.random.normal(ks[4], (D, D), dtype=jnp.float32) * s
        Wv = jax.random.normal(ks[5], (D, D), dtype=jnp.float32) * s
        Wo = jax.random.normal(ks[6], (D, D), dtype=jnp.float32) * s
        bq = jax.random.normal(ks[7], (D,), dtype=jnp.float32) * 0.01
        bk = jax.random.normal(ks[8], (D,), dtype=jnp.float32) * 0.01
        bv = jax.random.normal(ks[9], (D,), dtype=jnp.float32) * 0.01
        bo = jax.random.normal(ks[10], (D,), dtype=jnp.float32) * 0.01
        gamma = jnp.ones((D,), dtype=jnp.float32)
        beta = jnp.zeros((D,), dtype=jnp.float32)
        return {'x': x, 'edge_index': edge_index, 'Wq': Wq, 'bq': bq, 'Wk': Wk, 'bk': bk, 'Wv': Wv, 'bv': bv, 'Wo': Wo, 'bo': bo, 'gamma': gamma, 'beta': beta}
    _L1_attn_all = _L1_attn_setup()
    _L1_attn_in = {k: v for k, v in _L1_attn_all.items() if k in ('edge_index', 'Wq', 'bq', 'Wk', 'bk', 'Wv', 'bv', 'Wo', 'bo', 'gamma', 'beta', )}
    del _L1_attn_all

    def _L1_ffn_setup():
        import jax, jax.numpy as jnp
        import numpy as np
        N_EXPERTS = 8
        TOP_K = 2
        key = jax.random.key(seed)
        ks = jax.random.split(key, 5)
        B, T, C, E, H = (8, 2048, 256, 8, 682)
        scale = 1.0 / np.sqrt(C)
        return {'x': jax.random.normal(ks[0], (B, T, C), dtype=jnp.float32), 'router_w': jax.random.normal(ks[1], (E, C), dtype=jnp.float32) * scale, 'w1': jax.random.normal(ks[2], (E, H, C), dtype=jnp.float32) * scale, 'w2': jax.random.normal(ks[3], (E, C, H), dtype=jnp.float32) * (1.0 / np.sqrt(H)), 'w3': jax.random.normal(ks[4], (E, H, C), dtype=jnp.float32) * scale}
    _L1_ffn_all = _L1_ffn_setup()
    _L1_ffn_in = {k: v for k, v in _L1_ffn_all.items() if k in ('router_w', 'w1', 'w2', 'w3', )}
    del _L1_ffn_all

    return {
        "x": x,
        "L0_conv_norm1_w": _L0_conv_in["norm1_w"],
        "L0_conv_norm1_b": _L0_conv_in["norm1_b"],
        "L0_conv_qkv_w": _L0_conv_in["qkv_w"],
        "L0_conv_qkv_b": _L0_conv_in["qkv_b"],
        "L0_conv_rpb": _L0_conv_in["rpb"],
        "L0_conv_proj_w": _L0_conv_in["proj_w"],
        "L0_conv_proj_b": _L0_conv_in["proj_b"],
        "L0_conv_norm2_w": _L0_conv_in["norm2_w"],
        "L0_conv_norm2_b": _L0_conv_in["norm2_b"],
        "L0_conv_fc1_w": _L0_conv_in["fc1_w"],
        "L0_conv_fc1_b": _L0_conv_in["fc1_b"],
        "L0_conv_fc2_w": _L0_conv_in["fc2_w"],
        "L0_conv_fc2_b": _L0_conv_in["fc2_b"],
        "L0_conv_gamma_1": _L0_conv_in["gamma_1"],
        "L0_conv_gamma_2": _L0_conv_in["gamma_2"],
        "L1_attn_edge_index": _L1_attn_in["edge_index"],
        "L1_attn_Wq": _L1_attn_in["Wq"],
        "L1_attn_bq": _L1_attn_in["bq"],
        "L1_attn_Wk": _L1_attn_in["Wk"],
        "L1_attn_bk": _L1_attn_in["bk"],
        "L1_attn_Wv": _L1_attn_in["Wv"],
        "L1_attn_bv": _L1_attn_in["bv"],
        "L1_attn_Wo": _L1_attn_in["Wo"],
        "L1_attn_bo": _L1_attn_in["bo"],
        "L1_attn_gamma": _L1_attn_in["gamma"],
        "L1_attn_beta": _L1_attn_in["beta"],
        "L1_ffn_router_w": _L1_ffn_in["router_w"],
        "L1_ffn_w1": _L1_ffn_in["w1"],
        "L1_ffn_w2": _L1_ffn_in["w2"],
        "L1_ffn_w3": _L1_ffn_in["w3"],
    }

def reference(x, L0_conv_norm1_w, L0_conv_norm1_b, L0_conv_qkv_w, L0_conv_qkv_b, L0_conv_rpb, L0_conv_proj_w, L0_conv_proj_b, L0_conv_norm2_w, L0_conv_norm2_b, L0_conv_fc1_w, L0_conv_fc1_b, L0_conv_fc2_w, L0_conv_fc2_b, L0_conv_gamma_1, L0_conv_gamma_2, L1_attn_edge_index, L1_attn_Wq, L1_attn_bq, L1_attn_Wk, L1_attn_bk, L1_attn_Wv, L1_attn_bv, L1_attn_Wo, L1_attn_bo, L1_attn_gamma, L1_attn_beta, L1_ffn_router_w, L1_ffn_w1, L1_ffn_w2, L1_ffn_w3):
    import jax
    import jax.numpy as jnp
    def _L0_conv_ref(x, norm1_w, norm1_b, qkv_w, qkv_b, rpb, proj_w, proj_b, norm2_w, norm2_b, fc1_w, fc1_b, fc2_w, fc2_b, gamma_1, gamma_2, quality):
        import jax, jax.numpy as jnp
        import numpy as np
        KSIZE = 7
        HEADS = 8
        DIM = 256
        HID = int(DIM * 4.0)
        LEVELS = 8

        def _ln(x, w, b, eps=1e-05):
            m = x.mean(-1, keepdims=True)
            v = ((x - m) ** 2).mean(-1, keepdims=True)
            return (x - m) * jax.lax.rsqrt(v + eps) * w + b

        def _na2d(x, qkv_w, qkv_b, rpb, proj_w, proj_b, num_heads=HEADS, k=KSIZE):
            B, H, W, C = x.shape
            hd = C // num_heads
            qkv = (x @ qkv_w.T + qkv_b).reshape(B, H, W, 3, num_heads, hd)
            q, kk, v = (qkv[..., 0, :, :], qkv[..., 1, :, :], qkv[..., 2, :, :])
            start_h = jnp.clip(jnp.arange(H) - k // 2, 0, H - k)
            start_w = jnp.clip(jnp.arange(W) - k // 2, 0, W - k)
            idx_h = start_h[:, None] + jnp.arange(k)
            idx_w = start_w[:, None] + jnp.arange(k)
            Kn = jnp.take(jnp.take(kk, idx_h, axis=1), idx_w, axis=3)
            Kn = Kn.transpose(0, 1, 3, 5, 2, 4, 6)
            Vn = jnp.take(jnp.take(v, idx_h, axis=1), idx_w, axis=3)
            Vn = Vn.transpose(0, 1, 3, 5, 2, 4, 6)
            scale = hd ** (-0.5)
            attn = jnp.einsum('bijhd,bijhkld->bijhkl', q * scale, Kn)
            bidx_h = idx_h - jnp.arange(H)[:, None] + (k - 1)
            bidx_w = idx_w - jnp.arange(W)[:, None] + (k - 1)
            bias = rpb[:, bidx_h]
            bias = bias[..., bidx_w]
            bias = bias.transpose(1, 3, 0, 2, 4)
            attn = attn + bias[None]
            a = jax.nn.softmax(attn.reshape(B, H, W, num_heads, k * k), axis=-1)
            a = a.reshape(attn.shape)
            out = jnp.einsum('bijhkl,bijhkld->bijhd', a, Vn).reshape(B, H, W, C)
            return out @ proj_w.T + proj_b
        s = int(quality) - 1
        l = float(quality % 1)
        if s == LEVELS - 1:
            g1 = jnp.abs(gamma_1[s])
            g2 = jnp.abs(gamma_2[s])
        else:
            g1 = jnp.abs(gamma_1[s]) ** (1 - l) * jnp.abs(gamma_1[s + 1]) ** l
            g2 = jnp.abs(gamma_2[s]) ** (1 - l) * jnp.abs(gamma_2[s + 1]) ** l
        shortcut = x
        h = _ln(x, norm1_w, norm1_b)
        h = g1 * _na2d(h, qkv_w, qkv_b, rpb, proj_w, proj_b)
        x = shortcut + h
        m = _ln(x, norm2_w, norm2_b)
        m = jax.nn.gelu(m @ fc1_w.T + fc1_b, approximate=False)
        m = m @ fc2_w.T + fc2_b
        return x + g2 * m

    def _L1_attn_ref(x, edge_index, Wq, bq, Wk, bk, Wv, bv, Wo, bo, gamma, beta):
        import jax, jax.numpy as jnp
        import numpy as np
        H = 8
        LN_EPS = 1e-05
        B, N, D = x.shape
        hd = D // H

        def proj(W, b):
            return (x @ W + b).reshape(B, N, H, hd).transpose(0, 2, 1, 3)
        Q, K, V = (proj(Wq, bq), proj(Wk, bk), proj(Wv, bv))
        scores = jnp.einsum('bhnd,bhmd->bhnm', Q, K) / jnp.sqrt(jnp.float32(hd))
        mask = jnp.zeros((N, N), dtype=bool).at[edge_index[0], edge_index[1]].set(True)
        scores = jnp.where(mask[None, None], scores, -jnp.inf)
        attn = jax.nn.softmax(scores, axis=-1)
        attended = jnp.einsum('bhnm,bhmd->bhnd', attn, V)
        attended = attended.transpose(0, 2, 1, 3).reshape(B, N, D)
        out = attended @ Wo + bo
        y = x + out
        mu = jnp.mean(y, axis=-1, keepdims=True)
        var = jnp.mean((y - mu) ** 2, axis=-1, keepdims=True)
        return (y - mu) / jnp.sqrt(var + LN_EPS) * gamma + beta

    def _L1_ffn_ref(x, router_w, w1, w2, w3):
        import jax, jax.numpy as jnp
        import numpy as np
        N_EXPERTS = 8
        TOP_K = 2
        B, T, C = x.shape
        flat = x.reshape(-1, C)
        logits = flat @ router_w.T
        probs = jax.nn.softmax(logits, axis=-1)
        topk_probs, topk_idx = jax.lax.top_k(probs, TOP_K)
        topk_probs = topk_probs / (jnp.sum(topk_probs, axis=-1, keepdims=True) + 1e-09)
        onehot = jax.nn.one_hot(topk_idx, N_EXPERTS, dtype=flat.dtype)
        gates = jnp.einsum('nk,nke->ne', topk_probs, onehot)
        h1 = jnp.einsum('nc,ehc->neh', flat, w1)
        h3 = jnp.einsum('nc,ehc->neh', flat, w3)
        h = jax.nn.silu(h1) * h3
        y = jnp.einsum('neh,ech->nec', h, w2)
        out = jnp.einsum('ne,nec->nc', gates, y)
        return out.reshape(B, T, C)

    def _gn(v, G=32, eps=1e-5):
        B_, H_, W_, C_ = v.shape
        g = v.reshape(B_, H_, W_, G, C_ // G)
        m = jnp.mean(g, axis=(1, 2, 4), keepdims=True)
        s = jnp.var(g, axis=(1, 2, 4), keepdims=True)
        return ((g - m) / jnp.sqrt(s + eps)).reshape(v.shape)

    def _ln_c(v, eps=1e-6):
        m = jnp.mean(v, axis=-1, keepdims=True)
        s = jnp.var(v, axis=-1, keepdims=True)
        return (v - m) / jnp.sqrt(s + eps)

    def _ln_t(v, eps=1e-5):
        m = jnp.mean(v, axis=-1, keepdims=True)
        s = jnp.var(v, axis=-1, keepdims=True)
        return (v - m) / jnp.sqrt(s + eps)

    def _to_tokens(v):
        B_, H_, W_, C_ = v.shape
        return v.reshape(B_, H_ * W_, C_)
    def _from_tokens(t, like):
        return t.reshape(like.shape)

    x = _L0_conv_ref(x, L0_conv_norm1_w, L0_conv_norm1_b, L0_conv_qkv_w, L0_conv_qkv_b, L0_conv_rpb, L0_conv_proj_w, L0_conv_proj_b, L0_conv_norm2_w, L0_conv_norm2_b, L0_conv_fc1_w, L0_conv_fc1_b, L0_conv_fc2_w, L0_conv_fc2_b, L0_conv_gamma_1, L0_conv_gamma_2, 5)
    t = _to_tokens(x)
    t = t + _L1_attn_ref(_ln_t(t), L1_attn_edge_index, L1_attn_Wq, L1_attn_bq, L1_attn_Wk, L1_attn_bk, L1_attn_Wv, L1_attn_bv, L1_attn_Wo, L1_attn_bo, L1_attn_gamma, L1_attn_beta)
    t = t + _L1_ffn_ref(_ln_t(t), L1_ffn_router_w, L1_ffn_w1, L1_ffn_w2, L1_ffn_w3)
    x = _from_tokens(t, x)
    return x


_drawn_inputs = setup_inputs


def setup_inputs(seed=0):
    import zlib

    import numpy as np

    out = dict(_drawn_inputs(seed))
    spreads = {'L0_conv_norm1_w': (1.0, 0.6),
     'L0_conv_norm1_b': (0.0, 0.43),
     'L0_conv_qkv_b': (0.0, 0.1),
     'L0_conv_proj_b': (0.0, 0.1),
     'L0_conv_norm2_w': (1.0, 0.2),
     'L0_conv_norm2_b': (0.0, 0.357),
     'L0_conv_fc1_b': (0.0, 0.1),
     'L0_conv_fc2_b': (0.0, 0.1),
     'L0_conv_gamma_1': (1.0, 0.2),
     'L0_conv_gamma_2': (1.0, 0.2),
     'L1_attn_gamma': (1.0, 0.2),
     'L1_attn_beta': (0.0, 0.1)}
    factors = {'L0_conv_rpb': 44.06,
     'L1_attn_bq': 8.0,
     'L1_attn_bk': 64.0,
     'L1_attn_bv': 5.084,
     'L1_attn_bo': 7.446}
    for name, (base, spread) in spreads.items():
        noise = np.random.default_rng([zlib.crc32(name.encode()), seed]).standard_normal(out[name].shape)
        drawn = base * np.exp(spread * noise) if base else spread * noise
        out[name] = jnp.asarray(drawn.astype(out[name].dtype))
    for name, factor in factors.items():
        out[name] = (out[name] * factor).astype(out[name].dtype)
    return out
```

```python
from contextlib import ExitStack

import numpy as np

import concourse.bass as bass
from concourse import mybir

F32 = mybir.dt.float32
F32R = mybir.dt.float32r
BF16 = mybir.dt.bfloat16
I32 = mybir.dt.int32
ACT = mybir.ActivationFunctionType
ALU = mybir.AluOpType
AX = mybir.AxisListType

P = 128
BATCH, SIDE, C, HEADS, HD = 4, 32, 256, 8, 32
N = SIDE * SIDE
TOK = BATCH * N
KC = C // P
QT = N // P
TILES = TOK // P
HID = 4 * C
HCH = HID // P
KWIN = 7
ROWS = P // SIDE
WT = 3
WK = WT * P
EXPERTS = 8
FF = 682
FCH = 6
FCW = 114
HALF = FF // 2
SLOTS = 2 * TOK
MT = 72
CHUNKS = BATCH
EDGES = 69632
ECOL = EDGES // P
COPIES = 4
EBATCH = 16
CELLS = N * N
BIG = 3.0e38
NO_EDGE = 2.0 ** 31
SCALE = float(HD) ** -0.5
BANK = 512
FLOOR_TILES = (SLOTS + EXPERTS * (P - 1)) // P
assert FLOOR_TILES <= MT and ECOL % EBATCH == 0 and FCH * FCW >= FF


def build_program(nc, x, rpb_toeplitz, window_mask, cols, rows, w_qkv0, w_proj0, w_fc1, w_fc2,
                  w_qkv1, w_o1, w_router, edges, w13, w2, route_const, out):
    ctx = ExitStack()
    base = (nc.sbuf_base + 63) // 64 * 64
    place = {"at": base}

    def sb(name, shape, dt, at=None):
        size = 4 if dt in (F32, F32R, I32) else 2
        n = int(np.prod(shape[1:])) * size
        if at is None:
            at = place["at"]
            place["at"] = (at + n + 31) // 32 * 32
        return nc.alloc_sbuf_tensor_at(name, list(shape), dt, offset=at)

    def dram(name, shape, dt):
        return nc.dram_tensor(name, list(shape), dt, kind="Internal").ap()

    def sem(name):
        return ctx.enter_context(nc.semaphore(name))


    ident = sb("ident", [P, P], F32)
    zeros = sb("zeros", [P, C], F32)
    col = sb("col", [P, cols.shape[1]], F32)
    row = sb("row", [P, rows.shape[0] * C], F32)
    edge_at = sb("edge_at", [P, ECOL], I32)
    edge_slot = sb("edge_slot", [P, EBATCH], I32)
    stats = sb("stats", [P, QT, 6], F32)
    mv = sb("mv", [P, QT, 2], F32)
    nwt = sb("nwt", [P, 3, QT], F32)
    nwi = sb("nwi", [P, QT], I32)
    nmax = sb("nmax", [P, 2], F32)
    rsum = sb("rsum", [P, 2, HEADS], F32)
    rinv = sb("rinv", [P, 4], F32)
    rexp = sb("rexp", [P, 2, P], F32)
    rT = sb("rT", [P, 2, P], F32)
    oTn = sb("oTn", [P, 2, KC, P], F32)
    wo1 = sb("wo1", [P, KC, C], F32)
    wr = sb("wr", [P, KC, EXPERTS], F32)
    at_w0 = place["at"]
    wq0 = sb("wq0", [P, KC, 3 * C], F32)
    wp0 = sb("wp0", [P, KC, C], F32)
    wf1 = sb("wf1", [P, KC, HID], F32)
    wf2 = sb("wf2", [P, HCH, C], F32)
    wq1 = sb("wq1", [P, KC, 3 * C], F32, at=at_w0)
    at_bias = place["at"]
    bias = sb("bias", [P, 3, HEADS, WK], F32)
    mask = sb("mask", [P, QT, N], BF16, at=at_bias)
    mask_tile = sb("mask_tile", [P, 2, N], BF16, at=at_bias + 2 * QT * N)
    at_att = place["at"]
    pT = sb("pT", [P, HEADS, N], F32)
    pT0 = sb("pT0", [P, HEADS, WK], F32, at=at_att)
    xh = sb("xh", [P, QT, C], F32, at=at_att)
    hT = sb("hT", [P, KC, N], F32, at=at_att + 8192)
    k_hi = sb("k_hi", [P, KC, N], F32R, at=at_att + 16384)
    k_lo = sb("k_lo", [P, KC, N], F32R, at=at_att + 24576)
    at_k = place["at"]
    kst = sb("kst", [P, HEADS, N], F32R)
    toep = sb("toep", [P, 20, HEADS, SIDE], F32, at=at_k)
    qst = sb("qst", [P, 2, HEADS, P], F32R)
    q_pair = [sb("q_pair_a", [P, HEADS, 2 * P], F32R, at=place["at"] - 8192),
              sb("q_pair_b", [P, HEADS, 2 * P], F32R, at=at_att + 16384)]
    at_q = place["at"]
    q_hi = sb("q_hi", [P, KC, N], F32R)
    q_lo = sb("q_lo", [P, KC, N], F32R)
    vt = sb("vt", [P, QT, C], F32)
    at_m = place["at"]
    msc = sb("msc", [P, 2, N], F32)
    prob = sb("prob", [P, 2, N], F32)
    big = sb("big", [P, 2048], BF16, at=at_m - 8192)
    e_src = sb("e_src", [P, ECOL], I32, at=at_m + 4096)
    e_dst = sb("e_dst", [P, ECOL], I32, at=at_m + 6272)
    e_tmp = sb("e_tmp", [P, ECOL], F32, at=at_m + 8448)
    wmask = sb("wmask", [P, 3, WK], F32, at=at_m + 10624)
    mcopy = sb("mcopy", [P, 2, COPIES, N], BF16, at=at_m)
    at_xb = place["at"]
    xb = sb("xb", [P, QT, C], F32)
    res = sb("res", [P, QT, C], F32)
    assert place["at"] <= nc.sbuf_usable_end

    ps = nc.alloc_psum_tensor("ps", [P, 8, BANK], F32)

    x1_d = dram("x1_d", [TOK, C], F32)
    x2_d = dram("x2_d", [TOK, C], F32)
    y_d = dram("y_d", [TOK, C], F32)
    mask_d = dram("mask_d", [COPIES * CELLS, 1], BF16)
    t2_d = dram("t2_d", [TOK, C], F32)
    xs_d = dram("xs_d", [MT * P, C], F32)
    y2_d = dram("y2_d", [MT * P, C], F32)

    def tiles(ap):
        return ap.rearrange("(n p) c -> p n c", p=P)

    NCOL = ["n1w", "n1b", "n2w", "n2b", "qb0", "kb0", "fb", "qb1", "kb1"]
    cw = {"fb": HCH}
    cat, at_c = {}, 0
    for nme in NCOL:
        cat[nme] = at_c
        at_c += cw.get(nme, KC)
    NROW = ["vb0", "pb0", "g1", "f2b", "g2", "vb1", "ob1", "gam", "bet"]
    rat = {nme: i for i, nme in enumerate(NROW)}

    def rowv(nme):
        return row[:, rat[nme] * C:(rat[nme] + 1) * C]

    def colv(nme, i):
        return col[:, cat[nme] + i:cat[nme] + i + 1]

    ld = sem("ld")
    ld_b = sem("ld_b")
    edge_ld = sem("edge_ld")
    prep_v = sem("prep_v")
    prep_p = sem("prep_p")
    chain = sem("chain")
    edge_ready = sem("edge_ready")
    big_ready = sem("big_ready")
    mask_init = sem("mask_init")
    slot_copy = sem("slot_copy")
    scat = [sem(f"scat{k}") for k in range(COPIES)]
    mask_in = [sem(f"mask_in{k}") for k in range(2)]
    mask_half = sem("mask_half")
    mask_ok = sem("mask_ok")
    ld_f = sem("ld_f")
    wf_ok = sem("wf_ok")
    bias_ok = sem("bias_ok")
    sp_passed, pool_passed, dve_passed = sem("sp_passed"), sem("pool_passed"), sem("dve_passed")
    links = [0]

    def link(ins):
        links[0] += 1
        ins.then_inc(chain, 1)
        nc.vector.wait_ge(chain, links[0])

    def relink():
        nc.vector.sem_clear(chain)
        links[0] = 0

    def rsqrt(n, mv=mv, nwt=nwt, nwi=nwi):
        v, y, t = nwt[:, 0, 0:n], nwt[:, 1, 0:n], nwt[:, 2, 0:n]
        link(nc.vector.tensor_scalar(v, mv[:, 0:n, 1], 1e-5, None, ALU.add))
        link(nc.vector.tensor_scalar(nwi[:, 0:n], v.bitcast(I32), 1, None, ALU.logical_shift_right))
        link(nc.vector.tensor_scalar(nwi[:, 0:n], nwi[:, 0:n], -1.0, float(0x5F3759DF), ALU.mult, ALU.add))
        g = nwi[:, 0:n].bitcast(F32)
        for _ in range(3):
            link(nc.vector.tensor_tensor(t, g, g, ALU.mult))
            link(nc.vector.tensor_tensor(t, t, v, ALU.mult))
            link(nc.vector.tensor_scalar(t, t, -0.5, 1.5, ALU.mult, ALU.add))
            link(nc.vector.tensor_tensor(y, g, t, ALU.mult))
            g = y

    class Attention:

        def __init__(self, n, src, dst, wqkv, wout, kw, local):
            self.n, self.src, self.dst, self.wqkv, self.wout = n, src, dst, wqkv, wout
            self.kw, self.local = kw, local
            self.nb = (kw + BANK - 1) // BANK
            self.kc = kw // P
            self.pT = pT0 if local else pT
            c = lambda s: sem(f"{s}{n}")
            self.x_in = c("x_in")
            self.x_norm = c("x_norm")
            self.hT_ps = c("hT_ps")
            self.hT_act = c("hT_act")
            self.hT_dve = c("hT_dve")
            self.res_ok = c("res_ok")
            self.proj_ps = c("proj_ps")
            self.proj_hi = c("proj_hi")
            self.proj_out = c("proj_out")
            self.k_staged = c("k_staged")
            self.q_staged = [c("q_staged_a"), c("q_staged_b")]
            self.qk = c("qk")
            self.masked = c("masked")
            self.exp = c("exp")
            self.p_ps = c("p_ps")
            self.p_act = c("p_act")
            self.p_dve = c("p_dve")
            self.r_exp = c("r_exp")
            self.pv = c("pv")
            self.r_act = c("r_act")
            self.o_norm = c("o_norm")
            self.wo_ps = c("wo_ps")
            self.wo_out = c("wo_out")
            self.stored = c("stored")
            self.mask_set = c("mask_set")

        def steps(self, g, s):
            return g * 16 + s

        def chunk(self, g, s, j):
            m = self.nb * s + j
            return m % 2, g * (8 * self.nb) + m // 2

        def key_tile(self, tp, u):
            return min(max(2 * tp + u - 1, 0), QT - WT) if self.local else 0

        def kind(self, tp, u):
            return {0: 0, QT - 1: 2}.get(2 * tp + u, 1)

        def loop(self, eng, b, prelude, pair, tail):
            prelude(b)
            pair(b * 4, 0, False)
            if self.local:
                for tp in range(1, QT // 2):
                    pair(b * 4 + tp, tp, True)
            else:
                with eng.Fori(1, QT // 2) as tp:
                    pair(b * 4 + tp, tp, True)
            tail(b * 4 + 4)

        def load(self, sp, b):
            sp.dma_start(xb[:, :, :], tiles(self.src)[:, bass.ds(b * QT, QT), :]).then_inc(self.x_in, 16)

        def sp(self, sp):
            sp.sem_inc(self.stored, 16)
            dst = tiles(self.dst)

            def stage_k(b):
                if self.local:
                    sp.wait_ge(bias_ok, 3)
                sp.wait_ge(self.proj_out, b * 12 + 4)
                sp.sem_inc(sp_passed, 1)
                sp.wait_ge(self.qk, b * 64 + 1)
                sp.sem_inc(sp_passed, 1)
                for r in range(4):
                    half = k_hi if r < 2 else k_lo
                    for j in range(4):
                        sp.dma_start(kst[32 * r:32 * r + 32, :, :].rearrange("p (c j) n -> p c j n", j=4)[:, :, j, :]
                                     .bitcast(F32), half[32 * j:32 * j + 32, :, :].bitcast(F32)).then_inc(self.k_staged, 16)

            def stage(g, tp, u):
                sp.wait_ge(self.qk, (g * 16 + 8 * (u - 1) if u else g * 16 - 8 if not isinstance(tp, int) or tp else g * 16) + 1)
                sp.sem_inc(sp_passed, 1)
                t = tp * 2 + u
                for r in range(4):
                    half = q_lo if r % 2 else q_hi
                    for j in range(4):
                        sp.dma_start(
                            qst[32 * r:32 * r + 32, u, :, :].rearrange("p (c j) n -> p c j n", j=4)[:, :, j, :]
                            .bitcast(F32), half[32 * j:32 * j + 32, :, bass.ds(t * P, P)].bitcast(F32)).then_inc(self.q_staged[u], 16)

            def stage_pair(g, tp):
                for r in range(4):
                    half = q_lo if r % 2 else q_hi
                    for j in range(4):
                        sp.dma_start(
                            q_pair[tp % 2][32 * r:32 * r + 32, :, :].rearrange("p (c j) n -> p c j n", j=4)[:, :, j, :]
                            .bitcast(F32), half[32 * j:32 * j + 32, :, tp * 2 * P:(tp + 1) * 2 * P].bitcast(F32))\
                          .then_inc(self.q_staged[tp % 2], 16)

            def store(g, tp, u):
                sp.wait_ge(self.wo_out, g * 2 + (u + 1) + 1)
                sp.sem_inc(sp_passed, 1)
                sp.dma_start(dst[:, bass.ds(g * 2 + u, 1), :], res[:, bass.ds(tp * 2 + u, 1), :])\
                  .then_inc(self.stored, 16)

            def batch(b, more):
                stage_k(b)
                sp.wait_ge(self.proj_out, b * 12 + 8)
                sp.sem_inc(sp_passed, 1)
                if self.local:
                    stage_pair(b * 4, 0)
                    sp.wait_ge(self.k_staged, b * 256 + 256)
                    sp.sem_inc(sp_passed, 1)
                    stage_pair(b * 4 + 1, 1)
                else:
                    for u in range(2):
                        stage(b * 4, 0, u)
                if more:
                    self.load(sp, b + 1)
                if self.local:
                    for tp in range(QT // 2):
                        if tp + 2 < QT // 2:
                            sp.wait_ge(self.qk, b * 64 + (16 * tp + 17))
                            sp.sem_inc(sp_passed, 1)
                            stage_pair(b * 4 + (tp + 2), tp + 2)
                        for u in range(2):
                            store(b * 4 + tp, tp, u)
                else:
                    with sp.Fori(1, QT // 2) as tp:
                        for u in range(2):
                            stage(b * 4 + tp, tp, u)
                            store(b * 4 + tp - 1, tp - 1, u)
                    for u in range(2):
                        store(b * 4 + 3, QT // 2 - 1, u)

            with sp.Fori(0, BATCH - 1) as b:
                batch(b, True)
            batch(BATCH - 1, False)

        def pe(self, pe):
            pe.sem_inc(self.qk, 1)
            pe.sem_inc(self.p_ps, 1)
            pe.sem_inc(self.pv, 1)

            def prelude(b):
                for hf in range(2):
                    pe.wait_ge(self.x_norm, b * QT + 4 * hf + 4)
                    if hf == 1:
                        pe.wait_ge(self.wo_out, b * QT + 1)
                    for c in range(KC):
                        bank = 4 + 2 * hf + c
                        for t in range(4):
                            ins = nc.tensor.transpose(ps[:, bank, t * P:(t + 1) * P],
                                                      xh[:, 4 * hf + t, c * P:(c + 1) * P], ident[:, :])
                        ins.then_inc(self.hT_ps, 1)
                pe.wait_ge(self.hT_act, b * 2 + 2)
                pe.wait_ge(self.hT_dve, b * 2 + 2)
                job = 0
                for part in (1, 0):
                    for c in range(KC):
                        for hf in range(2):
                            if job >= 4:
                                pe.wait_ge(self.proj_out, b * 12 + (job - 3))
                            for k in range(KC):
                                ins = nc.tensor.matmul(ps[:, job % 4, :],
                                                       self.wqkv[:, k, part * C + c * P:part * C + (c + 1) * P],
                                                       hT[:, k, hf * BANK:(hf + 1) * BANK],
                                                       start=(k == 0), stop=(k == KC - 1))
                            ins.then_inc(self.proj_ps, 1)
                            job += 1
                for t2 in range(QT // 2):
                    pe.wait_ge(self.proj_out, b * 12 + (job - 3))
                    for u in range(2):
                        t = 2 * t2 + u
                        for k in range(KC):
                            ins = nc.tensor.matmul(ps[:, job % 4, u * C:(u + 1) * C], hT[:, k, t * P:(t + 1) * P],
                                                   self.wqkv[:, k, 2 * C:3 * C], start=(k == 0), stop=(k == KC - 1))
                    ins.then_inc(self.proj_ps, 1)
                    job += 1
                pe.wait_ge(self.proj_out, b * 12 + 12)
                pe.wait_ge(self.k_staged, b * 256 + 256)

            def scores(g, tp, s):
                u, h = divmod(s, HEADS)
                if h == 0 and not self.local:
                    pe.wait_ge(self.q_staged[u], g * 256 + 256)
                if s == 0 and self.local:
                    pe.wait_ge(self.q_staged[tp % 2], self.b * 512 + 256 * (tp // 2 + 1))
                q = q_pair[tp % 2][:, h, u * P:(u + 1) * P] if self.local else qst[:, u, h, :]
                pe.wait_ge(self.masked, (self.steps(g, s - 1) if s else g * 16 - 1 if self.prev else g * 16) + 1)
                k0 = self.key_tile(tp, u) * P
                for i in range(self.nb):
                    w = min(BANK, self.kw - i * BANK)
                    ins = nc.tensor.matmul(ps[:, 2 * (s % 2) + i, 0:w], q,
                                           kst[:, h, k0 + i * BANK:k0 + i * BANK + w], start=True, stop=True)
                ins.then_inc(self.qk, 1)

            def turn(g, s):
                pe.wait_ge(self.exp, self.steps(g, s + 1) + 1)
                for j in range(self.nb):
                    odd, m = self.chunk(g, s, j)
                    pe.wait_ge(self.p_dve if odd else self.p_act, m + 1)
                    n = min(4, self.kc - 4 * j)
                    for i in range(n):
                        k = 4 * j + i
                        ins = nc.tensor.transpose(ps[:, 4 + odd, i * P:(i + 1) * P],
                                                  prob[:, s % 2, k * P:(k + 1) * P], ident[:, :])
                    ins.then_inc(self.p_ps, 1)

            def values(g, u, c):
                s = 8 * u + 4 * c + 3
                for j in range(self.nb):
                    odd, m = self.chunk(g, s, j)
                    pe.wait_ge(self.p_dve if odd else self.p_act, m + 2)
                if self.nb == 1:
                    odd, m = self.chunk(g, s - 1, 0)
                    pe.wait_ge(self.p_dve if odd else self.p_act, m + 2)
                if c == 0:
                    pe.wait_ge(self.wo_out, g * 2 + u + 1)
                for k in range(self.kc):
                    for j in range(4):
                        h = 4 * c + j
                        v = vt[:, self.key_tile(self.tp_of, u) + k, 32 * h:32 * h + 32]
                        nc.tensor.matmul(ps[32 * j:32 * j + 32, 6 + c, 0:P], v,
                                         self.pT[:, h, k * P:(k + 1) * P], start=(k == 0), stop=(k == self.kc - 1))
                pe.wait_ge(self.r_exp, g * 4 + (2 * u + c + 1))
                nc.tensor.transpose(ps[:, 6 + c, P:2 * P], rexp[:, c, :], ident[:, :]).then_inc(self.pv, 1)

            def project(g, u):
                pe.wait_ge(self.o_norm, g * 4 + (2 * u + 2))
                for c in range(KC):
                    ins = nc.tensor.matmul(ps[:, 6, 2 * P:4 * P], oTn[:, u, c, :], self.wout[:, c, :],
                                           start=(c == 0), stop=(c == KC - 1))
                ins.then_inc(self.wo_ps, 1)

            def rest(g, s):
                if s - 2 in range(16):
                    turn(g, s - 2)
                for u in range(2):
                    for c in range(2):
                        if s == 8 * u + 4 * c + 6:
                            values(g, u, c)
                    if s == 8 * u + 12:
                        project(g, u)

            def pair(g, tp, prev):
                self.prev = prev
                for s in range(16):
                    scores(g, tp, s)
                    if prev and s < 5:
                        self.tp_of = tp - 1
                        rest(g - 1, s + 16)
                    self.tp_of = tp
                    rest(g, s)

            def tail(g):
                self.tp_of = QT // 2 - 1
                for s in range(5):
                    rest(g - 1, s + 16)

            with pe.Fori(0, BATCH) as b:
                self.b = b
                self.loop(pe, b, prelude, pair, tail)

        def act(self, act):
            act.sem_inc(self.exp, 1)
            act.sem_inc(self.p_act, 1)

            def prelude(b):
                for hf in range(2):
                    act.wait_ge(self.hT_ps, b * 4 + 2 * hf + 1)
                    o, i = hT[:, 0, hf * BANK:(hf + 1) * BANK], ps[:, 4 + 2 * hf, :]
                    if self.local:
                        ins = nc.scalar.activation(o, i, ACT.Identity, scale=colv("n1w", 0), bias=colv("n1b", 0))
                    else:
                        ins = nc.scalar.activation(o, i, ACT.Copy)
                    ins.then_inc(self.hT_act, 1)
                job = 0
                for name, hi in (("kb", k_hi), ("qb", q_hi)):
                    for c in range(KC):
                        for hf in range(2):
                            act.wait_ge(self.proj_ps, b * 12 + (job + 1))
                            nc.scalar.activation(hi[:, c, hf * BANK:(hf + 1) * BANK], ps[:, job % 4, :], ACT.Identity,
                                                 bias=colv(f"{name}{self.n}", c)).then_inc(self.proj_hi, 1)
                            job += 1

            def softmax(g, s):
                act.wait_ge(self.masked, self.steps(g, s + 1) + 1)
                self.p_ps_turned(act, g, s)
                u, h = divmod(s, HEADS)
                nc.scalar.activation(prob[:, s % 2, 0:self.kw], msc[:, s % 2, 0:self.kw], ACT.Exp,
                                     scale=-1.0, bias=nmax[:, s % 2:s % 2 + 1],
                                     accum_out=rsum[:, u, h:h + 1]).then_inc(self.exp, 1)

            def rest(g, s):
                if s - 2 in range(16):
                    for j in range(self.nb):
                        odd, m = self.chunk(g, s - 2, j)
                        if not odd:
                            self.copy_out(act, g, s - 2, j)
                for u in range(2):
                    for c in range(2):
                        if s == 8 * u + 4 * c + 7:
                            act.wait_ge(self.pv, g * 4 + (2 * u + c + 1) + 1)
                            nc.scalar.activation(rT[:, c, :], ps[:, 6 + c, P:2 * P], ACT.Copy)\
                              .then_inc(self.r_act, 1)

            def pair(g, tp, prev):
                self.prev = prev
                for s in range(16):
                    if prev and s < 5:
                        rest(g - 1, s + 16)
                    rest(g, s)
                    softmax(g, s)

            def tail(g):
                for s in range(5):
                    rest(g - 1, s + 16)

            with act.Fori(0, BATCH) as b:
                self.loop(act, b, prelude, pair, tail)

        def p_ps_turned(self, act, g, s):
            back = s - 2
            if back >= 0:
                act.wait_ge(self.p_ps, g * (16 * self.nb) + self.nb * (back + 1) + 1)
            elif self.prev:
                act.wait_ge(self.p_ps, g * (16 * self.nb) - self.nb * (-back - 1) + 1)

        def copy_out(self, eng, g, s, j):
            odd, m = self.chunk(g, s, j)
            u, h = divmod(s, HEADS)
            w = min(BANK, self.kw - j * BANK)
            eng.wait_ge(self.p_ps, g * (16 * self.nb) + (self.nb * s + j + 1) + 1)
            eng.wait_ge(self.pv, (g * 4 + (2 * u + h // 4 - 1) if 2 * u + h // 4 >= 1 else g * 4 - 1 if self.prev_of(s) else g * 4) + 1)
            o, i = self.pT[:, h, j * BANK:j * BANK + w], ps[:, 4 + odd, 0:w]
            if odd:
                nc.vector.tensor_copy(o, i).then_inc(self.p_dve, 1)
            else:
                nc.scalar.activation(o, i, ACT.Copy).then_inc(self.p_act, 1)

        def prev_of(self, s):
            return self.prev

        def pool(self, pool):
            def pair(g, tp, prev):
                for u in range(2):
                    if prev:
                        pool.wait_ge(self.masked, g * 16 + (8 * u - 8) + 1)
                        pool.sem_inc(pool_passed, 1)
                    nc.gpsimd.tensor_copy(mask_tile[:, u, :], mask[:, bass.ds(tp * 2 + u, 1), :].rearrange("p o n -> p (o n)"))\
                      .then_inc(self.mask_set, 1)

            pair(0, 0, False)
            with pool.Fori(1, QT // 2) as tp:
                pair(tp, tp, True)
            with pool.Fori(1, BATCH) as b:
                with pool.Fori(0, QT // 2) as tp:
                    pair(b * 4 + tp, tp, True)

        def dve(self, dve):
            dve.sem_inc(self.masked, 1)
            dve.sem_inc(self.p_dve, 1)
            dve.sem_inc(self.res_ok, 1)
            dve.sem_inc(self.wo_out, 1)
            n = self.n

            def prelude(b):
                relink()
                dve.wait_ge(self.x_in, b * 16 + 16)
                for t in range(QT):
                    ins = nc.vector.bn_stats(stats[:, t, :], xb[:, t, :])
                link(ins)
                for t in range(QT):
                    ins = nc.vector.bn_aggr(mv[:, t, :], stats[:, t, :])
                link(ins)
                rsqrt(QT)
                for t in range(QT):
                    nc.vector.tensor_scalar(xh[:, t, :], xb[:, t, :], mv[:, t, 0:1], nwt[:, 1, t:t + 1],
                                            ALU.subtract, ALU.mult).then_inc(self.x_norm, 1)
                for hf in range(2):
                    dve.wait_ge(self.hT_ps, b * 4 + 2 * hf + 2)
                    o, i = hT[:, 1, hf * BANK:(hf + 1) * BANK], ps[:, 5 + 2 * hf, :]
                    if self.local:
                        ins = nc.vector.tensor_scalar(o, i, colv("n1w", 1), colv("n1b", 1), ALU.mult, ALU.add)
                    else:
                        ins = nc.vector.tensor_copy(o, i)
                    ins.then_inc(self.hT_dve, 1)
                dve.wait_ge(self.stored, b * (16 * QT) + 16)
                r = rowv("pb0" if self.local else "ob1").rearrange("p (o c) -> p o c", o=1).broadcast_to([P, QT, C])
                nc.vector.tensor_tensor(res[:, :, :], xb[:, :, :] if self.local else xh[:, :, :], r, ALU.add)\
                  .then_inc(self.res_ok, 1)
                job = 0
                for name, hi, lo in (("kb", k_hi, k_lo), ("qb", q_hi, q_lo)):
                    for c in range(KC):
                        for hf in range(2):
                            dve.wait_ge(self.proj_hi, b * 8 + (job + 1))
                            w = slice(hf * BANK, (hf + 1) * BANK)
                            nc.vector.scalar_tensor_tensor(lo[:, c, w], ps[:, job % 4, :], colv(f"{name}{n}", c),
                                                           hi[:, c, w].bitcast(F32), ALU.add, ALU.subtract)\
                              .then_inc(self.proj_out, 1)
                            job += 1
                if self.local:
                    dve.wait_ge(mask_init, 16)
                vb = rowv(f"vb{n}").rearrange("p (o c) -> p o c", o=1).broadcast_to([P, 2, C])
                for t2 in range(QT // 2):
                    dve.wait_ge(self.proj_ps, b * 12 + (job + 1))
                    nc.vector.tensor_tensor(vt[:, 2 * t2:2 * t2 + 2, :],
                                            ps[:, job % 4, :].rearrange("p (u c) -> p u c", u=2), vb, ALU.add)\
                      .then_inc(self.proj_out, 1)
                    job += 1

            def add_mask(g, tp, s):
                u, h = divmod(s, HEADS)
                dve.wait_ge(self.qk, self.steps(g, s + 1) + 1)
                dve.wait_ge(self.exp, (self.steps(g, s - 1) if s else g * 16 - 1 if self.prev else g * 16) + 1)
                dve.sem_inc(dve_passed, 1)
                if self.local and tp == 0 and s == 0:
                    dve.wait_ge(bias_ok, 3)
                if self.local:
                    extra = bias[:, self.kind(tp, u), h, :]
                else:
                    extra = mask_tile[:, u, :]
                    if h == 0:
                        dve.wait_ge(self.mask_set, g * 2 + (u + 1))
                        dve.sem_inc(dve_passed, 1)
                sc = ps[:, 2 * (s % 2):2 * (s % 2) + 2, :].rearrange("p a n -> p (a n)")[:, 0:self.kw]
                nc.vector.tensor_tensor_reduce(out=msc[:, s % 2, 0:self.kw], in0=sc, in1=extra, scale=1.0,
                                               scalar=BIG, op0=ALU.add, op1=ALU.min,
                                               accum_out=nmax[:, s % 2:s % 2 + 1]).then_inc(self.masked, 1)

            def rest(g, s):
                if s - 2 in range(16):
                    for j in range(self.nb):
                        odd, m = self.chunk(g, s - 2, j)
                        if odd:
                            self.copy_out(dve, g, s - 2, j)
                for u in range(2):
                    for c in range(2):
                        if s == 8 * u + 4 * c + 5:
                            relink()
                            dve.wait_ge(self.exp, self.steps(g, 8 * u + 4 * c + 4) + 1)
                            link(nc.vector.reciprocal(rinv[:, :], rsum[:, u, 4 * c:4 * c + 4]))
                            nc.vector.tensor_copy(rexp[:, c, :].rearrange("p (h d) -> p h d", h=4),
                                                  rinv[:, :].rearrange("p (h o) -> p h o", o=1).broadcast_to([P, 4, HD]))\
                              .then_inc(self.r_exp, 1)
                        if s == 8 * u + 4 * c + 7:
                            dve.wait_ge(self.r_act, g * 4 + (2 * u + c + 1))
                            nc.vector.tensor_tensor(oTn[:, u, c, :], ps[:, 6 + c, 0:P], rT[:, c, :], ALU.mult)\
                              .then_inc(self.o_norm, 1)
                    if s == 8 * u + 12:
                        dve.wait_ge(self.wo_ps, g * 2 + (u + 1))
                        t = self.tp_of * 2 + u
                        r = res[:, bass.ds(t, 1), :].rearrange("p o c -> p (o c)")
                        nc.vector.tensor_tensor(r, ps[:, 6, 2 * P:4 * P], r, ALU.add).then_inc(self.wo_out, 1)

            def pair(g, tp, prev):
                self.prev = prev
                for s in range(16):
                    add_mask(g, tp, s)
                    if prev and s < 5:
                        self.tp_of = tp - 1
                        rest(g - 1, s + 16)
                    self.tp_of = tp
                    rest(g, s)

            def tail(g):
                self.tp_of = QT // 2 - 1
                for s in range(5):
                    rest(g - 1, s + 16)

            with dve.Fori(0, BATCH) as b:
                self.loop(dve, b, prelude, pair, tail)

    att0 = Attention(0, x, x1_d, wq0, wp0, WK, True)
    att1 = Attention(1, x2_d, y_d, wq1, wo1, N, False)

    xm = sb("xm", [P, 2, 4, C], F32, at=at_xb)
    xmh = sb("xmh", [P, 4, C], F32, at=at_xb + 8192)
    mT = sb("mT", [P, KC, BANK], F32, at=at_xb + 12288)
    gel = sb("gel", [P, HCH, BANK], F32, at=at_q)
    x2t = sb("x2t", [P, 2, 4, C], F32, at=at_q + 16384)
    m_in = [sem("m_in_a"), sem("m_in_b")]
    wq1_in = sem("wq1_in")
    m_norm = sem("m_norm")
    m_turn = sem("m_turn")
    m_act = sem("m_act")
    m_dve = sem("m_dve")
    f1_ps = sem("f1_ps")
    f1_out = sem("f1_out")
    f2_ps = sem("f2_ps")
    f2_out = sem("f2_out")
    m_stored = [sem("m_stored_a"), sem("m_stored_b")]
    GROUPS = TILES // 4

    def mlp_loop(eng, group):
        with eng.Fori(0, GROUPS // 2 - 1) as i:
            for u in range(2):
                group(i * 2 + u, i, u, True)
        for u in range(2):
            group(GROUPS - 2 + u, GROUPS // 2 - 1, u, u == 0)

    def mlp_sp(sp):
        for c in m_stored:
            sp.sem_inc(c, 16)
        x1, x2 = tiles(x1_d), tiles(x2_d)
        zero_sp(sp)
        sp.wait_ge(att0.stored, 16 * TILES + 16)
        sp.sem_inc(sp_passed, 1)

        def load(g, i, u):
            sp.dma_start(xm[:, u, :, :], x1[:, bass.ds(g * 4, 4), :]).then_inc(m_in[u], 16)

        def group(g, i, u, more):
            if more:
                sp.wait_ge(f2_out, g * 4 + 1)
                sp.sem_inc(sp_passed, 1)
                load(g + 1, i, 1 - u)
            sp.wait_ge(f2_out, g * 4 + 5)
            sp.sem_inc(sp_passed, 1)
            sp.dma_start(x2[:, bass.ds(g * 4, 4), :], x2t[:, u, :, :]).then_inc(m_stored[u], 16)

        load(0, 0, 0)
        sp.dma_start(wq1[:, :, :], w_qkv1.rearrange("(k p) n -> p k n", p=P)).then_inc(wq1_in, 16)
        mlp_loop(sp, group)

    def mlp_pe(pe):
        def turn(g):
            pe.wait_ge(m_norm, g + 1)
            for c in range(KC):
                for t in range(4):
                    ins = nc.tensor.transpose(ps[:, 6 + c, t * P:(t + 1) * P], xmh[:, t, c * P:(c + 1) * P], ident[:, :])
                ins.then_inc(m_turn, 1)

        def group(g, i, u, more):
            pe.wait_ge(m_act, g + 1)
            pe.wait_ge(m_dve, g + 1)
            for h in range(HCH):
                pe.wait_ge(f1_out, (g * HCH + (h - 3) if h >= 3 else g * HCH) + 1)
                for k in range(KC):
                    ins = nc.tensor.matmul(ps[:, h % 4, :], wf1[:, k, h * P:(h + 1) * P], mT[:, k, :],
                                           start=(k == 0), stop=(k == KC - 1))
                ins.then_inc(f1_ps, 1)
            if more:
                turn(g + 1)
            pe.wait_ge(f1_out, g * HCH + HCH + 1)
            for t in range(4):
                pe.wait_ge(f2_out, (g * 4 + (t - 1) if t else g * 4) + 1)
                for h in range(HCH):
                    ins = nc.tensor.matmul(ps[:, 4 + t % 2, 0:C], gel[:, h, t * P:(t + 1) * P], wf2[:, h, :],
                                           start=(h == 0), stop=(h == HCH - 1))
                ins.then_inc(f2_ps, 1)

        turn(0)
        pe.wait_ge(wf_ok, 1)
        mlp_loop(pe, group)

    def mlp_act(act):
        act.sem_inc(f1_out, 1)

        def bring(g):
            act.wait_ge(m_turn, g * 2 + 1)
            nc.scalar.activation(mT[:, 0, :], ps[:, 6, :], ACT.Identity, scale=colv("n2w", 0), bias=colv("n2b", 0))\
              .then_inc(m_act, 1)

        def group(g, i, u, more):
            act.wait_ge(f2_out, g * 4 + 1)
            for h in range(HCH):
                act.wait_ge(f1_ps, g * HCH + (h + 1))
                nc.scalar.activation(gel[:, h, :], ps[:, h % 4, :], ACT.Gelu, bias=colv("fb", h)).then_inc(f1_out, 1)
            if more:
                bring(g + 1)

        bring(0)
        mlp_loop(act, group)

    def mlp_dve(dve):
        dve.sem_inc(f2_out, 1)
        f2b = rowv("f2b").rearrange("p (o c) -> p o c", o=1).broadcast_to([P, 4, C])

        def normal(g, i, u):
            relink()
            dve.wait_ge(m_in[u], i * 16 + 16)
            for t in range(4):
                ins = nc.vector.bn_stats(stats[:, t, :], xm[:, u, t, :])
            link(ins)
            for t in range(4):
                ins = nc.vector.bn_aggr(mv[:, t, :], stats[:, t, :])
            link(ins)
            rsqrt(4)
            for t in range(4):
                ins = nc.vector.tensor_scalar(xmh[:, t, :], xm[:, u, t, :], mv[:, t, 0:1], nwt[:, 1, t:t + 1],
                                              ALU.subtract, ALU.mult)
            ins.then_inc(m_norm, 1)
            dve.wait_ge(m_turn, g * 2 + 2)
            nc.vector.tensor_scalar(mT[:, 1, :], ps[:, 7, :], colv("n2w", 1), colv("n2b", 1), ALU.mult, ALU.add)\
              .then_inc(m_dve, 1)
            link(nc.vector.tensor_tensor(xm[:, u, :, :], xm[:, u, :, :], f2b, ALU.add))

        def group(g, i, u, more):
            if more:
                normal(g + 1, i + u, 1 - u)
            dve.wait_ge(m_stored[u], i * 16 + 16)
            for t in range(4):
                dve.wait_ge(f2_ps, g * 4 + (t + 1))
                ins = nc.vector.tensor_tensor(x2t[:, u, t, :], ps[:, 4 + t % 2, 0:C], xm[:, u, t, :], ALU.add)
                ins.then_inc(f2_out, 1)

        relink()
        dve.wait_ge(ld_f, 64)
        scale_rows(dve, "g2", wf2, "f2b", HCH).then_inc(wf_ok, 1)
        dve.wait_ge(wf_ok, 1)
        normal(0, 0, 0)
        dve.wait_ge(wq1_in, 16)
        relink()
        link(nc.vector.tensor_scalar(wq1[:, :, 0:C], wq1[:, :, 0:C], -SCALE, None, ALU.mult))
        mlp_loop(dve, group)

    def prep_sp(sp):
        att0.load(sp, 0)
        edge_view = edges.rearrange("a (p n) -> a p n", p=P)
        sp.dma_start(e_src[:, :], edge_view[0]).then_inc(edge_ld, 16)
        sp.dma_start(e_dst[:, :], edge_view[1]).then_inc(edge_ld, 16)
        for dst, src in ((col[:, :], cols), (wq0[:, :, :], w_qkv0.rearrange("(k p) n -> p k n", p=P)),
                         (wp0[:, :, :], w_proj0.rearrange("(k p) n -> p k n", p=P))):
            sp.dma_start(dst, src).then_inc(ld, 16)
        sp.dma_start(row[:, :].rearrange("p (r c) -> p r c", c=C), rows.rearrange("(o r) c -> o r c", o=1).broadcast_to([P, len(NROW), C]))\
          .then_inc(ld, 16)
        sp.dma_start(wmask[:, :, :], window_mask).then_inc(ld_b, 16)
        sp.wait_ge(prep_p, 3)
        for i in range(ROWS):
            sp.dma_start(toep[32 * i:32 * i + 32, i + 2:i + 15, :, :].rearrange("p a h c -> p (a h c)"), rpb_toeplitz)\
              .then_inc(ld_b, 16)
        sp.wait_ge(big_ready, 1)
        sp.dma_start(mask_d.rearrange("(p k n) o -> p k (n o)", p=P, n=2048),
                     big[:, :].rearrange("p (o n) -> p o n", o=1).broadcast_to([P, 16, 2048])).then_inc(mask_init, 16)
        for dst, src in ((wf1, w_fc1), (wf2, w_fc2), (wo1, w_o1), (wr, w_router)):
            sp.dma_start(dst[:, :, :], src.rearrange("(k p) n -> p k n", p=P)).then_inc(ld_f, 16)

    def zero_sp(sp):
        sp.wait_ge(prep_p, 2)
        sp.dma_start(xs_d.rearrange("(n p) c -> p n c", p=P),
                     zeros[:, :].rearrange("p (o c) -> p o c", o=1).broadcast_to([P, MT, C])).then_inc(xs_zero, 16)

    def prep_pool(pool):
        nc.gpsimd.memset(ident[:, :], 0.0).then_inc(prep_p, 1)
        nc.gpsimd.memset(zeros[:, :], 0.0).then_inc(prep_p, 1)
        nc.gpsimd.memset(toep[:, :, :, :], 0.0).then_inc(prep_p, 1)
        pool.wait_ge(prep_p, 1)
        nc.gpsimd.affine_select(out=ident[:, :], in_=ident[:, :], compare_op=ALU.not_equal, fill=1.0,
                                base=0, pattern=[[-1, P]], channel_multiplier=1).then_inc(prep_p, 1)

    def scatter_pool(pool):
        pool.wait_ge(edge_ready, 1)
        pool.wait_ge(mask_init, 16)
        half = EBATCH // 2
        zero = zeros[:, :].bitcast(BF16)[:, 0:1]
        def columns(i):
            for x in range(EBATCH):
                if x in (0, 4):
                    a = 0 if x == 0 else half
                    nc.gpsimd.tensor_copy(edge_slot[:, a:a + half], edge_at[:, bass.ds(i * EBATCH + a, half)])\
                      .then_inc(slot_copy, 1)
                if x in (0, half):
                    pool.wait_ge(slot_copy, i * 2 + (1 if x == 0 else 2))
                    pool.sem_inc(pool_passed, 1)
                k = x % COPIES
                if x >= COPIES or not isinstance(i, int):
                    pool.wait_ge(scat[k], i * (EBATCH // COPIES * 16) + 16 * (x // COPIES))
                    pool.sem_inc(pool_passed, 1)
                pool.indirect_dma_start(mask_d, bass.IndirectOffsetOnAxis(edge_slot[:, x:x + 1], 0), zero, None,
                                        bounds_check=COPIES * CELLS - 1, oob_is_err=False).then_inc(scat[k], 16)

        columns(0)
        with pool.Fori(1, ECOL // EBATCH) as i:
            columns(i)

    def scale_rows(dve, nme, w, b, n):
        link(nc.vector.scalar_tensor_tensor(rowv(nme), rowv(nme), -1.0, rowv(nme), ALU.mult, ALU.max))
        g = rowv(nme).rearrange("p (o c) -> p o c", o=1).broadcast_to([P, n, C])
        nc.vector.tensor_tensor(rowv(b), rowv(b), rowv(nme), ALU.mult)
        return nc.vector.tensor_tensor(w[:, :, :], w[:, :, :], g, ALU.mult)

    def prep_dve(dve):
        nc.vector.memset(big[:, :], NO_EDGE).then_inc(big_ready, 1)
        relink()
        dve.wait_ge(edge_ld, 32)
        link(nc.vector.tensor_scalar(e_tmp[:, :], e_dst[:, :], float(N), None, ALU.is_ge))
        link(nc.vector.scalar_tensor_tensor(e_tmp[:, :], e_src[:, :], float(N), e_tmp[:, :], ALU.is_ge, ALU.max))
        link(nc.vector.scalar_tensor_tensor(e_src[:, :], e_src[:, :], float(N), e_dst[:, :], ALU.mult, ALU.add))
        link(nc.vector.scalar_tensor_tensor(edge_at[:, :], e_tmp[:, :], float(1 << 23), e_src[:, :], ALU.mult, ALU.add))
        for k in range(1, COPIES):
            v = edge_at[:, :].rearrange("p (n k) -> p n k", k=COPIES)[:, :, k]
            link(nc.vector.tensor_scalar(v, v, float(k * CELLS), None, ALU.add))
        nc.vector.memset(nwi[:, :], 0).then_inc(edge_ready, 1)
        dve.wait_ge(ld, 16 * 4)
        link(nc.vector.tensor_scalar(wq0[:, :, 0:C], wq0[:, :, 0:C], -SCALE, None, ALU.mult))
        for nme in ("qb0", "qb1"):
            link(nc.vector.tensor_scalar(col[:, cat[nme]:cat[nme] + KC], col[:, cat[nme]:cat[nme] + KC], -SCALE, None, ALU.mult))
        link(scale_rows(dve, "g1", wp0, "pb0", KC))
        nc.vector.memset(nwt[:, :, :], 0.0).then_inc(prep_v, 1)
        dve.wait_ge(prep_v, 1)

    def bias_pool(pool):
        pool.wait_ge(ld_b, 16 + 16 * ROWS)
        for kind, first in enumerate((8, 4, 0)):
            nc.gpsimd.tensor_tensor(
                bias[:, kind, :, :].rearrange("p h (r c) -> p h r c", c=SIDE),
                wmask[:, kind, :].rearrange("p (o r c) -> p o r c", o=1, c=SIDE).broadcast_to([P, HEADS, WT * ROWS, SIDE]),
                toep[:, first:first + WT * ROWS, :, :].rearrange("p r h c -> p h r c"), ALU.subtract)\
              .then_inc(bias_ok, 1)

    def mask_pool(pool):
        masks = mask_d.rearrange("(k t p n) o -> t p k (n o)", k=COPIES, t=QT, p=P)
        for c in scat:
            pool.wait_ge(c, 16 * (ECOL // COPIES))
        pool.wait_ge(att0.stored, 16 * TILES + 16)

        def load(t, u):
            pool.dma_start(mcopy[:, u, :, :], masks[t]).then_inc(mask_in[u], 16)

        load(0, 0)
        for t in range(QT):
            u = t % 2
            if t + 1 < QT:
                if t:
                    pool.wait_ge(mask_ok, t)
                load(t + 1, 1 - u)
            pool.wait_ge(mask_in[u], 16 * (t // 2 + 1))
            nc.gpsimd.tensor_tensor(mcopy[:, u, 0:2, :], mcopy[:, u, 0:2, :], mcopy[:, u, 2:4, :], ALU.mult)\
              .then_inc(mask_half, 1)
            pool.wait_ge(mask_half, t + 1)
            nc.gpsimd.tensor_tensor(mask[:, t, :], mcopy[:, u, 0, :], mcopy[:, u, 1, :], ALU.mult).then_inc(mask_ok, 1)
        pool.wait_ge(mask_ok, QT)

    at_z = at_w0 + 20480
    moe_at = {"at": at_w0}

    def mb(name, shape, dt=F32, at=None):
        n = 4 * int(np.prod(shape[1:]))
        if at is None:
            at = moe_at["at"]
            moe_at["at"] = (at + n + 31) // 32 * 32
        return sb(name, shape, dt, at=at)

    rc = mb("route", [P, EXPERTS + 2 * P + MT])
    st32 = mb("stats32", [P, TILES, 6])
    mv32 = mb("mv32", [P, TILES, 2])
    mvz = mb("mvz", [P, TILES, 2])
    nwt32 = mb("nwt32", [P, 3, TILES])
    nwi32 = mb("nwi32", [P, TILES], I32)
    at_zT = moe_at["at"]
    zT = mb("zT", [P, 2, KC, BANK])
    te_ge = mb("te_ge", [P, MT, EXPERTS], at=at_zT)
    te_f = mb("te_f", [P, MT], at=at_zT + 2304)
    acc_a = mb("acc_a", [P, TILES, EXPERTS], at=at_zT + 2304 + 512)
    acc_b = mb("acc_b", [P, TILES, EXPERTS], at=at_zT + 2304 + 512 + 1024)
    lg = mb("lg", [P, TILES, EXPERTS])
    pr = mb("pr", [P, TILES, EXPERTS])
    oh = mb("oh", [P, 2, TILES, EXPERTS])
    tot = mb("tot", [P, TILES, EXPERTS])
    m1 = mb("m1", [P, TILES])
    rsm = mb("rsm", [P, TILES])
    topp = mb("topp", [P, 2, TILES])
    posf = mb("posf", [P, 2, TILES])
    cnt = mb("cnt", [P, 4, EXPERTS])
    cnt_i = mb("cnt_i", [P, EXPERTS], I32)
    gate = mb("gate", [P, 2, TILES])
    pos = mb("pos", [P, TILES, 2], I32)
    te = mb("te", [P, MT], I32)
    assert moe_at["at"] <= at_z
    zall = sb("zall", [P, TILES, C], F32, at=at_z)
    at_w13 = at_z + 32768
    W13 = sb("W13", [P, EXPERTS, KC, 2 * FF], F32, at=at_w13)
    at_w2 = at_w13 + EXPERTS * KC * 2 * FF * 4
    W2 = sb("W2", [P, EXPERTS, FCH, C], F32, at=at_w2)
    zs2 = sb("zs2", [P, 2, 4, C], F32, at=at_w13 + 6 * KC * 2 * FF * 4)
    t2b = sb("t2b", [P, TILES, C], F32, at=at_w2 + 2 * FCH * C * 4)
    assert at_w2 + EXPERTS * FCH * C * 4 <= nc.sbuf_usable_end
    G1 = TILES // 4
    xs_zero = sem("xs_zero")
    rc_in = sem("rc_in")
    y_in = [sem(f"y_in{q}") for q in range(CHUNKS)]
    x2_in = [sem(f"x2_in{q}") for q in range(CHUNKS)]
    t2_ok = sem("t2_ok")
    t2_stored = sem("t2_stored")
    w13_in = sem("w13_in")
    w2_in = sem("w2_in")
    x2b_ok = sem("x2b_ok")
    z_ok = sem("z_ok")
    z_turn = sem("z_turn")
    z_act = sem("z_act")
    z_copy = sem("z_copy")
    z_dve = sem("z_dve")
    lg_ps = sem("lg_ps")
    lg_ok = sem("lg_ok")
    lg_exp = sem("lg_exp")
    oh_ok = sem("oh_ok")
    rank_ps = sem("rank_ps")
    routed = sem("routed")

    def m1_sp(sp):
        sp.wait_ge(att1.stored, 16 * TILES + 16)
        sp.sem_inc(sp_passed, 1)
        sp.dma_start(rc[:, :], route_const).then_inc(rc_in, 16)
        ty, tx = tiles(y_d), tiles(x2_d)
        for q in range(CHUNKS):
            w = slice(q * QT, (q + 1) * QT)
            sp.dma_start(zall[:, w, :], ty[:, w, :]).then_inc(y_in[q], 16)
            sp.dma_start(t2b[:, w, :], tx[:, w, :]).then_inc(x2_in[q], 16)
        for e in range(0, EXPERTS - 2, 2):
            load_w13(sp, e)
        load_w2(sp, 0)
        sp.wait_ge(t2_ok, G1)
        sp.sem_inc(sp_passed, 1)
        sp.dma_start(tiles(t2_d), t2b[:, :, :]).then_inc(t2_stored, 16)
        sp.wait_ge(t2_stored, 16)
        sp.wait_ge(z_ok, G1)
        for e in range(2, EXPERTS, 2):
            load_w2(sp, e)
        sp.wait_ge(z_turn, 2 * G1 + 1)
        sp.wait_ge(z_copy, G1 + 1)
        load_w13(sp, EXPERTS - 2)

    def load_w13(sp, e):
        sp.dma_start(W13[:, e:e + 2, :, :].rearrange("p e k n -> p (e k) n"),
                     w13[e:e + 2].rearrange("e (k p) n -> p (e k) n", p=P)).then_inc(w13_in, 16)

    def load_w2(sp, e):
        sp.dma_start(W2[0:FCW, e:e + 2, :, :].rearrange("p e k n -> p (e k) n"),
                     w2[e:e + 2].rearrange("e (k p) n -> p (e k) n", p=FCW)).then_inc(w2_in, 16)

    def m1_pool(pool):
        bet = rowv("bet").rearrange("p (o c) -> p o c", o=1).broadcast_to([P, QT, C])
        for q in range(CHUNKS):
            pool.wait_ge(x2_in[q], 16)
            v = t2b[:, q * QT:(q + 1) * QT, :]
            nc.gpsimd.tensor_tensor(v, v, bet, ALU.add).then_inc(x2b_ok, 1)

    def m1_pe(pe):
        pe.sem_inc(z_turn, 1)
        with pe.Fori(0, G1 // 2) as i:
            for u in range(2):
                g = i * 2 + u
                pe.wait_ge(z_ok, g + 1)
                pe.wait_ge(z_act, g + 1)
                pe.wait_ge(z_dve, g + 1)
                for c in range(KC):
                    for t in range(4):
                        ins = nc.tensor.transpose(
                            ps[:, 6 + c, t * P:(t + 1) * P],
                            zs2[:, u, t, c * P:(c + 1) * P], ident[:, :])
                    ins.then_inc(z_turn, 1)
                pe.wait_ge(z_act, g + 2)
                pe.wait_ge(z_dve, g + 2)
                for t in range(4):
                    for k in range(KC):
                        ins = nc.tensor.matmul(ps[:, 5, bass.ds(g * 4 * EXPERTS + t * EXPERTS, EXPERTS)],
                                               zT[:, u, k, t * P:(t + 1) * P], wr[:, k, :],
                                               start=(k == 0), stop=(k == KC - 1))
                ins.then_inc(lg_ps, 1)
        pe.wait_ge(oh_ok, 1)
        chosen = pr[:, :, :].rearrange("p t e -> p (t e)")
        nc.tensor.matmul(ps[:, 4, 0:TILES * EXPERTS], rc[:, EXPERTS:EXPERTS + P], chosen, start=True, stop=True)
        nc.tensor.matmul(ps[:, 4, TILES * EXPERTS:2 * TILES * EXPERTS], rc[:, EXPERTS + P:EXPERTS + 2 * P], chosen,
                         start=True, stop=True).then_inc(rank_ps, 1)

    def m1_act(act):
        act.sem_inc(z_act, 1)
        act.sem_inc(z_copy, 1)
        with act.Fori(0, G1 // 2) as i:
            for u in range(2):
                act.wait_ge(z_ok, i * 2 + (u + 1))
                nc.scalar.activation(zall[:, bass.ds(i * 8 + u * 4, 4), :], zs2[:, u, :, :], ACT.Copy)\
                  .then_inc(z_copy, 1)
                act.wait_ge(z_turn, i * 4 + (2 * u + 1) + 1)
                nc.scalar.activation(zT[:, u, 0, :], ps[:, 6, :], ACT.Copy).then_inc(z_act, 1)
        act.wait_ge(lg_ok, 1)
        nc.scalar.activation(pr[:, :, :], lg[:, :, :], ACT.Exp).then_inc(lg_exp, 1)

    def over(ap, n):
        return ap.rearrange("p (a o) -> p a o", o=1).broadcast_to([P, ap.shape[1], n])

    def m1_dve(dve):
        dve.sem_inc(z_dve, 1)
        gam = rowv("gam")

        def tile_of(buf, g):
            return [buf[:, bass.ds(g * 4 + t, 1), :].rearrange("p o c -> p (o c)") for t in range(4)]

        relink()
        for q in range(CHUNKS):
            dve.wait_ge(y_in[q], 16)
            for t in range(q * QT, (q + 1) * QT):
                ins = nc.vector.bn_stats(st32[:, t, :], zall[:, t, :])
            link(ins)
            for t in range(q * QT, (q + 1) * QT):
                ins = nc.vector.bn_aggr(mv32[:, t, :], st32[:, t, :])
            link(ins)
        rsqrt(TILES, mv32, nwt32, nwi32)
        with dve.Fori(0, CHUNKS) as i:
          for u in range(2):
            g = i * 2 + u
            relink()
            dve.wait_ge(x2b_ok, i + 1)
            zs, ts = tile_of(zall, g), tile_of(t2b, g)
            for t in range(4):
                ins = nc.vector.scalar_tensor_tensor(zs[t], zs[t], mv32[:, bass.ds(g * 4 + t, 1), 0], gam,
                                                     ALU.subtract, ALU.mult)
            link(ins)
            for t in range(4):
                ins = nc.vector.scalar_tensor_tensor(ts[t], zs[t], nwt32[:, 1, bass.ds(g * 4 + t, 1)], ts[t],
                                                     ALU.mult, ALU.add)
            ins.then_inc(t2_ok, 1)
            dve.wait_ge(t2_ok, g + 1)
            dve.sem_inc(dve_passed, 1)
            for t in range(4):
                ins = nc.vector.bn_stats(st32[:, t, :], ts[t])
            link(ins)
            for t in range(4):
                ins = nc.vector.bn_aggr(mv[:, t, :], st32[:, t, :])
            link(ins)
            link(nc.vector.tensor_copy(mvz[:, bass.ds(g * 4, 4), :], mv[:, 0:4, :]))
        relink()
        rsqrt(TILES, mvz, nwt32, nwi32)
        with dve.Fori(0, G1 // 2) as i:
            for u in range(2):
                g = i * 2 + u
                ts = tile_of(t2b, g)
                if u == 0:
                    dve.wait_ge(z_turn, i * 4 + 1)
                    dve.wait_ge(z_copy, i * 2 + 1)
                for t in range(4):
                    ins = nc.vector.tensor_scalar(zs2[:, u, t, :], ts[t], mvz[:, bass.ds(g * 4 + t, 1), 0],
                                                  nwt32[:, 1, bass.ds(g * 4 + t, 1)], ALU.subtract, ALU.mult)
                ins.then_inc(z_ok, 1)
                dve.wait_ge(z_turn, i * 4 + (2 * u + 2) + 1)
                nc.vector.tensor_copy(zT[:, u, 1, :], ps[:, 7, :]).then_inc(z_dve, 1)
        relink()
        dve.wait_ge(lg_ps, G1)
        dve.wait_ge(rc_in, 16)
        nop = EXPERTS
        flat = ps[:, 5, 0:TILES * EXPERTS].rearrange("p (t e) -> p t e", e=EXPERTS)
        link(nc.vector.tensor_reduce(m1[:, :], flat, AX.X, ALU.max))
        nc.vector.tensor_tensor(lg[:, :, :], flat, over(m1[:, :], nop), ALU.subtract).then_inc(lg_ok, 1)
        dve.wait_ge(lg_exp, 1)
        link(nc.vector.tensor_reduce(rsm[:, :], pr[:, :, :], AX.X, ALU.add))
        link(nc.vector.reciprocal(rsm[:, :], rsm[:, :]))
        link(nc.vector.tensor_tensor(pr[:, :, :], pr[:, :, :], over(rsm[:, :], nop), ALU.mult))
        ids = rc[:, 0:EXPERTS].rearrange("p (o e) -> p o e", o=1).broadcast_to([P, TILES, EXPERTS])
        for k in range(2):
            link(nc.vector.tensor_reduce(topp[:, k, :], pr[:, :, :], AX.X, ALU.max))
            link(nc.vector.tensor_tensor(oh[:, k, :, :], pr[:, :, :], over(topp[:, k, :], nop), ALU.is_equal))
            link(nc.vector.tensor_tensor(oh[:, k, :, :], oh[:, k, :, :], ids, ALU.mult))
            link(nc.vector.tensor_reduce(m1[:, :], oh[:, k, :, :], AX.X, ALU.min))
            link(nc.vector.tensor_tensor(oh[:, k, :, :], ids, over(m1[:, :], nop), ALU.is_equal))
            if k == 0:
                link(nc.vector.scalar_tensor_tensor(pr[:, :, :], oh[:, 0, :, :], -2.0, pr[:, :, :], ALU.mult, ALU.add))
        nc.vector.tensor_tensor(pr[:, :, :], oh[:, 0, :, :], oh[:, 1, :, :], ALU.add).then_inc(oh_ok, 1)
        link(nc.vector.tensor_tensor(rsm[:, :], topp[:, 0, :], topp[:, 1, :], ALU.add))
        link(nc.vector.tensor_scalar(rsm[:, :], rsm[:, :], 1e-9, None, ALU.add))
        link(nc.vector.reciprocal(rsm[:, :], rsm[:, :]))
        for k in range(2):
            link(nc.vector.tensor_tensor(gate[:, k, :], topp[:, k, :], rsm[:, :], ALU.mult))
        dve.wait_ge(rank_ps, 1)
        totals = ps[:, 4, TILES * EXPERTS:2 * TILES * EXPERTS].rearrange("p (t e) -> p t e", e=EXPERTS)
        link(nc.vector.tensor_copy(tot[:, :, :], totals))
        src, a, b = tot, acc_a, acc_b
        d = 1
        while d < TILES:
            nc.vector.tensor_copy(a[:, 0:d, :], src[:, 0:d, :])
            link(nc.vector.tensor_tensor(a[:, d:, :], src[:, d:, :], src[:, 0:TILES - d, :], ALU.add))
            src, a, b = a, b, a
            d *= 2
        inc = src
        link(nc.vector.tensor_scalar(cnt_i[:, :], inc[:, TILES - 1, :], float(P - 1), None, ALU.add))
        link(nc.vector.tensor_scalar(cnt_i[:, :], cnt_i[:, :], 7, None, ALU.logical_shift_right))
        link(nc.vector.tensor_copy(cnt[:, 0, :], cnt_i[:, :]))
        s, d = 0, 1
        while d < EXPERTS:
            nc.vector.tensor_copy(cnt[:, s + 1, 0:d], cnt[:, s, 0:d])
            link(nc.vector.tensor_tensor(cnt[:, s + 1, d:], cnt[:, s, d:], cnt[:, s, 0:EXPERTS - d], ALU.add))
            s += 1
            d *= 2
        ends = cnt[:, s, :]
        nums = rc[:, EXPERTS + 2 * P:].rearrange("p (j o) -> p j o", o=1).broadcast_to([P, MT, EXPERTS])
        link(nc.vector.tensor_tensor(te_ge[:, :, :], nums,
                                     ends.rearrange("p (o e) -> p o e", o=1).broadcast_to([P, MT, EXPERTS]), ALU.is_ge))
        link(nc.vector.tensor_reduce(te_f[:, :], te_ge[:, :, :], AX.X, ALU.add))
        link(nc.vector.tensor_scalar(te[:, :], te_f[:, :], float(EXPERTS - 1), None, ALU.min))
        link(nc.vector.tensor_tensor(cnt[:, 1, :], ends, cnt[:, 0, :], ALU.subtract))
        link(nc.vector.tensor_scalar(cnt[:, 1, :], cnt[:, 1, :], float(P), None, ALU.mult))
        link(nc.vector.tensor_tensor(inc[:, :, :], inc[:, :, :], tot[:, :, :], ALU.subtract))
        link(nc.vector.tensor_tensor(inc[:, :, :], inc[:, :, :], ps[:, 4, 0:TILES * EXPERTS].rearrange("p (t e) -> p t e", e=EXPERTS), ALU.add))
        link(nc.vector.tensor_tensor(inc[:, :, :], inc[:, :, :], cnt[:, 1, :].rearrange("p (o e) -> p o e", o=1).broadcast_to([P, TILES, EXPERTS]), ALU.add))
        for k in range(2):
            link(nc.vector.tensor_tensor(oh[:, k, :, :], oh[:, k, :, :], inc[:, :, :], ALU.mult))
            link(nc.vector.tensor_reduce(posf[:, k, :], oh[:, k, :, :], AX.X, ALU.add))
            ins = nc.vector.tensor_copy(pos[:, :, k], posf[:, k, :])
            link(ins)
        nc.vector.memset(st32[:, 0, :], 0.0).then_inc(routed, 1)

    at_s = at_z
    xs = sb("xs", [P, 2, C], F32, at=at_s)
    xsT = sb("xsT", [P, 2, KC, P], F32, at=at_s + 2048)
    sil = sb("sil", [P, 2, HALF + 3], F32, at=at_s + 4096)
    hm = sb("hm", [P, 2, FF + 6], F32, at=at_s + 4096 + 2752)
    hmT = sb("hmT", [P, 2, FCH, P], F32, at=at_s + 6848 + 5504)
    yo = sb("yo", [P, 2, C], F32, at=at_s + 12352 + 6144)
    ya = sb("ya", [P, 2, 4, 2, C], F32, at=at_w13)
    tc = sb("tc", [P, 2, 4, C], F32, at=at_w13 + 16384)
    oc = sb("oc", [P, 2, 4, C], F32, at=at_w13 + 24576)

    sent = sem("sent")
    xs_in = [sem("xs_in_a"), sem("xs_in_b")]
    xs_turn = sem("xs_turn")
    xs_out = sem("xs_out")
    h_ps = sem("h_ps")
    silu_ok = sem("silu_ok")
    hm_ok = sem("hm_ok")
    hm_turn = sem("hm_turn")
    hmT_act = sem("hmT_act")
    hmT_dve = sem("hmT_dve")
    y_ps = sem("y_ps")
    y_out = sem("y_out")
    y_stored = [sem("y_stored_a"), sem("y_stored_b")]

    def dispatch_pool(pool):
        pool.wait_ge(xs_zero, 16)
        pool.wait_ge(routed, 1)
        pool.wait_ge(z_copy, G1 + 1)
        for t in range(TILES):
            for k in range(2):
                pool.indirect_dma_start(xs_d, bass.IndirectOffsetOnAxis(pos[:, t, k:k + 1], 0), zall[:, t, :], None,
                                        bounds_check=MT * P - 1, oob_is_err=False).then_inc(sent, 16)

    def moe_loop(eng, step):
        for u in range(2):
            step(u, 0, u, u == 0, False)
        with eng.Fori(1, MT // 2 - 1) as i:
            for u in range(2):
                step(i * 2 + u, i, u, False, False)
        for u in range(2):
            step(MT - 2 + u, MT // 2 - 1, u, False, u == 1)

    def moe_sp(sp):
        for c in y_stored:
            sp.sem_inc(c, 16)
        xt, yt = tiles(xs_d), tiles(y2_d)
        sp.wait_ge(sent, 16 * SLOTS // P)

        def load(j, u):
            sp.dma_start(xs[:, u, :].rearrange("p (o c) -> p o c", o=1), xt[:, bass.ds(j, 1), :]).then_inc(xs_in[u], 16)

        def store(j, u):
            sp.wait_ge(y_out, j + 2)
            sp.sem_inc(sp_passed, 1)
            sp.dma_start(yt[:, bass.ds(j, 1), :], yo[:, u, :].rearrange("p (o c) -> p o c", o=1)).then_inc(y_stored[u], 16)

        def step(j, i, u, first, last):
            if not last:
                sp.wait_ge(xs_turn, j + 2)
                sp.sem_inc(sp_passed, 1)
                load(j + 1, 1 - u)
            if not first:
                store(j - 1, 1 - u)

        load(0, 0)
        moe_loop(sp, step)
        store(MT - 1, (MT - 1) % 2)

    def moe_pe(pe):
        pe.sem_inc(xs_turn, 2)
        pe.sem_inc(y_ps, 1)

        def turn_x(j, i, u):
            pe.wait_ge(xs_in[u], i * 16 + 16)
            if not isinstance(j, int) or j:
                pe.wait_ge(xs_out, j)
            for k in range(KC):
                ins = nc.tensor.transpose(ps[:, 4, k * P:(k + 1) * P], xs[:, u, k * P:(k + 1) * P], ident[:, :])
            ins.then_inc(xs_turn, 1)

        def hidden(j, u, e):
            pe.wait_ge(xs_out, j + 1)
            for hf in range(2):
                pe.wait_ge(hm_ok, j * 2 + hf + 1)
                for m in range(2):
                    for k in range(KC):
                        a = m * FF + hf * HALF
                        ins = nc.tensor.matmul(ps[:, 2 * hf + m, 0:HALF], xsT[:, u, k, :],
                                               W13[:, bass.ds(e, 1), k, a:a + HALF].rearrange("p o n -> p (o n)"),
                                               start=(k == 0), stop=(k == KC - 1))
                ins.then_inc(h_ps, 1)

        def turn_h(j, u):
            pe.wait_ge(hmT_act, j + 1)
            pe.wait_ge(hmT_dve, j + 1)
            pe.wait_ge(hm_ok, j * 2 + 4)
            for c in range(FCH):
                w = min(FCW, FF - c * FCW)
                ins = nc.tensor.transpose(ps[0:w, 5 + c // 4, (c % 4) * P:(c % 4 + 1) * P],
                                          hm[:, u, c * FCW:c * FCW + w], ident[:, :])
                if c in (3, 5):
                    ins.then_inc(hm_turn, 1)

        def down(j, u, e):
            pe.wait_ge(hmT_act, j + 2)
            pe.wait_ge(hmT_dve, j + 2)
            pe.wait_ge(y_out, j + 1)
            for c in range(FCH):
                w = min(FCW, FF - c * FCW)
                ins = nc.tensor.matmul(ps[:, 7, 0:C], hmT[0:w, u, c, :],
                                       W2[0:w, bass.ds(e, 1), c, :].rearrange("p o n -> p (o n)"),
                                       start=(c == 0), stop=(c == FCH - 1))
            ins.then_inc(y_ps, 1)

        def step(j, i, u, first, last):
            e = pe.value_load(te[0:1, bass.ds(j, 1)], min_val=0, max_val=EXPERTS - 1)
            hidden(j, u, e)
            if not last:
                turn_x(j + 1, i + u, 1 - u)
            if not first:
                d = pe.value_load(te[0:1, bass.ds(j - 1, 1)], min_val=0, max_val=EXPERTS - 1)
                down(j - 1, 1 - u, d)
            turn_h(j, u)
            
        pe.wait_ge(w13_in, 16 * EXPERTS // 2)
        pe.wait_ge(routed, 1)
        turn_x(0, 0, 0)
        pe.wait_ge(w2_in, 16 * EXPERTS // 2)
        moe_loop(pe, step)
        d = pe.value_load(te[0:1, MT - 1:MT], min_val=0, max_val=EXPERTS - 1)
        down(MT - 1, (MT - 1) % 2, d)

    def moe_act(act):
        act.sem_inc(silu_ok, 2)
        act.sem_inc(hmT_act, 1)

        def bring(j, u):
            act.wait_ge(xs_turn, j + 3)
            nc.scalar.activation(xsT[:, u, :, :].rearrange("p k n -> p (k n)"), ps[:, 4, 0:C], ACT.Copy)\
              .then_inc(xs_out, 1)

        def step(j, i, u, first, last):
            for hf in range(2):
                act.wait_ge(h_ps, j * 2 + (hf + 1))
                act.wait_ge(hm_ok, j * 2 + hf + 1)
                nc.scalar.activation(sil[:, hf, 0:HALF], ps[:, 2 * hf, 0:HALF], ACT.Silu).then_inc(silu_ok, 1)
            if not last:
                bring(j + 1, 1 - u)
            act.wait_ge(hm_turn, j * 2 + 1)
            act.wait_ge(y_ps, (j - 1 if not (isinstance(j, int) and j == 0) else 0) + 1)
            nc.scalar.activation(hmT[0:FCW, u, 0:4, :].rearrange("p k n -> p (k n)"), ps[0:FCW, 5, :], ACT.Copy)\
              .then_inc(hmT_act, 1)

        bring(0, 0)
        moe_loop(act, step)

    def moe_dve(dve):
        dve.sem_inc(hm_ok, 2)
        dve.sem_inc(hmT_dve, 1)
        dve.sem_inc(y_out, 1)

        def evac(j, i, u):
            dve.wait_ge(y_ps, j + 2)
            dve.wait_ge(y_stored[u], i * 16 + 16)
            nc.vector.tensor_copy(yo[:, u, :], ps[:, 7, 0:C]).then_inc(y_out, 1)

        def step(j, i, u, first, last):
            for hf in range(2):
                dve.wait_ge(silu_ok, j * 2 + (hf + 1) + 2)
                if isinstance(j, int) and j < 2:
                    pass
                else:
                    dve.wait_ge(hm_turn, j * 2 - 2)
                nc.vector.tensor_tensor(hm[:, u, hf * HALF:(hf + 1) * HALF], sil[:, hf, 0:HALF],
                                        ps[:, 2 * hf + 1, 0:HALF], ALU.mult).then_inc(hm_ok, 1)
            if not first:
                evac(j - 1, i - 1 + u, 1 - u)
            dve.wait_ge(hm_turn, j * 2 + 2)
            dve.wait_ge(y_ps, (j - 1 if not (isinstance(j, int) and j == 0) else 0) + 1)
            w = FF - (FCH - 1) * FCW
            nc.vector.tensor_copy(hmT[0:FCW, u, 4, :], ps[0:FCW, 6, 0:P])
            nc.vector.tensor_copy(hmT[0:w, u, 5, :], ps[0:w, 6, P:2 * P]).then_inc(hmT_dve, 1)

        moe_loop(dve, step)
        evac(MT - 1, MT // 2 - 1, (MT - 1) % 2)

    back = [sem("back_a"), sem("back_b")]
    tc_in = [sem("tc_in_a"), sem("tc_in_b")]
    mixed = sem("mixed")
    out_stored = [sem("out_stored_a"), sem("out_stored_b")]

    def combine_pool(pool):
        for c in y_stored:
            pool.wait_ge(c, 16 * MT // 2 + 16)
        pool.wait_ge(y_ps, MT + 1)

        for g in range(G1):
            if g >= 2:
                pool.wait_ge(mixed, g)
            for t in range(4):
                for k in range(2):
                    pool.indirect_dma_start(ya[:, g % 2, t, k, :], None, y2_d,
                                            bass.IndirectOffsetOnAxis(pos[:, g * 4 + t, k:k + 1], 0),
                                            bounds_check=MT * P - 1, oob_is_err=False).then_inc(back[g % 2], 16)

    def combine_sp(sp):
        for c in out_stored:
            sp.sem_inc(c, 16)
        sp.wait_ge(y_ps, MT + 1)
        t2, o = tiles(t2_d), tiles(out.rearrange("b h w c -> (b h w) c"))

        def load(g, u):
            sp.dma_start(tc[:, u, :, :], t2[:, bass.ds(g * 4, 4), :]).then_inc(tc_in[u], 16)

        load(0, 0)
        load(1, 1)

        def store(g, u):
            sp.wait_ge(mixed, g + 2)
            sp.sem_inc(sp_passed, 1)
            sp.dma_start(o[:, bass.ds(g * 4, 4), :], oc[:, u, :, :]).then_inc(out_stored[u], 16)

        with sp.Fori(0, G1 // 2 - 1) as i:
            for u in range(2):
                store(i * 2 + u, u)
                load(i * 2 + (u + 2), u)
        for u in range(2):
            store(G1 - 2 + u, u)
        for c in out_stored:
            sp.wait_ge(c, 16 * G1 // 2 + 16)

    def combine_dve(dve):
        dve.sem_inc(mixed, 1)
        with dve.Fori(0, G1 // 2) as i:
            for u in range(2):
                relink()
                dve.wait_ge(tc_in[u], i * 16 + 16)
                dve.wait_ge(back[u], i * 128 + 128)
                dve.wait_ge(out_stored[u], i * 16 + 16)
                for k in range(2):
                    for t in range(4):
                        ins = nc.vector.scalar_tensor_tensor(
                            oc[:, u, t, :], ya[:, u, t, k, :], gate[:, k, bass.ds(i * 8 + u * 4 + t, 1)],
                            (tc if k == 0 else oc)[:, u, t, :], ALU.mult, ALU.add)
                    if k == 0:
                        link(ins)
                ins.then_inc(mixed, 1)

    block = ctx.enter_context(nc.Block())

    @block.sync
    def _(sp):
        prep_sp(sp)
        att0.sp(sp)
        mlp_sp(sp)
        for c in m_stored:
            sp.wait_ge(c, 16 * GROUPS // 2 + 16)
        att1.load(sp, 0)
        att1.sp(sp)
        m1_sp(sp)
        moe_sp(sp)
        combine_sp(sp)

    @block.gpsimd
    def _(pool):
        prep_pool(pool)
        bias_pool(pool)
        scatter_pool(pool)
        mask_pool(pool)
        att1.pool(pool)
        m1_pool(pool)
        dispatch_pool(pool)
        combine_pool(pool)

    @block.tensor
    def _(pe):
        pe.wait_ge(prep_p, 4)
        pe.wait_ge(prep_v, 1)
        att0.pe(pe)
        mlp_pe(pe)
        att1.pe(pe)
        m1_pe(pe)
        moe_pe(pe)

    @block.scalar
    def _(act):
        act.wait_ge(prep_v, 1)
        att0.act(act)
        mlp_act(act)
        att1.act(act)
        m1_act(act)
        moe_act(act)

    @block.vector
    def _(dve):
        prep_dve(dve)
        att0.dve(dve)
        mlp_dve(dve)
        att1.dve(dve)
        m1_dve(dve)
        moe_dve(dve)
        combine_dve(dve)


def layout(inputs):
    f = {k: np.asarray(v) for k, v in inputs.items()}
    two = lambda v: v.reshape(-1, P).T
    cols = np.concatenate([two(f["L0_conv_norm1_w"]), two(f["L0_conv_norm1_b"]), two(f["L0_conv_norm2_w"]),
                           two(f["L0_conv_norm2_b"]), two(f["L0_conv_qkv_b"][0:C]), two(f["L0_conv_qkv_b"][C:2 * C]),
                           two(f["L0_conv_fc1_b"]), two(f["L1_attn_bq"]), two(f["L1_attn_bk"])], axis=1)
    rows = np.stack([f["L0_conv_qkv_b"][2 * C:], f["L0_conv_proj_b"], f["L0_conv_gamma_1"][4], f["L0_conv_fc2_b"],
                     f["L0_conv_gamma_2"][4], f["L1_attn_bv"], f["L1_attn_bo"], f["L1_attn_gamma"], f["L1_attn_beta"]])
    rpb = np.pad(f["L0_conv_rpb"].transpose(1, 0, 2), ((0, 0), (0, 0), (SIDE, SIDE - 1)))
    toeplitz = np.stack([rpb[:, :, 38 - j:70 - j] for j in range(SIDE)]).reshape(SIDE, -1)
    shut = np.full((3, ROWS, SIDE, WT * ROWS, SIDE), BIG, np.float32)
    for kind, (row0, key0) in enumerate(((0, 0), (2 * ROWS, ROWS), (SIDE - ROWS, SIDE - WT * ROWS))):
        for i in range(ROWS):
            for j in range(SIDE):
                a = min(max(row0 + i - KWIN // 2, 0), SIDE - KWIN) - key0
                b = min(max(j - KWIN // 2, 0), SIDE - KWIN)
                shut[kind, i, j, a:a + KWIN, b:b + KWIN] = 0.0
    shut = shut.reshape(3, P, WK).transpose(1, 0, 2)
    w13 = np.concatenate([f["L1_ffn_w1"], f["L1_ffn_w3"]], axis=1).transpose(0, 2, 1)
    route_const = np.zeros((P, EXPERTS + 2 * P + MT), np.float32)
    route_const[:, 0:EXPERTS] = np.arange(EXPERTS) - EXPERTS
    route_const[:, EXPERTS:EXPERTS + P] = np.triu(np.ones((P, P)), 1)
    route_const[:, EXPERTS + P:EXPERTS + 2 * P] = 1.0
    route_const[:, EXPERTS + 2 * P:] = np.arange(MT)
    return {
        "x": f["x"].reshape(TOK, C), "rpb_toeplitz": toeplitz, "window_mask": shut, "cols": cols, "rows": rows,
        "w_qkv0": f["L0_conv_qkv_w"].T, "w_proj0": f["L0_conv_proj_w"].T, "w_fc1": f["L0_conv_fc1_w"].T,
        "w_fc2": f["L0_conv_fc2_w"].T,
        "w_qkv1": np.concatenate([f["L1_attn_Wq"], f["L1_attn_Wk"], f["L1_attn_Wv"]], axis=1),
        "w_o1": f["L1_attn_Wo"], "w_router": f["L1_ffn_router_w"].T, "edges": f["L1_attn_edge_index"],
        "w13": w13, "w2": np.pad(f["L1_ffn_w2"].transpose(0, 2, 1), ((0, 0), (0, FCH * FCW - FF), (0, 0))),
        "route_const": route_const,
    }


def kernel(**inputs):
    import concourse.bacc as bacc
    from concourse.bass_utils import run_bass_kernel_spmd

    arrays = {name: np.ascontiguousarray(a) for name, a in layout(inputs).items()}
    nc = bacc.Bacc("TRN2", target_bir_lowering=False, num_devices=1)
    args = [nc.dram_tensor(f"in_{name}_dram", a.shape, mybir.dt.from_np(a.dtype), kind="ExternalInput").ap()
            for name, a in arrays.items()]
    out = nc.dram_tensor("out_0_dram", (BATCH, SIDE, SIDE, C), F32, kind="ExternalOutput").ap()
    build_program(nc, *args, out)
    if not nc.is_finalized():
        nc.finalize()
    r = run_bass_kernel_spmd(nc, [{f"in_{name}_dram": a for name, a in arrays.items()}], core_ids=[0])
    return r.results[0]["out_0_dram"]
```

```python
from contextlib import ExitStack

import numpy as np

import concourse.bass as bass
from concourse import mybir

F32 = mybir.dt.float32
F32R = mybir.dt.float32r
BF16 = mybir.dt.bfloat16
I32 = mybir.dt.int32
ACT = mybir.ActivationFunctionType
ALU = mybir.AluOpType
AX = mybir.AxisListType

P = 128
BATCH, SIDE, C, HEADS, HD = 4, 32, 256, 8, 32
N = SIDE * SIDE
TOK = BATCH * N
KC = C // P
QT = N // P
TILES = TOK // P
HID = 4 * C
HCH = HID // P
KWIN = 7
ROWS = P // SIDE
WT = 3
WK = WT * P
EXPERTS = 8
FF = 682
FCH = 6
FCW = 114
HALF = FF // 2
SLOTS = 2 * TOK
MT = 72
CHUNKS = BATCH
EDGES = 69632
ECOL = EDGES // P
COPIES = 4
EBATCH = 16
CELLS = N * N
BIG = 3.0e38
NO_EDGE = 2.0 ** 31
SCALE = float(HD) ** -0.5
BANK = 512
PARTS = 3
STAGE = 16 * PARTS * 4
FLOOR_TILES = (SLOTS + EXPERTS * (P - 1)) // P
assert FLOOR_TILES <= MT and ECOL % EBATCH == 0 and FCH * FCW >= FF


def build_program(nc, x, rpb_toeplitz, window_mask, cols, rows, w_qkv0, w_proj0, w_fc1, w_fc2,
                  w_qkv1, w_o1, w_router, edges, w13, w2, route_const, out):
    ctx = ExitStack()
    base = (nc.sbuf_base + 63) // 64 * 64
    place = {"at": base}

    def sb(name, shape, dt, at=None):
        size = 4 if dt in (F32, F32R, I32) else 2
        n = int(np.prod(shape[1:])) * size
        if at is None:
            at = place["at"]
            place["at"] = (at + n + 31) // 32 * 32
        return nc.alloc_sbuf_tensor_at(name, list(shape), dt, offset=at)

    def dram(name, shape, dt):
        return nc.dram_tensor(name, list(shape), dt, kind="Internal").ap()

    def sem(name):
        return ctx.enter_context(nc.semaphore(name))


    ident = sb("ident", [P, P], F32)
    zeros = sb("zeros", [P, C], F32)
    col = sb("col", [P, cols.shape[1]], F32)
    row = sb("row", [P, rows.shape[0] * C], F32)
    edge_at = sb("edge_at", [P, ECOL], I32)
    edge_slot = sb("edge_slot", [P, EBATCH], I32)
    stats = sb("stats", [P, QT, 6], F32)
    mv = sb("mv", [P, QT, 2], F32)
    nwt = sb("nwt", [P, 3, QT], F32)
    nwi = sb("nwi", [P, QT], I32)
    nmax = sb("nmax", [P, 4], F32)
    rsum = sb("rsum", [P, 2, HEADS], F32)
    rinv = sb("rinv", [P, 4], F32)
    rexp = sb("rexp", [P, 2, P], F32)
    rT = sb("rT", [P, 2, P], F32)
    oTn = sb("oTn", [P, 2, KC, P], F32)
    wo1 = sb("wo1", [P, KC, C], F32)
    wr = sb("wr", [P, KC, EXPERTS], F32)
    at_w0 = place["at"]
    wq0 = sb("wq0", [P, KC, 3 * C], F32)
    wp0 = sb("wp0", [P, KC, C], F32)
    at_wf1 = place["at"]
    wf1 = sb("wf1", [P, KC, HID], F32)
    wf2 = sb("wf2", [P, HCH, C], F32)
    wq1 = sb("wq1", [P, KC, 3 * C], F32, at=at_w0)
    at_bias = place["at"]
    bias = sb("bias", [P, 3, HEADS, WK], F32)
    mask = sb("mask", [P, QT, N], BF16, at=at_bias)
    mask_tile = sb("mask_tile", [P, 2, N], BF16, at=at_bias + 2 * QT * N)
    at_att = place["at"]
    pT = sb("pT", [P, HEADS, N], F32)
    pT0 = sb("pT0", [P, HEADS, WK], F32, at=at_att)
    xhs = [sb("xh0", [P, QT, C], F32, at=at_att + 24576), sb("xh1", [P, QT, C], F32, at=at_bias + 2 * QT * N + 4 * N)]
    hT = sb("hT", [P, KC, N], F32, at=at_att + 8192)
    k_hi = sb("k_hi", [P, KC, N], F32R, at=at_att + 16384)
    k_lo = sb("k_lo", [P, KC, N], F32R, at=at_att + 24576)
    at_k = place["at"]
    kst = sb("kst", [P, HEADS, N], F32R)
    toep = sb("toep", [P, 20, HEADS, SIDE], F32, at=at_k)
    qst = sb("qst", [P, 2, HEADS, P], F32R)
    q_pair = [sb("q_pair_a", [P, HEADS, 2 * P], F32R, at=place["at"] - 8192),
              sb("q_pair_b", [P, HEADS, 2 * P], F32R, at=at_att + 16384)]
    at_q = place["at"]
    q_hi = sb("q_hi", [P, KC, N], F32R)
    q_lo = sb("q_lo", [P, KC, N], F32R)
    vt = sb("vt", [P, QT, C], F32)
    at_m = place["at"]
    msc = sb("msc", [P, 2, N], F32)
    prob = sb("prob", [P, 2, N], F32)
    msc0 = sb("msc0", [P, 4, WK], F32, at=at_m)
    prob0 = sb("prob0", [P, 4, WK], F32, at=at_m + 4 * WK * 4)
    big = sb("big", [P, 2048], BF16, at=at_m - 8192)
    e_src = sb("e_src", [P, ECOL], I32, at=at_att + 4608)
    e_dst = sb("e_dst", [P, ECOL], I32, at=at_att + 6784)
    e_tmp = sb("e_tmp", [P, ECOL], F32, at=at_att + 8960)
    wmask = sb("wmask", [P, 3, WK], F32, at=at_att)
    mcopy = sb("mcopy", [P, 2, COPIES, N], BF16, at=at_m)
    at_xb = place["at"]
    xb = sb("xb", [P, QT, C], F32)
    res = sb("res", [P, QT, C], F32)
    assert place["at"] <= nc.sbuf_usable_end

    ps = nc.alloc_psum_tensor("ps", [P, 8, BANK], F32)

    x1_d = dram("x1_d", [TOK, C], F32)
    x2_d = dram("x2_d", [TOK, C], F32)
    y_d = dram("y_d", [TOK, C], F32)
    mask_d = dram("mask_d", [COPIES * CELLS, 1], BF16)
    t2_d = dram("t2_d", [TOK, C], F32)
    xs_d = dram("xs_d", [MT * P, C], F32)
    y2_d = dram("y2_d", [MT * P, C], F32)

    def tiles(ap):
        return ap.rearrange("(n p) c -> p n c", p=P)

    NCOL = ["n1w", "n1b", "n2w", "n2b", "qb0", "kb0", "fb", "qb1", "kb1"]
    cw = {"fb": HCH}
    cat, at_c = {}, 0
    for nme in NCOL:
        cat[nme] = at_c
        at_c += cw.get(nme, KC)
    NROW = ["vb0", "pb0", "g1", "f2b", "g2", "vb1", "ob1", "gam", "bet"]
    rat = {nme: i for i, nme in enumerate(NROW)}

    def rowv(nme):
        return row[:, rat[nme] * C:(rat[nme] + 1) * C]

    def colv(nme, i):
        return col[:, cat[nme] + i:cat[nme] + i + 1]

    ld = sem("ld")
    ld_b = sem("ld_b")
    edge_ld = sem("edge_ld")
    prep_v = sem("prep_v")
    prep_p = sem("prep_p")
    chain = sem("chain")
    edge_ready = sem("edge_ready")
    big_ready = sem("big_ready")
    mask_init = sem("mask_init")
    slot_copy = sem("slot_copy")
    scat = [sem(f"scat{k}") for k in range(COPIES)]
    mask_in = [sem(f"mask_in{k}") for k in range(2)]
    mask_half = sem("mask_half")
    mask_ok = sem("mask_ok")
    ld_f = sem("ld_f")
    wf_ok = sem("wf_ok")
    bias_ok = sem("bias_ok")
    sp_passed, pool_passed, dve_passed = sem("sp_passed"), sem("pool_passed"), sem("dve_passed")
    links = [0]

    def link(ins):
        links[0] += 1
        ins.then_inc(chain, 1)
        nc.vector.wait_ge(chain, links[0])

    def relink():
        nc.vector.sem_clear(chain)
        links[0] = 0

    def rsqrt(n, mv=mv, nwt=nwt, nwi=nwi, parts=(0, 1, 2)):
        v, y, t = nwt[:, 0, 0:n], nwt[:, 1, 0:n], nwt[:, 2, 0:n]
        g = nwi[:, 0:n].bitcast(F32)
        if 0 in parts:
            link(nc.vector.tensor_scalar(v, mv[:, 0:n, 1], 1e-5, None, ALU.add))
            link(nc.vector.tensor_scalar(nwi[:, 0:n], v.bitcast(I32), 1, None, ALU.logical_shift_right))
            link(nc.vector.tensor_scalar(nwi[:, 0:n], nwi[:, 0:n], -1.0, float(0x5F3759DF), ALU.mult, ALU.add))
        for k in parts:
            g = g if k == 0 else y
            link(nc.vector.tensor_tensor(t, g, g, ALU.mult))
            link(nc.vector.tensor_tensor(t, t, v, ALU.mult))
            link(nc.vector.tensor_scalar(t, t, -0.5, 1.5, ALU.mult, ALU.add))
            link(nc.vector.tensor_tensor(y, g, t, ALU.mult))

    class Attention:

        def __init__(self, n, src, dst, wqkv, wout, kw, local):
            self.n, self.src, self.dst, self.wqkv, self.wout = n, src, dst, wqkv, wout
            self.kw, self.local = kw, local
            self.nb = (kw + BANK - 1) // BANK
            self.kc = kw // P
            self.xh = xhs[n]
            self.depth, self.lag = (4, 1) if local else (2, 0)
            self.over = 8
            self.msc, self.prob = (msc0, prob0) if local else (msc, prob)
            self.pT = pT0 if local else pT
            c = lambda s: sem(f"{s}{n}")
            self.x_in = c("x_in")
            self.x_norm = c("x_norm")
            self.hT_ps = c("hT_ps")
            self.hT_act = c("hT_act")
            self.hT_dve = c("hT_dve")
            self.res_ok = c("res_ok")
            self.proj_ps = c("proj_ps")
            self.proj_hi = c("proj_hi")
            self.proj_out = c("proj_out")
            self.k_staged = c("k_staged")
            self.q_staged = [c("q_staged_a"), c("q_staged_b")]
            self.qk = c("qk")
            self.masked = c("masked")
            self.exp = c("exp")
            self.p_ps = c("p_ps")
            self.p_act = c("p_act")
            self.p_dve = c("p_dve")
            self.r_exp = c("r_exp")
            self.pv = c("pv")
            self.r_act = c("r_act")
            self.o_norm = c("o_norm")
            self.wo_ps = c("wo_ps")
            self.wo_out = c("wo_out")
            self.stored = c("stored")
            self.mask_set = c("mask_set")

        def steps(self, g, s):
            return g * 16 + s

        def set_tile(self, tp):
            self.tp_of = tp

        def freed(self, g, s):
            back = s + 1 - self.depth
            return g * 16 + (back if back >= 0 or self.prev else 0)

        def later(self, g, s, prev, rest, of=lambda pair: None):
            r = s - self.lag
            if prev and r < self.over:
                of(-1)
                rest(g - 1, r + 16)
            of(0)
            if r >= 0:
                rest(g, r)

        def chunk(self, g, s, j):
            m = self.nb * s + j
            return m % 2, g * (8 * self.nb) + m // 2

        def key_tile(self, tp, u):
            return min(max(2 * tp + u - 1, 0), QT - WT) if self.local else 0

        def kind(self, tp, u):
            return {0: 0, QT - 1: 2}.get(2 * tp + u, 1)

        def loop(self, eng, b, prelude, pair, tail):
            prelude(b)
            pair(b * 4, 0, False)
            if self.local:
                for tp in range(1, QT // 2):
                    pair(b * 4 + tp, tp, True)
            else:
                with eng.Fori(1, QT // 2) as tp:
                    pair(b * 4 + tp, tp, True)
            tail(b * 4 + 4)

        def load(self, sp, b):
            sp.dma_start(xb[:, :, :], tiles(self.src)[:, bass.ds(b * QT, QT), :]).then_inc(self.x_in, 16)

        def sp(self, sp):
            sp.sem_inc(self.stored, 16)
            dst = tiles(self.dst)

            def stage_k(b):
                if self.local:
                    sp.wait_ge(bias_ok, 3)
                sp.wait_ge(self.proj_out, b * 12 + 4)
                sp.sem_inc(sp_passed, 1)
                sp.wait_ge(self.qk, b * 64 + 1)
                sp.sem_inc(sp_passed, 1)
                for r, half in enumerate((k_hi, k_hi, k_lo)):
                    for j in range(4):
                        sp.dma_start(kst[32 * r:32 * r + 32, :, :].rearrange("p (c j) n -> p c j n", j=4)[:, :, j, :]
                                     .bitcast(F32), half[32 * j:32 * j + 32, :, :].bitcast(F32)).then_inc(self.k_staged, 16)

            def stage(g, tp, u):
                sp.wait_ge(self.qk, (g * 16 + 8 * (u - 1) if u else g * 16 - 8 if not isinstance(tp, int) or tp else g * 16) + 1)
                sp.sem_inc(sp_passed, 1)
                t = tp * 2 + u
                for r, half in enumerate((q_hi, q_lo, q_hi)):
                    for j in range(4):
                        sp.dma_start(
                            qst[32 * r:32 * r + 32, u, :, :].rearrange("p (c j) n -> p c j n", j=4)[:, :, j, :]
                            .bitcast(F32), half[32 * j:32 * j + 32, :, bass.ds(t * P, P)].bitcast(F32)).then_inc(self.q_staged[u], 16)

            def stage_pair(g, tp):
                for r, half in enumerate((q_hi, q_lo, q_hi)):
                    for j in range(4):
                        sp.dma_start(
                            q_pair[tp % 2][32 * r:32 * r + 32, :, :].rearrange("p (c j) n -> p c j n", j=4)[:, :, j, :]
                            .bitcast(F32), half[32 * j:32 * j + 32, :, tp * 2 * P:(tp + 1) * 2 * P].bitcast(F32))\
                          .then_inc(self.q_staged[tp % 2], 16)

            def store(g, tp, u):
                sp.wait_ge(self.wo_out, g * 2 + (u + 1) + 1)
                sp.sem_inc(sp_passed, 1)
                sp.dma_start(dst[:, bass.ds(g * 2 + u, 1), :], res[:, bass.ds(tp * 2 + u, 1), :])\
                  .then_inc(self.stored, 16)

            def batch(b, more):
                stage_k(b)
                sp.wait_ge(self.proj_out, b * 12 + 8)
                sp.sem_inc(sp_passed, 1)
                if self.local:
                    stage_pair(b * 4, 0)
                    sp.wait_ge(self.k_staged, b * STAGE + STAGE)
                    sp.sem_inc(sp_passed, 1)
                    stage_pair(b * 4 + 1, 1)
                else:
                    for u in range(2):
                        stage(b * 4, 0, u)
                if more:
                    sp.wait_ge(self.res_ok, b + 2)
                    sp.sem_inc(sp_passed, 1)
                    self.load(sp, b + 1)
                if self.local:
                    for tp in range(QT // 2):
                        if tp + 2 < QT // 2:
                            sp.wait_ge(self.qk, b * 64 + (16 * tp + 17))
                            sp.sem_inc(sp_passed, 1)
                            stage_pair(b * 4 + (tp + 2), tp + 2)
                        for u in range(2):
                            store(b * 4 + tp, tp, u)
                else:
                    with sp.Fori(1, QT // 2) as tp:
                        for u in range(2):
                            stage(b * 4 + tp, tp, u)
                            store(b * 4 + tp - 1, tp - 1, u)
                    for u in range(2):
                        store(b * 4 + 3, QT // 2 - 1, u)

            with sp.Fori(0, BATCH - 1) as b:
                batch(b, True)
            batch(BATCH - 1, False)

        def pe(self, pe):
            pe.sem_inc(self.qk, 1)
            pe.sem_inc(self.p_ps, 1)
            pe.sem_inc(self.pv, 1)

            def prelude(b):
                for hf in range(2):
                    pe.wait_ge(self.x_norm, b * QT + 4 * hf + 4)
                    if hf == 1:
                        pe.wait_ge(self.wo_out, b * QT + 1)
                    for c in range(KC):
                        bank = 4 + 2 * hf + c
                        for t in range(4):
                            ins = nc.tensor.transpose(ps[:, bank, t * P:(t + 1) * P],
                                                      self.xh[:, 4 * hf + t, c * P:(c + 1) * P], ident[:, :])
                        ins.then_inc(self.hT_ps, 1)
                pe.wait_ge(self.hT_act, b * 2 + 2)
                pe.wait_ge(self.hT_dve, b * 2 + 2)
                job = 0
                for part in (1, 0):
                    for c in range(KC):
                        for hf in range(2):
                            if job >= 4:
                                pe.wait_ge(self.proj_out, b * 12 + (job - 3))
                            for k in range(KC):
                                ins = nc.tensor.matmul(ps[:, job % 4, :],
                                                       self.wqkv[:, k, part * C + c * P:part * C + (c + 1) * P],
                                                       hT[:, k, hf * BANK:(hf + 1) * BANK],
                                                       start=(k == 0), stop=(k == KC - 1))
                            ins.then_inc(self.proj_ps, 1)
                            job += 1
                for t2 in range(QT // 2):
                    pe.wait_ge(self.proj_out, b * 12 + (job - 3))
                    for u in range(2):
                        t = 2 * t2 + u
                        for k in range(KC):
                            ins = nc.tensor.matmul(ps[:, job % 4, u * C:(u + 1) * C], hT[:, k, t * P:(t + 1) * P],
                                                   self.wqkv[:, k, 2 * C:3 * C], start=(k == 0), stop=(k == KC - 1))
                    ins.then_inc(self.proj_ps, 1)
                    job += 1
                pe.wait_ge(self.proj_out, b * 12 + 12)
                pe.wait_ge(self.k_staged, b * STAGE + STAGE)

            def scores(g, tp, s):
                u, h = divmod(s, HEADS)
                if h == 0 and not self.local:
                    pe.wait_ge(self.q_staged[u], g * STAGE + STAGE)
                if s == 0 and self.local:
                    pe.wait_ge(self.q_staged[tp % 2], self.b * (2 * STAGE) + STAGE * (tp // 2 + 1))
                rows = PARTS * HD
                q = q_pair[tp % 2][0:rows, h, u * P:(u + 1) * P] if self.local else qst[0:rows, u, h, :]
                pe.wait_ge(self.masked, self.freed(g, s) + 1)
                k0 = self.key_tile(tp, u) * P
                for i in range(self.nb):
                    w = min(BANK, self.kw - i * BANK)
                    ins = nc.tensor.matmul(ps[:, (self.nb * s) % 4 + i, 0:w], q,
                                           kst[0:rows, h, k0 + i * BANK:k0 + i * BANK + w], start=True, stop=True)
                ins.then_inc(self.qk, 1)

            def turn(g, s):
                pe.wait_ge(self.exp, self.steps(g, s + 1) + 1)
                for j in range(self.nb):
                    odd, m = self.chunk(g, s, j)
                    pe.wait_ge(self.p_dve if odd else self.p_act, m + 1)
                    n = min(4, self.kc - 4 * j)
                    for i in range(n):
                        k = 4 * j + i
                        ins = nc.tensor.transpose(ps[:, 4 + odd, i * P:(i + 1) * P],
                                                  self.prob[:, s % self.depth, k * P:(k + 1) * P], ident[:, :])
                    ins.then_inc(self.p_ps, 1)

            def values(g, u, c, half):
                s = 8 * u + 4 * c + 3
                for j in range(self.nb):
                    odd, m = self.chunk(g, s, j)
                    pe.wait_ge(self.p_dve if odd else self.p_act, m + 2)
                if self.nb == 1:
                    odd, m = self.chunk(g, s - 1, 0)
                    pe.wait_ge(self.p_dve if odd else self.p_act, m + 2)
                if c == 1 and half == 0:
                    pe.wait_ge(self.wo_out, g * 2 + u + 1)
                split = (self.kc + 1) // 2
                for k in range(split) if half == 0 else range(split, self.kc):
                    for j in range(4):
                        h = 4 * c + j
                        v = vt[:, self.key_tile(self.tp_of, u) + k, 32 * h:32 * h + 32]
                        nc.tensor.matmul(ps[32 * j:32 * j + 32, 6 + c, 0:P], v,
                                         self.pT[:, h, k * P:(k + 1) * P], start=(k == 0), stop=(k == self.kc - 1))
                if half == 0:
                    return
                pe.wait_ge(self.r_exp, g * 4 + (2 * u + c + 1))
                nc.tensor.transpose(ps[:, 6 + c, P:2 * P], rexp[:, c, :], ident[:, :]).then_inc(self.pv, 1)

            def project(g, u):
                pe.wait_ge(self.o_norm, g * 4 + (2 * u + 2))
                for c in range(KC):
                    ins = nc.tensor.matmul(ps[:, 7, 2 * P:4 * P], oTn[:, u, c, :], self.wout[:, c, :],
                                           start=(c == 0), stop=(c == KC - 1))
                ins.then_inc(self.wo_ps, 1)

            def rest(g, s):
                if s - 2 in range(16):
                    turn(g, s - 2)
                for u in range(2):
                    if s == 8 * u + 14:
                        project(g, u)
                for u in range(2):
                    for c in range(2):
                        if s - (8 * u + 4 * c) in (6, 7):
                            values(g, u, c, s % 2)

            def pair(g, tp, prev):
                self.prev = prev
                for s in range(16):
                    scores(g, tp, s)
                    self.later(g, s, prev, rest, lambda n: self.set_tile(tp + n))

            def tail(g):
                self.tp_of = QT // 2 - 1
                for s in range(-self.lag, self.over):
                    rest(g - 1, s + 16)

            with pe.Fori(0, BATCH) as b:
                self.b = b
                self.loop(pe, b, prelude, pair, tail)

        def act(self, act):
            act.sem_inc(self.exp, 1)
            act.sem_inc(self.p_act, 1)

            def prelude(b):
                for hf in range(2):
                    act.wait_ge(self.hT_ps, b * 4 + 2 * hf + 1)
                    o, i = hT[:, 0, hf * BANK:(hf + 1) * BANK], ps[:, 4 + 2 * hf, :]
                    if self.local:
                        ins = nc.scalar.activation(o, i, ACT.Identity, scale=colv("n1w", 0), bias=colv("n1b", 0))
                    else:
                        ins = nc.scalar.activation(o, i, ACT.Copy)
                    ins.then_inc(self.hT_act, 1)
                job = 0
                for name, hi in (("kb", k_hi), ("qb", q_hi)):
                    for c in range(KC):
                        for hf in range(2):
                            act.wait_ge(self.proj_ps, b * 12 + (job + 1))
                            nc.scalar.activation(hi[:, c, hf * BANK:(hf + 1) * BANK], ps[:, job % 4, :], ACT.Identity,
                                                 bias=colv(f"{name}{self.n}", c)).then_inc(self.proj_hi, 1)
                            job += 1

            def softmax(g, s):
                act.wait_ge(self.masked, self.steps(g, s + 1) + 1)
                self.p_ps_turned(act, g, s)
                u, h = divmod(s, HEADS)
                d = s % self.depth
                nc.scalar.activation(self.prob[:, d, 0:self.kw], self.msc[:, d, 0:self.kw], ACT.Exp,
                                     scale=-1.0, bias=nmax[:, d:d + 1],
                                     accum_out=rsum[:, u, h:h + 1]).then_inc(self.exp, 1)

            def rest(g, s):
                if s - 2 in range(16):
                    for j in range(self.nb):
                        odd, m = self.chunk(g, s - 2, j)
                        if not odd:
                            self.copy_out(act, g, s - 2, j)
                for u in range(2):
                    for c in range(2):
                        if s == 8 * u + 4 * c + 8:
                            act.wait_ge(self.pv, g * 4 + (2 * u + c + 1) + 1)
                            nc.scalar.activation(rT[:, c, :], ps[:, 6 + c, P:2 * P], ACT.Copy)\
                              .then_inc(self.r_act, 1)

            def pair(g, tp, prev):
                self.prev = prev
                for s in range(16):
                    self.later(g, s, prev, rest)
                    softmax(g, s)

            def tail(g):
                for s in range(-self.lag, self.over):
                    rest(g - 1, s + 16)

            with act.Fori(0, BATCH) as b:
                self.loop(act, b, prelude, pair, tail)

        def p_ps_turned(self, act, g, s):
            back = s - self.depth
            if back >= 0:
                act.wait_ge(self.p_ps, g * (16 * self.nb) + self.nb * (back + 1) + 1)
            elif self.prev:
                act.wait_ge(self.p_ps, g * (16 * self.nb) - self.nb * (-back - 1) + 1)

        def copy_out(self, eng, g, s, j):
            odd, m = self.chunk(g, s, j)
            u, h = divmod(s, HEADS)
            w = min(BANK, self.kw - j * BANK)
            eng.wait_ge(self.p_ps, g * (16 * self.nb) + (self.nb * s + j + 1) + 1)
            eng.wait_ge(self.pv, (g * 4 + (2 * u + h // 4 - 1) if 2 * u + h // 4 >= 1 else g * 4 - 1 if self.prev else g * 4) + 1)
            o, i = self.pT[:, h, j * BANK:j * BANK + w], ps[:, 4 + odd, 0:w]
            if odd:
                nc.vector.tensor_copy(o, i).then_inc(self.p_dve, 1)
            else:
                nc.scalar.activation(o, i, ACT.Copy).then_inc(self.p_act, 1)

        def pool(self, pool):
            def pair(g, tp, prev):
                for u in range(2):
                    if prev:
                        pool.wait_ge(self.masked, g * 16 + (8 * u - 8) + 1)
                        pool.sem_inc(pool_passed, 1)
                    nc.gpsimd.tensor_copy(mask_tile[:, u, :], mask[:, bass.ds(tp * 2 + u, 1), :].rearrange("p o n -> p (o n)"))\
                      .then_inc(self.mask_set, 1)

            pair(0, 0, False)
            with pool.Fori(1, QT // 2) as tp:
                pair(tp, tp, True)
            with pool.Fori(1, BATCH) as b:
                with pool.Fori(0, QT // 2) as tp:
                    pair(b * 4 + tp, tp, True)

        def dve(self, dve):
            dve.sem_inc(self.masked, 1)
            dve.sem_inc(self.p_dve, 1)
            dve.sem_inc(self.res_ok, 1)
            dve.sem_inc(self.wo_out, 1)
            n = self.n

            def normal(b, s):
                if s > 12:
                    return
                relink()
                if s < 2:
                    if s == 0:
                        dve.wait_ge(self.x_in, b * 16 + 16)
                    for t in range(4 * s, 4 * s + 4):
                        ins = nc.vector.bn_stats(stats[:, t, :], xb[:, t, :])
                    link(ins)
                    for t in range(4 * s, 4 * s + 4):
                        ins = nc.vector.bn_aggr(mv[:, t, :], stats[:, t, :])
                    link(ins)
                elif s < 5:
                    rsqrt(QT, parts=(s - 2,))
                else:
                    t = s - 5
                    nc.vector.tensor_scalar(self.xh[:, t, :], xb[:, t, :], mv[:, t, 0:1], nwt[:, 1, t:t + 1],
                                            ALU.subtract, ALU.mult).then_inc(self.x_norm, 1)

            def prelude(b):
                for hf in range(2):
                    dve.wait_ge(self.hT_ps, b * 4 + 2 * hf + 2)
                    o, i = hT[:, 1, hf * BANK:(hf + 1) * BANK], ps[:, 5 + 2 * hf, :]
                    if self.local:
                        ins = nc.vector.tensor_scalar(o, i, colv("n1w", 1), colv("n1b", 1), ALU.mult, ALU.add)
                    else:
                        ins = nc.vector.tensor_copy(o, i)
                    ins.then_inc(self.hT_dve, 1)
                job = 0
                for name, hi, lo in (("kb", k_hi, k_lo), ("qb", q_hi, q_lo)):
                    for c in range(KC):
                        for hf in range(2):
                            dve.wait_ge(self.proj_hi, b * 8 + (job + 1))
                            w = slice(hf * BANK, (hf + 1) * BANK)
                            nc.vector.scalar_tensor_tensor(lo[:, c, w], ps[:, job % 4, :], colv(f"{name}{n}", c),
                                                           hi[:, c, w].bitcast(F32), ALU.add, ALU.subtract)\
                              .then_inc(self.proj_out, 1)
                            job += 1
                dve.wait_ge(self.stored, b * (16 * QT) + 16)
                r = rowv("pb0" if self.local else "ob1").rearrange("p (o c) -> p o c", o=1).broadcast_to([P, QT, C])
                nc.vector.tensor_tensor(res[:, :, :], xb[:, :, :] if self.local else self.xh[:, :, :], r, ALU.add)\
                  .then_inc(self.res_ok, 1)
                if self.local:
                    dve.wait_ge(mask_init, 16)
                vb = rowv(f"vb{n}").rearrange("p (o c) -> p o c", o=1).broadcast_to([P, 2, C])
                for t2 in range(QT // 2):
                    dve.wait_ge(self.proj_ps, b * 12 + (job + 1))
                    nc.vector.tensor_tensor(vt[:, 2 * t2:2 * t2 + 2, :],
                                            ps[:, job % 4, :].rearrange("p (u c) -> p u c", u=2), vb, ALU.add)\
                      .then_inc(self.proj_out, 1)
                    job += 1

            def add_mask(g, tp, s):
                u, h = divmod(s, HEADS)
                dve.wait_ge(self.qk, self.steps(g, s + 1) + 1)
                dve.wait_ge(self.exp, self.freed(g, s) + 1)
                dve.sem_inc(dve_passed, 1)
                if self.local and tp == 0 and s == 0:
                    dve.wait_ge(bias_ok, 3)
                if self.local:
                    extra = bias[:, self.kind(tp, u), h, :]
                else:
                    extra = mask_tile[:, u, :]
                    if h == 0:
                        dve.wait_ge(self.mask_set, g * 2 + (u + 1))
                        dve.sem_inc(dve_passed, 1)
                sc = ps[:, (self.nb * s) % 4:(self.nb * s) % 4 + self.nb, :].rearrange("p a n -> p (a n)")[:, 0:self.kw]
                d = s % self.depth
                nc.vector.tensor_tensor_reduce(out=self.msc[:, d, 0:self.kw], in0=sc, in1=extra, scale=1.0,
                                               scalar=BIG, op0=ALU.add, op1=ALU.min,
                                               accum_out=nmax[:, d:d + 1]).then_inc(self.masked, 1)

            def rest(g, s):
                if s - 2 in range(16):
                    for j in range(self.nb):
                        odd, m = self.chunk(g, s - 2, j)
                        if odd:
                            self.copy_out(dve, g, s - 2, j)
                for u in range(2):
                    for c in range(2):
                        if s == 8 * u + 4 * c + 5:
                            relink()
                            dve.wait_ge(self.exp, self.steps(g, 8 * u + 4 * c + 4) + 1)
                            link(nc.vector.reciprocal(rinv[:, :], rsum[:, u, 4 * c:4 * c + 4]))
                            nc.vector.tensor_copy(rexp[:, c, :].rearrange("p (h d) -> p h d", h=4),
                                                  rinv[:, :].rearrange("p (h o) -> p h o", o=1).broadcast_to([P, 4, HD]))\
                              .then_inc(self.r_exp, 1)
                        if s == 8 * u + 4 * c + 9:
                            dve.wait_ge(self.r_act, g * 4 + (2 * u + c + 1))
                            nc.vector.tensor_tensor(oTn[:, u, c, :], ps[:, 6 + c, 0:P], rT[:, c, :], ALU.mult)\
                              .then_inc(self.o_norm, 1)
                    if s == 8 * u + 15:
                        dve.wait_ge(self.wo_ps, g * 2 + (u + 1))
                        t = self.tp_of * 2 + u
                        r = res[:, bass.ds(t, 1), :].rearrange("p o c -> p (o c)")
                        nc.vector.tensor_tensor(r, ps[:, 7, 2 * P:4 * P], r, ALU.add).then_inc(self.wo_out, 1)

            def pair(g, tp, prev, following=None):
                self.prev = prev
                for s in range(16):
                    add_mask(g, tp, s)
                    if following is not None:
                        normal(following, s)
                    self.later(g, s, prev, rest, lambda n: self.set_tile(tp + n))

            def tail(g):
                self.tp_of = QT // 2 - 1
                for s in range(-self.lag, self.over):
                    rest(g - 1, s + 16)

            def batch(b, more):
                following = b + 1 if more else None
                last = QT // 2 - 1
                prelude(b)
                pair(b * 4, 0, False)
                if self.local:
                    for tp in range(1, last):
                        pair(b * 4 + tp, tp, True)
                else:
                    with dve.Fori(1, last) as tp:
                        pair(b * 4 + tp, tp, True)
                pair(b * 4 + last, last, True, following)
                tail(b * 4 + 4)

            for s in range(13):
                normal(0, s)
            with dve.Fori(0, BATCH - 1) as b:
                batch(b, True)
            batch(BATCH - 1, False)

    att0 = Attention(0, x, x1_d, wq0, wp0, WK, True)
    att1 = Attention(1, x2_d, y_d, wq1, wo1, N, False)

    xm = sb("xm", [P, 2, 4, C], F32, at=at_xb)
    xmh = sb("xmh", [P, 4, C], F32, at=at_xb + 8192)
    mT = sb("mT", [P, KC, BANK], F32, at=at_xb + 12288)
    gel = sb("gel", [P, HCH, BANK], F32, at=at_q)
    gel_hi = sb("gel_hi", [P, HCH, BANK], F32R, at=at_k)
    gel_lo = sb("gel_lo", [P, HCH, BANK], F32R, at=at_q)
    mT_hi = sb("mT_hi", [P, KC, BANK], F32R, at=at_k + 16384)
    mT_lo = sb("mT_lo", [P, KC, BANK], F32R, at=at_xb + 12288)
    wf1_hi = sb("wf1_hi", [P, KC, HID], F32R, at=at_bias + 20480)
    wf2_hi = sb("wf2_hi", [P, HCH, C], F32R, at=at_bias + 28672)
    wf1_lo = sb("wf1_lo", [P, KC, HID], F32R, at=at_wf1)
    wf2_lo = sb("wf2_lo", [P, HCH, C], F32R, at=at_wf1 + 8192)
    x2t = sb("x2t", [P, 2, 4, C], F32, at=at_q + 16384)
    m_in = [sem("m_in_a"), sem("m_in_b")]
    wq1_in = sem("wq1_in")
    m_norm = sem("m_norm")
    m_turn = sem("m_turn")
    m_act = sem("m_act")
    m_dve = sem("m_dve")
    m_used = sem("m_used")
    m_hi = sem("m_hi")
    m_lo = sem("m_lo")
    g_hi = sem("g_hi")
    g_lo = sem("g_lo")
    wf_hi = sem("wf_hi")
    wf_lo = sem("wf_lo")
    f1_ps = sem("f1_ps")
    f1_out = sem("f1_out")
    f2_ps = sem("f2_ps")
    f2_out = sem("f2_out")
    m_stored = [sem("m_stored_a"), sem("m_stored_b")]
    GROUPS = TILES // 4

    def mlp_loop(eng, group):
        with eng.Fori(0, GROUPS // 2 - 1) as i:
            for u in range(2):
                group(i * 2 + u, i, u, True)
        for u in range(2):
            group(GROUPS - 2 + u, GROUPS // 2 - 1, u, u == 0)

    def mlp_sp(sp):
        for c in m_stored:
            sp.sem_inc(c, 16)
        x1, x2 = tiles(x1_d), tiles(x2_d)
        sp.wait_ge(att0.stored, 16 * TILES + 16)
        sp.sem_inc(sp_passed, 1)

        def load(g, i, u):
            sp.dma_start(xm[:, u, :, :], x1[:, bass.ds(g * 4, 4), :]).then_inc(m_in[u], 16)

        def group(g, i, u, more):
            if not isinstance(g, int):
                sp.wait_ge(m_used, g + 1)
                sp.sem_inc(sp_passed, 1)
                load(g + 2, i, u)
            zero_sp(sp, g)
            sp.wait_ge(f2_out, g * 4 + 5)
            sp.sem_inc(sp_passed, 1)
            sp.dma_start(x2[:, bass.ds(g * 4, 4), :], x2t[:, u, :, :]).then_inc(m_stored[u], 16)

        load(0, 0, 0)
        load(1, 0, 1)
        sp.dma_start(wq1[:, :, :], w_qkv1.rearrange("(k p) n -> p k n", p=P)).then_inc(wq1_in, 16)
        mlp_loop(sp, group)

    def mlp_pe(pe):
        def turn(g):
            pe.wait_ge(m_norm, g + 1)
            for c in range(KC):
                for t in range(4):
                    ins = nc.tensor.transpose(ps[:, 6 + c, t * P:(t + 1) * P], xmh[:, t, c * P:(c + 1) * P], ident[:, :])
                ins.then_inc(m_turn, 1)

        def group(g, i, u, more):
            pe.wait_ge(m_lo, g + 1)
            for h in range(HCH):
                pe.wait_ge(f1_out, (g * HCH + (h - 3) if h >= 3 else g * HCH) + 1)
                cols = slice(h * P, (h + 1) * P)
                parts = [(w, m, k) for k in range(KC) for w, m in ((wf1_hi, mT_hi), (wf1_hi, mT_lo), (wf1_lo, mT_hi))]
                for n, (w, m, k) in enumerate(parts):
                    ins = nc.tensor.matmul(ps[:, h % 4, :], w[:, k, cols], m[:, k, :],
                                           start=(n == 0), stop=(n == len(parts) - 1))
                ins.then_inc(f1_ps, 1)
            if more:
                turn(g + 1)
            pe.wait_ge(g_lo, g * HCH + HCH)
            for t in range(4):
                pe.wait_ge(f2_out, (g * 4 + (t - 1) if t else g * 4) + 1)
                parts = [(q, w, h) for h in range(HCH) for q, w in ((gel_hi, wf2_hi), (gel_hi, wf2_lo), (gel_lo, wf2_hi))]
                for n, (q, w, h) in enumerate(parts):
                    ins = nc.tensor.matmul(ps[:, 4 + t % 2, 0:C], q[:, h, t * P:(t + 1) * P], w[:, h, :],
                                           start=(n == 0), stop=(n == len(parts) - 1))
                ins.then_inc(f2_ps, 1)

        turn(0)
        pe.wait_ge(wf_lo, 2)
        mlp_loop(pe, group)

    def mlp_act(act):
        act.sem_inc(f1_out, 1)

        def bring(g):
            act.wait_ge(m_turn, g * 2 + 1)
            nc.scalar.activation(mT[:, 0, :], ps[:, 6, :], ACT.Identity, scale=colv("n2w", 0), bias=colv("n2b", 0))\
              .then_inc(m_act, 1)
            act.wait_ge(m_act, g + 1)
            act.wait_ge(m_dve, g + 1)
            nc.scalar.activation(mT_hi[:, :, :], mT[:, :, :], ACT.Copy).then_inc(m_hi, 1)

        def high(g, h):
            act.wait_ge(f1_out, g * HCH + (h + 1) + 1)
            nc.scalar.activation(gel_hi[:, h, :], gel[:, h, :], ACT.Copy).then_inc(g_hi, 1)

        def group(g, i, u, more):
            act.wait_ge(f2_out, g * 4 + 1)
            for h in range(HCH):
                act.wait_ge(f1_ps, g * HCH + (h + 1))
                nc.scalar.activation(gel[:, h, :], ps[:, h % 4, :], ACT.Gelu, bias=colv("fb", h)).then_inc(f1_out, 1)
                if h:
                    high(g, h - 1)
            high(g, HCH - 1)
            if more:
                bring(g + 1)

        act.wait_ge(wf_ok, 1)
        nc.scalar.activation(wf1_hi[:, :, :], wf1[:, :, :], ACT.Copy).then_inc(wf_hi, 1)
        nc.scalar.activation(wf2_hi[:, :, :], wf2[:, :, :], ACT.Copy).then_inc(wf_hi, 1)
        bring(0)
        mlp_loop(act, group)

    def mlp_dve(dve):
        dve.sem_inc(f2_out, 1)
        f2b = rowv("f2b").rearrange("p (o c) -> p o c", o=1).broadcast_to([P, 4, C])

        def normal(g, i, u):
            relink()
            dve.wait_ge(m_in[u], i * 16 + 16)
            for t in range(4):
                ins = nc.vector.bn_stats(stats[:, t, :], xm[:, u, t, :])
            link(ins)
            for t in range(4):
                ins = nc.vector.bn_aggr(mv[:, t, :], stats[:, t, :])
            link(ins)
            rsqrt(4)
            for t in range(4):
                ins = nc.vector.tensor_scalar(xmh[:, t, :], xm[:, u, t, :], mv[:, t, 0:1], nwt[:, 1, t:t + 1],
                                              ALU.subtract, ALU.mult)
            ins.then_inc(m_norm, 1)
            dve.wait_ge(m_stored[u], i * 16 + 16)
            nc.vector.tensor_tensor(x2t[:, u, :, :], xm[:, u, :, :], f2b, ALU.add).then_inc(m_used, 1)

        def turned(g, i, u):
            relink()
            dve.wait_ge(m_turn, g * 2 + 2)
            nc.vector.tensor_scalar(mT[:, 1, :], ps[:, 7, :], colv("n2w", 1), colv("n2b", 1), ALU.mult, ALU.add)\
              .then_inc(m_dve, 1)
            dve.wait_ge(m_hi, g + 1)
            nc.vector.tensor_tensor(mT_lo[:, :, :], mT[:, :, :], mT_hi[:, :, :].bitcast(F32), ALU.subtract).then_inc(m_lo, 1)

        def group(g, i, u, more):
            if more:
                normal(g + 1, i + u, 1 - u)
            for h in range(HCH):
                dve.wait_ge(g_hi, g * HCH + (h + 1))
                nc.vector.tensor_tensor(gel_lo[:, h, :], gel[:, h, :], gel_hi[:, h, :].bitcast(F32), ALU.subtract)\
                  .then_inc(g_lo, 1)
            if more:
                turned(g + 1, i + u, 1 - u)
            dve.wait_ge(m_used, g + 1)
            for t in range(4):
                dve.wait_ge(f2_ps, g * 4 + (t + 1))
                ins = nc.vector.tensor_tensor(x2t[:, u, t, :], ps[:, 4 + t % 2, 0:C], x2t[:, u, t, :], ALU.add)
                ins.then_inc(f2_out, 1)

        relink()
        dve.wait_ge(ld_f, 64)
        scale_rows(dve, "g2", wf2, "f2b", HCH).then_inc(wf_ok, 1)
        dve.wait_ge(wf_ok, 1)
        normal(0, 0, 0)
        for n, (lo, w, hi) in enumerate(((wf1_lo, wf1, wf1_hi), (wf2_lo, wf2, wf2_hi))):
            dve.wait_ge(wf_hi, n + 1)
            nc.vector.tensor_tensor(lo[:, :, :], w[:, :, :], hi[:, :, :].bitcast(F32), ALU.subtract).then_inc(wf_lo, 1)
        turned(0, 0, 0)
        dve.wait_ge(wq1_in, 16)
        relink()
        link(nc.vector.tensor_scalar(wq1[:, :, 0:C], wq1[:, :, 0:C], -SCALE, None, ALU.mult))
        mlp_loop(dve, group)

    def prep_sp(sp):
        att0.load(sp, 0)
        edge_view = edges.rearrange("a (p n) -> a p n", p=P)
        sp.dma_start(e_src[:, :], edge_view[0]).then_inc(edge_ld, 16)
        sp.dma_start(e_dst[:, :], edge_view[1]).then_inc(edge_ld, 16)
        for dst, src in ((col[:, :], cols), (wq0[:, :, :], w_qkv0.rearrange("(k p) n -> p k n", p=P)),
                         (wp0[:, :, :], w_proj0.rearrange("(k p) n -> p k n", p=P))):
            sp.dma_start(dst, src).then_inc(ld, 16)
        sp.dma_start(row[:, :].rearrange("p (r c) -> p r c", c=C), rows.rearrange("(o r) c -> o r c", o=1).broadcast_to([P, len(NROW), C]))\
          .then_inc(ld, 16)
        sp.dma_start(wmask[:, :, :], window_mask).then_inc(ld_b, 16)
        sp.wait_ge(prep_p, 3)
        for i in range(ROWS):
            sp.dma_start(toep[32 * i:32 * i + 32, i + 2:i + 15, :, :].rearrange("p a h c -> p (a h c)"), rpb_toeplitz)\
              .then_inc(ld_b, 16)
        sp.wait_ge(big_ready, 1)
        sp.dma_start(mask_d.rearrange("(p k n) o -> p k (n o)", p=P, n=2048),
                     big[:, :].rearrange("p (o n) -> p o n", o=1).broadcast_to([P, 16, 2048])).then_inc(mask_init, 16)
        for dst, src in ((wf1, w_fc1), (wf2, w_fc2), (wo1, w_o1), (wr, w_router)):
            sp.dma_start(dst[:, :, :], src.rearrange("(k p) n -> p k n", p=P)).then_inc(ld_f, 16)

    def zero_sp(sp, g):
        n = MT // GROUPS
        sp.dma_start(tiles(xs_d)[:, bass.ds(g * n, n), :],
                     zeros[:, :].rearrange("p (o c) -> p o c", o=1).broadcast_to([P, n, C])).then_inc(xs_zero, 16)

    def prep_pool(pool):
        nc.gpsimd.memset(ident[:, :], 0.0).then_inc(prep_p, 1)
        nc.gpsimd.memset(zeros[:, :], 0.0).then_inc(prep_p, 1)
        nc.gpsimd.memset(toep[:, :, :, :], 0.0).then_inc(prep_p, 1)
        pool.wait_ge(prep_p, 1)
        nc.gpsimd.affine_select(out=ident[:, :], in_=ident[:, :], compare_op=ALU.not_equal, fill=1.0,
                                base=0, pattern=[[-1, P]], channel_multiplier=1).then_inc(prep_p, 1)

    def scatter_pool(pool):
        pool.wait_ge(edge_ready, 1)
        pool.wait_ge(mask_init, 16)
        half = EBATCH // 2
        zero = zeros[:, :].bitcast(BF16)[:, 0:1]
        def columns(i):
            for x in range(EBATCH):
                if x in (0, 4):
                    a = 0 if x == 0 else half
                    nc.gpsimd.tensor_copy(edge_slot[:, a:a + half], edge_at[:, bass.ds(i * EBATCH + a, half)])\
                      .then_inc(slot_copy, 1)
                if x in (0, half):
                    pool.wait_ge(slot_copy, i * 2 + (1 if x == 0 else 2))
                    pool.sem_inc(pool_passed, 1)
                k = x % COPIES
                if x >= COPIES or not isinstance(i, int):
                    pool.wait_ge(scat[k], i * (EBATCH // COPIES * 16) + 16 * (x // COPIES))
                    pool.sem_inc(pool_passed, 1)
                pool.indirect_dma_start(mask_d, bass.IndirectOffsetOnAxis(edge_slot[:, x:x + 1], 0), zero, None,
                                        bounds_check=COPIES * CELLS - 1, oob_is_err=False).then_inc(scat[k], 16)

        columns(0)
        with pool.Fori(1, ECOL // EBATCH) as i:
            columns(i)

    def scale_rows(dve, nme, w, b, n):
        link(nc.vector.scalar_tensor_tensor(rowv(nme), rowv(nme), -1.0, rowv(nme), ALU.mult, ALU.max))
        g = rowv(nme).rearrange("p (o c) -> p o c", o=1).broadcast_to([P, n, C])
        nc.vector.tensor_tensor(rowv(b), rowv(b), rowv(nme), ALU.mult)
        return nc.vector.tensor_tensor(w[:, :, :], w[:, :, :], g, ALU.mult)

    def prep_dve(dve):
        nc.vector.memset(big[:, :], NO_EDGE).then_inc(big_ready, 1)
        relink()
        dve.wait_ge(edge_ld, 32)
        link(nc.vector.tensor_scalar(e_tmp[:, :], e_dst[:, :], float(N), None, ALU.is_ge))
        link(nc.vector.scalar_tensor_tensor(e_tmp[:, :], e_src[:, :], float(N), e_tmp[:, :], ALU.is_ge, ALU.max))
        link(nc.vector.scalar_tensor_tensor(e_src[:, :], e_src[:, :], float(N), e_dst[:, :], ALU.mult, ALU.add))
        link(nc.vector.scalar_tensor_tensor(edge_at[:, :], e_tmp[:, :], float(1 << 23), e_src[:, :], ALU.mult, ALU.add))
        for k in range(1, COPIES):
            v = edge_at[:, :].rearrange("p (n k) -> p n k", k=COPIES)[:, :, k]
            link(nc.vector.tensor_scalar(v, v, float(k * CELLS), None, ALU.add))
        nc.vector.memset(nwi[:, :], 0).then_inc(edge_ready, 1)
        dve.wait_ge(ld, 16 * 4)
        link(nc.vector.tensor_scalar(wq0[:, :, 0:C], wq0[:, :, 0:C], -SCALE, None, ALU.mult))
        for nme in ("qb0", "qb1"):
            link(nc.vector.tensor_scalar(col[:, cat[nme]:cat[nme] + KC], col[:, cat[nme]:cat[nme] + KC], -SCALE, None, ALU.mult))
        link(scale_rows(dve, "g1", wp0, "pb0", KC))
        nc.vector.memset(nwt[:, :, :], 0.0).then_inc(prep_v, 1)
        dve.wait_ge(prep_v, 1)

    def bias_pool(pool):
        pool.wait_ge(ld_b, 16 + 16 * ROWS)
        for kind, first in enumerate((8, 4, 0)):
            nc.gpsimd.tensor_tensor(
                bias[:, kind, :, :].rearrange("p h (r c) -> p h r c", c=SIDE),
                wmask[:, kind, :].rearrange("p (o r c) -> p o r c", o=1, c=SIDE).broadcast_to([P, HEADS, WT * ROWS, SIDE]),
                toep[:, first:first + WT * ROWS, :, :].rearrange("p r h c -> p h r c"), ALU.subtract)\
              .then_inc(bias_ok, 1)

    def mask_pool(pool):
        masks = mask_d.rearrange("(k t p n) o -> t p k (n o)", k=COPIES, t=QT, p=P)
        for c in scat:
            pool.wait_ge(c, 16 * (ECOL // COPIES))
        pool.wait_ge(att0.stored, 16 * TILES + 16)

        def load(t, u):
            pool.dma_start(mcopy[:, u, :, :], masks[t]).then_inc(mask_in[u], 16)

        load(0, 0)
        for t in range(QT):
            u = t % 2
            if t + 1 < QT:
                if t:
                    pool.wait_ge(mask_ok, t)
                load(t + 1, 1 - u)
            pool.wait_ge(mask_in[u], 16 * (t // 2 + 1))
            nc.gpsimd.tensor_tensor(mcopy[:, u, 0:2, :], mcopy[:, u, 0:2, :], mcopy[:, u, 2:4, :], ALU.mult)\
              .then_inc(mask_half, 1)
            pool.wait_ge(mask_half, t + 1)
            nc.gpsimd.tensor_tensor(mask[:, t, :], mcopy[:, u, 0, :], mcopy[:, u, 1, :], ALU.mult).then_inc(mask_ok, 1)
        pool.wait_ge(mask_ok, QT)

    at_z = at_w0 + 20480
    moe_at = {"at": at_w0}

    def mb(name, shape, dt=F32, at=None):
        n = 4 * int(np.prod(shape[1:]))
        if at is None:
            at = moe_at["at"]
            moe_at["at"] = (at + n + 31) // 32 * 32
        return sb(name, shape, dt, at=at)

    rc = mb("route", [P, EXPERTS + 2 * P + MT])
    st32 = mb("stats32", [P, TILES, 6])
    mv32 = mb("mv32", [P, TILES, 2])
    mvz = mb("mvz", [P, TILES, 2])
    nwt32 = mb("nwt32", [P, 3, TILES])
    nwi32 = mb("nwi32", [P, TILES], I32)
    at_zT = moe_at["at"]
    zT = mb("zT", [P, 2, KC, BANK])
    te_ge = mb("te_ge", [P, MT, EXPERTS], at=at_zT)
    te_f = mb("te_f", [P, MT], at=at_zT + 2304)
    acc_a = mb("acc_a", [P, TILES, EXPERTS], at=at_zT + 2304 + 512)
    acc_b = mb("acc_b", [P, TILES, EXPERTS], at=at_zT + 2304 + 512 + 1024)
    lg = mb("lg", [P, TILES, EXPERTS])
    pr = mb("pr", [P, TILES, EXPERTS])
    oh = mb("oh", [P, 2, TILES, EXPERTS])
    tot = mb("tot", [P, TILES, EXPERTS])
    m1 = mb("m1", [P, TILES])
    rsm = mb("rsm", [P, TILES])
    topp = mb("topp", [P, 2, TILES])
    posf = mb("posf", [P, 2, TILES])
    cnt = mb("cnt", [P, 4, EXPERTS])
    cnt_i = mb("cnt_i", [P, EXPERTS], I32)
    gate = mb("gate", [P, 2, TILES])
    pos = mb("pos", [P, TILES, 2], I32)
    te = mb("te", [P, MT], I32)
    assert moe_at["at"] <= at_z
    zall = sb("zall", [P, TILES, C], F32, at=at_z)
    at_w13 = at_z + 32768
    W13 = sb("W13", [P, EXPERTS, KC, 2 * FF], F32, at=at_w13)
    at_w2 = at_w13 + EXPERTS * KC * 2 * FF * 4
    W2 = sb("W2", [P, EXPERTS, FCH, C], F32, at=at_w2)
    zs2 = sb("zs2", [P, 2, 4, C], F32, at=at_w13 + 6 * KC * 2 * FF * 4)
    t2b = sb("t2b", [P, TILES, C], F32, at=at_w2 + 2 * FCH * C * 4)
    assert at_w2 + EXPERTS * FCH * C * 4 <= nc.sbuf_usable_end
    G1 = TILES // 4
    xs_zero = sem("xs_zero")
    rc_in = sem("rc_in")
    y_in = [sem(f"y_in{q}") for q in range(CHUNKS)]
    x2_in = [sem(f"x2_in{q}") for q in range(CHUNKS)]
    t2_ok = sem("t2_ok")
    t2_stored = sem("t2_stored")
    w13_in = sem("w13_in")
    w2_in = sem("w2_in")
    x2b_ok = sem("x2b_ok")
    z_ok = sem("z_ok")
    z_turn = sem("z_turn")
    z_act = sem("z_act")
    z_copy = sem("z_copy")
    z_dve = sem("z_dve")
    lg_ps = sem("lg_ps")
    lg_ok = sem("lg_ok")
    lg_exp = sem("lg_exp")
    oh_ok = sem("oh_ok")
    rank_ps = sem("rank_ps")
    routed = sem("routed")

    def m1_sp(sp):
        sp.wait_ge(att1.stored, 16 * TILES + 16)
        sp.sem_inc(sp_passed, 1)
        sp.dma_start(rc[:, :], route_const).then_inc(rc_in, 16)
        ty, tx = tiles(y_d), tiles(x2_d)
        for q in range(CHUNKS):
            w = slice(q * QT, (q + 1) * QT)
            sp.dma_start(zall[:, w, :], ty[:, w, :]).then_inc(y_in[q], 16)
            sp.dma_start(t2b[:, w, :], tx[:, w, :]).then_inc(x2_in[q], 16)
        for e in range(0, EXPERTS - 2, 2):
            load_w13(sp, e)
        load_w2(sp, 0)
        sp.wait_ge(t2_ok, G1)
        sp.sem_inc(sp_passed, 1)
        sp.dma_start(tiles(t2_d), t2b[:, :, :]).then_inc(t2_stored, 16)
        sp.wait_ge(t2_stored, 16)
        sp.wait_ge(z_ok, G1)
        for e in range(2, EXPERTS, 2):
            load_w2(sp, e)
        sp.wait_ge(z_turn, 2 * G1 + 1)
        sp.wait_ge(z_copy, G1 + 2)
        load_w13(sp, EXPERTS - 2)

    def load_w13(sp, e):
        sp.dma_start(W13[:, e:e + 2, :, :].rearrange("p e k n -> p (e k) n"),
                     w13[e:e + 2].rearrange("e (k p) n -> p (e k) n", p=P)).then_inc(w13_in, 16)

    def load_w2(sp, e):
        sp.dma_start(W2[0:FCW, e:e + 2, :, :].rearrange("p e k n -> p (e k) n"),
                     w2[e:e + 2].rearrange("e (k p) n -> p (e k) n", p=FCW)).then_inc(w2_in, 16)

    def m1_pool(pool):
        bet = rowv("bet").rearrange("p (o c) -> p o c", o=1).broadcast_to([P, QT, C])
        for q in range(CHUNKS):
            pool.wait_ge(x2_in[q], 16)
            v = t2b[:, q * QT:(q + 1) * QT, :]
            nc.gpsimd.tensor_tensor(v, v, bet, ALU.add).then_inc(x2b_ok, 1)

    def m1_pe(pe):
        pe.sem_inc(z_turn, 1)

        def turn(g, u):
            pe.wait_ge(z_ok, g + 1)
            pe.wait_ge(z_act, g + 1)
            pe.wait_ge(z_dve, g + 1)
            for c in range(KC):
                for t in range(4):
                    ins = nc.tensor.transpose(ps[:, 2 * u + c, t * P:(t + 1) * P],
                                              zs2[:, u, t, c * P:(c + 1) * P], ident[:, :])
                ins.then_inc(z_turn, 1)

        def route(g, u):
            pe.wait_ge(z_act, g + 3)
            pe.wait_ge(z_dve, g + 3)
            for t in range(4):
                for k in range(KC):
                    ins = nc.tensor.matmul(ps[:, 5, bass.ds(g * 4 * EXPERTS + t * EXPERTS, EXPERTS)],
                                           zT[:, u, k, t * P:(t + 1) * P], wr[:, k, :],
                                           start=(k == 0), stop=(k == KC - 1))
            ins.then_inc(lg_ps, 1)

        turn(0, 0)
        with pe.Fori(0, G1 // 2 - 1) as i:
            for u in range(2):
                turn(i * 2 + (u + 1), 1 - u)
                route(i * 2 + u, u)
        turn(G1 - 1, 1)
        for u in range(2):
            route(G1 - 2 + u, u)
        pe.wait_ge(oh_ok, 1)
        chosen = pr[:, :, :].rearrange("p t e -> p (t e)")
        nc.tensor.matmul(ps[:, 4, 0:TILES * EXPERTS], rc[:, EXPERTS:EXPERTS + P], chosen, start=True, stop=True)
        nc.tensor.matmul(ps[:, 4, TILES * EXPERTS:2 * TILES * EXPERTS], rc[:, EXPERTS + P:EXPERTS + 2 * P], chosen,
                         start=True, stop=True).then_inc(rank_ps, 1)

    def m1_act(act):
        act.sem_inc(z_act, 2)
        act.sem_inc(z_copy, 2)
        with act.Fori(0, G1 // 2) as i:
            for u in range(2):
                act.wait_ge(z_ok, i * 2 + (u + 1))
                nc.scalar.activation(zall[:, bass.ds(i * 8 + u * 4, 4), :], zs2[:, u, :, :], ACT.Copy)\
                  .then_inc(z_copy, 1)
                act.wait_ge(z_turn, i * 4 + (2 * u + 1) + 1)
                nc.scalar.activation(zT[:, u, 0, :], ps[:, 2 * u, :], ACT.Copy).then_inc(z_act, 1)
        act.wait_ge(lg_ok, 1)
        nc.scalar.activation(pr[:, :, :], lg[:, :, :], ACT.Exp).then_inc(lg_exp, 1)

    def over(ap, n):
        return ap.rearrange("p (a o) -> p a o", o=1).broadcast_to([P, ap.shape[1], n])

    def m1_dve(dve):
        dve.sem_inc(z_dve, 2)
        gam = rowv("gam")

        def tile_of(buf, g):
            return [buf[:, bass.ds(g * 4 + t, 1), :].rearrange("p o c -> p (o c)") for t in range(4)]

        relink()
        for q in range(CHUNKS):
            dve.wait_ge(y_in[q], 16)
            for t in range(q * QT, (q + 1) * QT):
                ins = nc.vector.bn_stats(st32[:, t, :], zall[:, t, :])
            link(ins)
            for t in range(q * QT, (q + 1) * QT):
                ins = nc.vector.bn_aggr(mv32[:, t, :], st32[:, t, :])
            link(ins)
        rsqrt(TILES, mv32, nwt32, nwi32)
        with dve.Fori(0, CHUNKS) as i:
          for u in range(2):
            g = i * 2 + u
            relink()
            dve.wait_ge(x2b_ok, i + 1)
            zs, ts = tile_of(zall, g), tile_of(t2b, g)
            for t in range(4):
                ins = nc.vector.scalar_tensor_tensor(zs[t], zs[t], mv32[:, bass.ds(g * 4 + t, 1), 0], gam,
                                                     ALU.subtract, ALU.mult)
            link(ins)
            for t in range(4):
                ins = nc.vector.scalar_tensor_tensor(ts[t], zs[t], nwt32[:, 1, bass.ds(g * 4 + t, 1)], ts[t],
                                                     ALU.mult, ALU.add)
            ins.then_inc(t2_ok, 1)
            dve.wait_ge(t2_ok, g + 1)
            dve.sem_inc(dve_passed, 1)
            for t in range(4):
                ins = nc.vector.bn_stats(st32[:, t, :], ts[t])
            link(ins)
            for t in range(4):
                ins = nc.vector.bn_aggr(mv[:, t, :], st32[:, t, :])
            link(ins)
            link(nc.vector.tensor_copy(mvz[:, bass.ds(g * 4, 4), :], mv[:, 0:4, :]))
        relink()
        rsqrt(TILES, mvz, nwt32, nwi32)

        def normal(g, u, again):
            ts = tile_of(t2b, g)
            if again:
                dve.wait_ge(z_turn, g * 2 - 1)
                dve.wait_ge(z_copy, g + 1)
            for t in range(4):
                ins = nc.vector.tensor_scalar(zs2[:, u, t, :], ts[t], mvz[:, bass.ds(g * 4 + t, 1), 0],
                                              nwt32[:, 1, bass.ds(g * 4 + t, 1)], ALU.subtract, ALU.mult)
            ins.then_inc(z_ok, 1)

        def bring(g, u):
            dve.wait_ge(z_turn, g * 2 + 3)
            nc.vector.tensor_copy(zT[:, u, 1, :], ps[:, 2 * u + 1, :]).then_inc(z_dve, 1)

        for u in range(2):
            normal(u, u, False)
        with dve.Fori(0, G1 // 2 - 1) as i:
            for u in range(2):
                bring(i * 2 + u, u)
                normal(i * 2 + (u + 2), u, True)
        for u in range(2):
            bring(G1 - 2 + u, u)
        relink()
        dve.wait_ge(lg_ps, G1)
        dve.wait_ge(rc_in, 16)
        nop = EXPERTS
        flat = ps[:, 5, 0:TILES * EXPERTS].rearrange("p (t e) -> p t e", e=EXPERTS)
        link(nc.vector.tensor_reduce(m1[:, :], flat, AX.X, ALU.max))
        nc.vector.tensor_tensor(lg[:, :, :], flat, over(m1[:, :], nop), ALU.subtract).then_inc(lg_ok, 1)
        dve.wait_ge(lg_exp, 1)
        link(nc.vector.tensor_reduce(rsm[:, :], pr[:, :, :], AX.X, ALU.add))
        link(nc.vector.reciprocal(rsm[:, :], rsm[:, :]))
        link(nc.vector.tensor_tensor(pr[:, :, :], pr[:, :, :], over(rsm[:, :], nop), ALU.mult))
        ids = rc[:, 0:EXPERTS].rearrange("p (o e) -> p o e", o=1).broadcast_to([P, TILES, EXPERTS])
        for k in range(2):
            link(nc.vector.tensor_reduce(topp[:, k, :], pr[:, :, :], AX.X, ALU.max))
            link(nc.vector.tensor_tensor(oh[:, k, :, :], pr[:, :, :], over(topp[:, k, :], nop), ALU.is_equal))
            link(nc.vector.tensor_tensor(oh[:, k, :, :], oh[:, k, :, :], ids, ALU.mult))
            link(nc.vector.tensor_reduce(m1[:, :], oh[:, k, :, :], AX.X, ALU.min))
            link(nc.vector.tensor_tensor(oh[:, k, :, :], ids, over(m1[:, :], nop), ALU.is_equal))
            if k == 0:
                link(nc.vector.scalar_tensor_tensor(pr[:, :, :], oh[:, 0, :, :], -2.0, pr[:, :, :], ALU.mult, ALU.add))
        nc.vector.tensor_tensor(pr[:, :, :], oh[:, 0, :, :], oh[:, 1, :, :], ALU.add).then_inc(oh_ok, 1)
        link(nc.vector.tensor_tensor(rsm[:, :], topp[:, 0, :], topp[:, 1, :], ALU.add))
        link(nc.vector.tensor_scalar(rsm[:, :], rsm[:, :], 1e-9, None, ALU.add))
        link(nc.vector.reciprocal(rsm[:, :], rsm[:, :]))
        for k in range(2):
            link(nc.vector.tensor_tensor(gate[:, k, :], topp[:, k, :], rsm[:, :], ALU.mult))
        dve.wait_ge(rank_ps, 1)
        totals = ps[:, 4, TILES * EXPERTS:2 * TILES * EXPERTS].rearrange("p (t e) -> p t e", e=EXPERTS)
        link(nc.vector.tensor_copy(tot[:, :, :], totals))
        src, a, b = tot, acc_a, acc_b
        d = 1
        while d < TILES:
            nc.vector.tensor_copy(a[:, 0:d, :], src[:, 0:d, :])
            link(nc.vector.tensor_tensor(a[:, d:, :], src[:, d:, :], src[:, 0:TILES - d, :], ALU.add))
            src, a, b = a, b, a
            d *= 2
        inc = src
        link(nc.vector.tensor_scalar(cnt_i[:, :], inc[:, TILES - 1, :], float(P - 1), None, ALU.add))
        link(nc.vector.tensor_scalar(cnt_i[:, :], cnt_i[:, :], 7, None, ALU.logical_shift_right))
        link(nc.vector.tensor_copy(cnt[:, 0, :], cnt_i[:, :]))
        s, d = 0, 1
        while d < EXPERTS:
            nc.vector.tensor_copy(cnt[:, s + 1, 0:d], cnt[:, s, 0:d])
            link(nc.vector.tensor_tensor(cnt[:, s + 1, d:], cnt[:, s, d:], cnt[:, s, 0:EXPERTS - d], ALU.add))
            s += 1
            d *= 2
        ends = cnt[:, s, :]
        nums = rc[:, EXPERTS + 2 * P:].rearrange("p (j o) -> p j o", o=1).broadcast_to([P, MT, EXPERTS])
        link(nc.vector.tensor_tensor(te_ge[:, :, :], nums,
                                     ends.rearrange("p (o e) -> p o e", o=1).broadcast_to([P, MT, EXPERTS]), ALU.is_ge))
        link(nc.vector.tensor_reduce(te_f[:, :], te_ge[:, :, :], AX.X, ALU.add))
        link(nc.vector.tensor_scalar(te[:, :], te_f[:, :], float(EXPERTS - 1), None, ALU.min))
        link(nc.vector.tensor_tensor(cnt[:, 1, :], ends, cnt[:, 0, :], ALU.subtract))
        link(nc.vector.tensor_scalar(cnt[:, 1, :], cnt[:, 1, :], float(P), None, ALU.mult))
        link(nc.vector.tensor_tensor(inc[:, :, :], inc[:, :, :], tot[:, :, :], ALU.subtract))
        link(nc.vector.tensor_tensor(inc[:, :, :], inc[:, :, :], ps[:, 4, 0:TILES * EXPERTS].rearrange("p (t e) -> p t e", e=EXPERTS), ALU.add))
        link(nc.vector.tensor_tensor(inc[:, :, :], inc[:, :, :], cnt[:, 1, :].rearrange("p (o e) -> p o e", o=1).broadcast_to([P, TILES, EXPERTS]), ALU.add))
        for k in range(2):
            link(nc.vector.tensor_tensor(oh[:, k, :, :], oh[:, k, :, :], inc[:, :, :], ALU.mult))
            link(nc.vector.tensor_reduce(posf[:, k, :], oh[:, k, :, :], AX.X, ALU.add))
            ins = nc.vector.tensor_copy(pos[:, :, k], posf[:, k, :])
            link(ins)
        nc.vector.memset(st32[:, 0, :], 0.0).then_inc(routed, 1)

    at_s = at_z
    xs = sb("xs", [P, 2, C], F32, at=at_s)
    xsT = sb("xsT", [P, 2, KC, P], F32, at=at_s + 2048)
    sil = sb("sil", [P, 2, HALF + 3], F32, at=at_s + 4096)
    hm = sb("hm", [P, 2, FF + 6], F32, at=at_s + 4096 + 2752)
    hmT = sb("hmT", [P, 2, FCH, P], F32, at=at_s + 6848 + 5504)
    yo = sb("yo", [P, 2, C], F32, at=at_s + 12352 + 6144)
    ya = sb("ya", [P, 2, 4, 2, C], F32, at=at_w13)
    tc = sb("tc", [P, 2, 4, C], F32, at=at_w13 + 16384)
    oc = sb("oc", [P, 2, 4, C], F32, at=at_w13 + 24576)

    sent = sem("sent")
    xs_in = [sem("xs_in_a"), sem("xs_in_b")]
    xs_turn = sem("xs_turn")
    xs_out = sem("xs_out")
    h_ps = sem("h_ps")
    silu_ok = sem("silu_ok")
    hm_ok = sem("hm_ok")
    hm_turn = sem("hm_turn")
    hmT_act = sem("hmT_act")
    hmT_dve = sem("hmT_dve")
    y_ps = sem("y_ps")
    y_out = sem("y_out")
    y_stored = [sem("y_stored_a"), sem("y_stored_b")]

    def dispatch_pool(pool):
        pool.wait_ge(xs_zero, 16 * GROUPS)
        pool.wait_ge(routed, 1)
        pool.wait_ge(z_copy, G1 + 2)
        for t in range(TILES):
            for k in range(2):
                pool.indirect_dma_start(xs_d, bass.IndirectOffsetOnAxis(pos[:, t, k:k + 1], 0), zall[:, t, :], None,
                                        bounds_check=MT * P - 1, oob_is_err=False).then_inc(sent, 16)

    def moe_loop(eng, step):
        for u in range(2):
            step(u, 0, u, u == 0, False)
        with eng.Fori(1, MT // 2 - 1) as i:
            for u in range(2):
                step(i * 2 + u, i, u, False, False)
        for u in range(2):
            step(MT - 2 + u, MT // 2 - 1, u, False, u == 1)

    def moe_sp(sp):
        for c in y_stored:
            sp.sem_inc(c, 16)
        xt, yt = tiles(xs_d), tiles(y2_d)
        sp.wait_ge(sent, 16 * SLOTS // P)

        def load(j, u):
            sp.dma_start(xs[:, u, :].rearrange("p (o c) -> p o c", o=1), xt[:, bass.ds(j, 1), :]).then_inc(xs_in[u], 16)

        def store(j, u):
            sp.wait_ge(y_out, j + 2)
            sp.sem_inc(sp_passed, 1)
            sp.dma_start(yt[:, bass.ds(j, 1), :], yo[:, u, :].rearrange("p (o c) -> p o c", o=1)).then_inc(y_stored[u], 16)

        def step(j, i, u, first, last):
            if not last:
                sp.wait_ge(xs_turn, j + 2)
                sp.sem_inc(sp_passed, 1)
                load(j + 1, 1 - u)
            if not first:
                store(j - 1, 1 - u)

        load(0, 0)
        moe_loop(sp, step)
        store(MT - 1, (MT - 1) % 2)

    def moe_pe(pe):
        pe.sem_inc(xs_turn, 2)
        pe.sem_inc(y_ps, 1)

        def turn_x(j, i, u):
            pe.wait_ge(xs_in[u], i * 16 + 16)
            if not isinstance(j, int) or j:
                pe.wait_ge(xs_out, j)
            for k in range(KC):
                ins = nc.tensor.transpose(ps[:, 4, k * P:(k + 1) * P], xs[:, u, k * P:(k + 1) * P], ident[:, :])
            ins.then_inc(xs_turn, 1)

        def hidden(j, u, e):
            pe.wait_ge(xs_out, j + 1)
            for hf in range(2):
                pe.wait_ge(hm_ok, j * 2 + hf + 1)
                for m in range(2):
                    for k in range(KC):
                        a = m * FF + hf * HALF
                        ins = nc.tensor.matmul(ps[:, 2 * hf + m, 0:HALF], xsT[:, u, k, :],
                                               W13[:, bass.ds(e, 1), k, a:a + HALF].rearrange("p o n -> p (o n)"),
                                               start=(k == 0), stop=(k == KC - 1))
                ins.then_inc(h_ps, 1)

        def turn_h(j, u):
            pe.wait_ge(hmT_act, j + 1)
            pe.wait_ge(hmT_dve, j + 1)
            pe.wait_ge(hm_ok, j * 2 + 4)
            for c in range(FCH):
                w = min(FCW, FF - c * FCW)
                ins = nc.tensor.transpose(ps[0:w, 5 + c // 4, (c % 4) * P:(c % 4 + 1) * P],
                                          hm[:, u, c * FCW:c * FCW + w], ident[:, :])
                if c in (3, 5):
                    ins.then_inc(hm_turn, 1)

        def down(j, u, e):
            pe.wait_ge(hmT_act, j + 2)
            pe.wait_ge(hmT_dve, j + 2)
            pe.wait_ge(y_out, j + 1)
            for c in range(FCH):
                w = min(FCW, FF - c * FCW)
                ins = nc.tensor.matmul(ps[:, 7, 0:C], hmT[0:w, u, c, :],
                                       W2[0:w, bass.ds(e, 1), c, :].rearrange("p o n -> p (o n)"),
                                       start=(c == 0), stop=(c == FCH - 1))
            ins.then_inc(y_ps, 1)

        def step(j, i, u, first, last):
            e = pe.value_load(te[0:1, bass.ds(j, 1)], min_val=0, max_val=EXPERTS - 1)
            hidden(j, u, e)
            if not last:
                turn_x(j + 1, i + u, 1 - u)
            if not first:
                d = pe.value_load(te[0:1, bass.ds(j - 1, 1)], min_val=0, max_val=EXPERTS - 1)
                down(j - 1, 1 - u, d)
            turn_h(j, u)
            
        pe.wait_ge(w13_in, 16 * EXPERTS // 2)
        pe.wait_ge(routed, 1)
        turn_x(0, 0, 0)
        pe.wait_ge(w2_in, 16 * EXPERTS // 2)
        moe_loop(pe, step)
        d = pe.value_load(te[0:1, MT - 1:MT], min_val=0, max_val=EXPERTS - 1)
        down(MT - 1, (MT - 1) % 2, d)

    def moe_act(act):
        act.sem_inc(silu_ok, 2)
        act.sem_inc(hmT_act, 1)

        def bring(j, u):
            act.wait_ge(xs_turn, j + 3)
            nc.scalar.activation(xsT[:, u, :, :].rearrange("p k n -> p (k n)"), ps[:, 4, 0:C], ACT.Copy)\
              .then_inc(xs_out, 1)

        def step(j, i, u, first, last):
            for hf in range(2):
                act.wait_ge(h_ps, j * 2 + (hf + 1))
                act.wait_ge(hm_ok, j * 2 + hf + 1)
                nc.scalar.activation(sil[:, hf, 0:HALF], ps[:, 2 * hf, 0:HALF], ACT.Silu).then_inc(silu_ok, 1)
            if not last:
                bring(j + 1, 1 - u)
            act.wait_ge(hm_turn, j * 2 + 1)
            act.wait_ge(y_ps, (j - 1 if not (isinstance(j, int) and j == 0) else 0) + 1)
            nc.scalar.activation(hmT[0:FCW, u, 0:4, :].rearrange("p k n -> p (k n)"), ps[0:FCW, 5, :], ACT.Copy)\
              .then_inc(hmT_act, 1)

        bring(0, 0)
        moe_loop(act, step)

    def moe_dve(dve):
        dve.sem_inc(hm_ok, 2)
        dve.sem_inc(hmT_dve, 1)
        dve.sem_inc(y_out, 1)

        def evac(j, i, u):
            dve.wait_ge(y_ps, j + 2)
            dve.wait_ge(y_stored[u], i * 16 + 16)
            nc.vector.tensor_copy(yo[:, u, :], ps[:, 7, 0:C]).then_inc(y_out, 1)

        def step(j, i, u, first, last):
            for hf in range(2):
                dve.wait_ge(silu_ok, j * 2 + (hf + 1) + 2)
                if isinstance(j, int) and j < 2:
                    pass
                else:
                    dve.wait_ge(hm_turn, j * 2 - 2)
                nc.vector.tensor_tensor(hm[:, u, hf * HALF:(hf + 1) * HALF], sil[:, hf, 0:HALF],
                                        ps[:, 2 * hf + 1, 0:HALF], ALU.mult).then_inc(hm_ok, 1)
            if not first:
                evac(j - 1, i - 1 + u, 1 - u)
            dve.wait_ge(hm_turn, j * 2 + 2)
            dve.wait_ge(y_ps, (j - 1 if not (isinstance(j, int) and j == 0) else 0) + 1)
            w = FF - (FCH - 1) * FCW
            nc.vector.tensor_copy(hmT[0:FCW, u, 4, :], ps[0:FCW, 6, 0:P])
            nc.vector.tensor_copy(hmT[0:w, u, 5, :], ps[0:w, 6, P:2 * P]).then_inc(hmT_dve, 1)

        moe_loop(dve, step)
        evac(MT - 1, MT // 2 - 1, (MT - 1) % 2)

    back = [sem("back_a"), sem("back_b")]
    tc_in = [sem("tc_in_a"), sem("tc_in_b")]
    mixed = sem("mixed")
    out_stored = [sem("out_stored_a"), sem("out_stored_b")]

    def combine_pool(pool):
        for c in y_stored:
            pool.wait_ge(c, 16 * MT // 2 + 16)
        pool.wait_ge(y_ps, MT + 1)

        for g in range(G1):
            if g >= 2:
                pool.wait_ge(mixed, g)
            for t in range(4):
                for k in range(2):
                    pool.indirect_dma_start(ya[:, g % 2, t, k, :], None, y2_d,
                                            bass.IndirectOffsetOnAxis(pos[:, g * 4 + t, k:k + 1], 0),
                                            bounds_check=MT * P - 1, oob_is_err=False).then_inc(back[g % 2], 16)

    def combine_sp(sp):
        for c in out_stored:
            sp.sem_inc(c, 16)
        sp.wait_ge(y_ps, MT + 1)
        t2, o = tiles(t2_d), tiles(out.rearrange("b h w c -> (b h w) c"))

        def load(g, u):
            sp.dma_start(tc[:, u, :, :], t2[:, bass.ds(g * 4, 4), :]).then_inc(tc_in[u], 16)

        load(0, 0)
        load(1, 1)

        def store(g, u):
            sp.wait_ge(mixed, g + 2)
            sp.sem_inc(sp_passed, 1)
            sp.dma_start(o[:, bass.ds(g * 4, 4), :], oc[:, u, :, :]).then_inc(out_stored[u], 16)

        with sp.Fori(0, G1 // 2 - 1) as i:
            for u in range(2):
                store(i * 2 + u, u)
                load(i * 2 + (u + 2), u)
        for u in range(2):
            store(G1 - 2 + u, u)
        for c in out_stored:
            sp.wait_ge(c, 16 * G1 // 2 + 16)

    def combine_dve(dve):
        dve.sem_inc(mixed, 1)
        with dve.Fori(0, G1 // 2) as i:
            for u in range(2):
                relink()
                dve.wait_ge(tc_in[u], i * 16 + 16)
                dve.wait_ge(back[u], i * 128 + 128)
                dve.wait_ge(out_stored[u], i * 16 + 16)
                for k in range(2):
                    for t in range(4):
                        ins = nc.vector.scalar_tensor_tensor(
                            oc[:, u, t, :], ya[:, u, t, k, :], gate[:, k, bass.ds(i * 8 + u * 4 + t, 1)],
                            (tc if k == 0 else oc)[:, u, t, :], ALU.mult, ALU.add)
                    if k == 0:
                        link(ins)
                ins.then_inc(mixed, 1)

    block = ctx.enter_context(nc.Block())

    @block.sync
    def _(sp):
        prep_sp(sp)
        att0.sp(sp)
        mlp_sp(sp)
        for c in m_stored:
            sp.wait_ge(c, 16 * GROUPS // 2 + 16)
        att1.load(sp, 0)
        att1.sp(sp)
        m1_sp(sp)
        moe_sp(sp)
        combine_sp(sp)

    @block.gpsimd
    def _(pool):
        prep_pool(pool)
        bias_pool(pool)
        scatter_pool(pool)
        mask_pool(pool)
        att1.pool(pool)
        m1_pool(pool)
        dispatch_pool(pool)
        combine_pool(pool)

    @block.tensor
    def _(pe):
        pe.wait_ge(prep_p, 4)
        pe.wait_ge(prep_v, 1)
        att0.pe(pe)
        mlp_pe(pe)
        att1.pe(pe)
        m1_pe(pe)
        moe_pe(pe)

    @block.scalar
    def _(act):
        act.wait_ge(prep_v, 1)
        att0.act(act)
        mlp_act(act)
        att1.act(act)
        m1_act(act)
        moe_act(act)

    @block.vector
    def _(dve):
        prep_dve(dve)
        att0.dve(dve)
        mlp_dve(dve)
        att1.dve(dve)
        m1_dve(dve)
        moe_dve(dve)
        combine_dve(dve)


def layout(inputs):
    f = {k: np.asarray(v) for k, v in inputs.items()}
    two = lambda v: v.reshape(-1, P).T
    cols = np.concatenate([two(f["L0_conv_norm1_w"]), two(f["L0_conv_norm1_b"]), two(f["L0_conv_norm2_w"]),
                           two(f["L0_conv_norm2_b"]), two(f["L0_conv_qkv_b"][0:C]), two(f["L0_conv_qkv_b"][C:2 * C]),
                           two(f["L0_conv_fc1_b"]), two(f["L1_attn_bq"]), two(f["L1_attn_bk"])], axis=1)
    rows = np.stack([f["L0_conv_qkv_b"][2 * C:], f["L0_conv_proj_b"], f["L0_conv_gamma_1"][4], f["L0_conv_fc2_b"],
                     f["L0_conv_gamma_2"][4], f["L1_attn_bv"], f["L1_attn_bo"], f["L1_attn_gamma"], f["L1_attn_beta"]])
    rpb = np.pad(f["L0_conv_rpb"].transpose(1, 0, 2), ((0, 0), (0, 0), (SIDE, SIDE - 1)))
    toeplitz = np.stack([rpb[:, :, 38 - j:70 - j] for j in range(SIDE)]).reshape(SIDE, -1)
    shut = np.full((3, ROWS, SIDE, WT * ROWS, SIDE), BIG, np.float32)
    for kind, (row0, key0) in enumerate(((0, 0), (2 * ROWS, ROWS), (SIDE - ROWS, SIDE - WT * ROWS))):
        for i in range(ROWS):
            for j in range(SIDE):
                a = min(max(row0 + i - KWIN // 2, 0), SIDE - KWIN) - key0
                b = min(max(j - KWIN // 2, 0), SIDE - KWIN)
                shut[kind, i, j, a:a + KWIN, b:b + KWIN] = 0.0
    shut = shut.reshape(3, P, WK).transpose(1, 0, 2)
    w13 = np.concatenate([f["L1_ffn_w1"], f["L1_ffn_w3"]], axis=1).transpose(0, 2, 1)
    route_const = np.zeros((P, EXPERTS + 2 * P + MT), np.float32)
    route_const[:, 0:EXPERTS] = np.arange(EXPERTS) - EXPERTS
    route_const[:, EXPERTS:EXPERTS + P] = np.triu(np.ones((P, P)), 1)
    route_const[:, EXPERTS + P:EXPERTS + 2 * P] = 1.0
    route_const[:, EXPERTS + 2 * P:] = np.arange(MT)
    return {
        "x": f["x"].reshape(TOK, C), "rpb_toeplitz": toeplitz, "window_mask": shut, "cols": cols, "rows": rows,
        "w_qkv0": f["L0_conv_qkv_w"].T, "w_proj0": f["L0_conv_proj_w"].T, "w_fc1": f["L0_conv_fc1_w"].T,
        "w_fc2": f["L0_conv_fc2_w"].T,
        "w_qkv1": np.concatenate([f["L1_attn_Wq"], f["L1_attn_Wk"], f["L1_attn_Wv"]], axis=1),
        "w_o1": f["L1_attn_Wo"], "w_router": f["L1_ffn_router_w"].T, "edges": f["L1_attn_edge_index"],
        "w13": w13, "w2": np.pad(f["L1_ffn_w2"].transpose(0, 2, 1), ((0, 0), (0, FCH * FCW - FF), (0, 0))),
        "route_const": route_const,
    }


def kernel(**inputs):
    import concourse.bacc as bacc
    from concourse.bass_utils import run_bass_kernel_spmd

    arrays = {name: np.ascontiguousarray(a) for name, a in layout(inputs).items()}
    nc = bacc.Bacc("TRN2", target_bir_lowering=False, num_devices=1)
    args = [nc.dram_tensor(f"in_{name}_dram", a.shape, mybir.dt.from_np(a.dtype), kind="ExternalInput").ap()
            for name, a in arrays.items()]
    out = nc.dram_tensor("out_0_dram", (BATCH, SIDE, SIDE, C), F32, kind="ExternalOutput").ap()
    build_program(nc, *args, out)
    if not nc.is_finalized():
        nc.finalize()
    r = run_bass_kernel_spmd(nc, [{f"in_{name}_dram": a for name, a in arrays.items()}], core_ids=[0])
    return r.results[0]["out_0_dram"]
```

```python
from contextlib import ExitStack

import numpy as np

import concourse.bass as bass
from concourse import mybir

F32 = mybir.dt.float32
F32R = mybir.dt.float32r
BF16 = mybir.dt.bfloat16
I32 = mybir.dt.int32
ACT = mybir.ActivationFunctionType
ALU = mybir.AluOpType
AX = mybir.AxisListType

P = 128
BATCH, SIDE, C, HEADS, HD = 4, 32, 256, 8, 32
N = SIDE * SIDE
TOK = BATCH * N
KC = C // P
QT = N // P
TILES = TOK // P
HID = 4 * C
HCH = HID // P
KWIN = 7
ROWS = P // SIDE
WT = 3
WK = WT * P
EXPERTS = 8
FF = 682
FCH = 6
FCW = -(-FF // FCH)
HALF = -(-FF // 4) * 2
HALVES = (HALF, FF - HALF)
SLOTS = 2 * TOK
BLOCK = 2 * P
BLOCKS = (SLOTS + EXPERTS * (BLOCK - 1)) // BLOCK
MT = BLOCKS * BLOCK // P
XT = -(-MT // (TILES // 4)) * (TILES // 4)
CHUNKS = BATCH
EDGES = 69632
ECOL = EDGES // P
COPIES = 4
EBATCH = 16
CELLS = N * N
BIG = 3.0e38
NO_EDGE = 2.0 ** 31
SCALE = float(HD) ** -0.5
BANK = 512
PARTS = 3
STAGE = 16 * PARTS * 4
assert ECOL % EBATCH == 0 and FCH * FCW >= FF


def build_program(nc, x, rpb_toeplitz, window_mask, cols, rows, w_qkv0, w_proj0, w_fc1, w_fc2,
                  w_qkv1, w_o1, w_router, edges, w13, w2, route_const, out):
    ctx = ExitStack()
    base = (nc.sbuf_base + 63) // 64 * 64
    place = {"at": base}

    def sb(name, shape, dt, at=None):
        size = 4 if dt in (F32, F32R, I32) else 2
        n = int(np.prod(shape[1:])) * size
        if at is None:
            at = place["at"]
            place["at"] = (at + n + 31) // 32 * 32
        return nc.alloc_sbuf_tensor_at(name, list(shape), dt, offset=at)

    def dram(name, shape, dt):
        return nc.dram_tensor(name, list(shape), dt, kind="Internal").ap()

    def sem(name):
        return ctx.enter_context(nc.semaphore(name))


    ident = sb("ident", [P, P], F32)
    zeros = sb("zeros", [P, C], F32)
    col = sb("col", [P, cols.shape[1]], F32)
    at_row = place["at"]
    row = sb("row", [P, rows.shape[0] * C], F32)
    edge_at = sb("edge_at", [P, ECOL], I32)
    row_end = place["at"]
    edge_slot = sb("edge_slot", [P, EBATCH], I32)
    stats = sb("stats", [P, QT, 6], F32)
    mv = sb("mv", [P, QT, 2], F32)
    nwt = sb("nwt", [P, 3, QT], F32)
    nwi = sb("nwi", [P, QT], I32)
    nmax = sb("nmax", [P, 4], F32)
    rsum = sb("rsum", [P, 2, HEADS], F32)
    rinv = sb("rinv", [P, 4], F32)
    rexp = sb("rexp", [P, 2, P], F32)
    rT = sb("rT", [P, 2, P], F32)
    oTn = sb("oTn", [P, 2, KC, P], F32)
    wo1 = sb("wo1", [P, KC, C], F32)
    wr = sb("wr", [P, KC, EXPERTS], F32)
    at_w0 = place["at"]
    wq0 = sb("wq0", [P, KC, 3 * C], F32)
    wp0 = sb("wp0", [P, KC, C], F32)
    at_wf1 = place["at"]
    wf1 = sb("wf1", [P, KC, HID], F32)
    wf2 = sb("wf2", [P, HCH, C], F32)
    wq1 = sb("wq1", [P, KC, 3 * C], F32, at=at_w0)
    at_bias = place["at"]
    bias = sb("bias", [P, 3, HEADS, WK], F32)
    mask = sb("mask", [P, QT, N], BF16, at=at_bias)
    mask_tile = sb("mask_tile", [P, 2, N], BF16, at=at_bias + 2 * QT * N)
    at_att = place["at"]
    pT = sb("pT", [P, HEADS, N], F32)
    pT0 = sb("pT0", [P, HEADS, WK], F32, at=at_att)
    xhs = [sb("xh0", [P, QT, C], F32, at=at_att + 24576), sb("xh1", [P, QT, C], F32, at=at_bias + 2 * QT * N + 4 * N)]
    hT = sb("hT", [P, KC, N], F32, at=at_att + 8192)
    k_hi = sb("k_hi", [P, KC, N], F32R, at=at_att + 16384)
    k_lo = sb("k_lo", [P, KC, N], F32R, at=at_att + 24576)
    at_k = place["at"]
    kst = sb("kst", [P, HEADS, N], F32R)
    toep = sb("toep", [P, 20, HEADS, SIDE], F32, at=at_k)
    qst = sb("qst", [P, 2, HEADS, P], F32R)
    q_pair = [sb("q_pair_a", [P, HEADS, 2 * P], F32R, at=place["at"] - 8192),
              sb("q_pair_b", [P, HEADS, 2 * P], F32R, at=at_att + 16384)]
    at_q = place["at"]
    q_hi = sb("q_hi", [P, KC, N], F32R)
    q_lo = sb("q_lo", [P, KC, N], F32R)
    vt = sb("vt", [P, QT, C], F32)
    at_m = place["at"]
    msc = sb("msc", [P, 2, N], F32)
    prob = sb("prob", [P, 2, N], F32)
    msc0 = sb("msc0", [P, 4, WK], F32, at=at_m)
    prob0 = sb("prob0", [P, 4, WK], F32, at=at_m + 4 * WK * 4)
    big = sb("big", [P, 2048], BF16, at=at_m - 8192)
    e_src = sb("e_src", [P, ECOL], I32, at=at_att + 4608)
    e_dst = sb("e_dst", [P, ECOL], I32, at=at_att + 6784)
    e_tmp = sb("e_tmp", [P, ECOL], F32, at=at_att + 8960)
    wmask = sb("wmask", [P, 3, WK], F32, at=at_att)
    mcopy = sb("mcopy", [P, 2, COPIES, N], BF16, at=at_m)
    at_xb = place["at"]
    xb = sb("xb", [P, QT, C], F32)
    res = sb("res", [P, QT, C], F32)
    assert place["at"] <= nc.sbuf_usable_end

    ps = nc.alloc_psum_tensor("ps", [P, 8, BANK], F32)

    x1_d = dram("x1_d", [TOK, C], F32)
    x2_d = dram("x2_d", [TOK, C], F32)
    y_d = dram("y_d", [TOK, C], F32)
    mask_d = dram("mask_d", [COPIES * CELLS, 1], BF16)
    t2_d = dram("t2_d", [TOK, C], F32)
    xs_d = dram("xs_d", [XT * P, C], F32)
    y2_d = dram("y2_d", [MT * P, C], F32)

    def tiles(ap):
        return ap.rearrange("(n p) c -> p n c", p=P)

    NCOL = ["n1w", "n1b", "n2w", "n2b", "qb0", "kb0", "fb", "qb1", "kb1"]
    cw = {"fb": HCH}
    cat, at_c = {}, 0
    for nme in NCOL:
        cat[nme] = at_c
        at_c += cw.get(nme, KC)
    NROW = ["vb0", "pb0", "g1", "f2b", "g2", "vb1", "ob1", "gam", "bet"]
    rat = {nme: i for i, nme in enumerate(NROW)}

    def rowv(nme):
        return row[:, rat[nme] * C:(rat[nme] + 1) * C]

    def colv(nme, i):
        return col[:, cat[nme] + i:cat[nme] + i + 1]

    ld = sem("ld")
    ld_b = sem("ld_b")
    edge_ld = sem("edge_ld")
    prep_v = sem("prep_v")
    prep_p = sem("prep_p")
    chain = sem("chain")
    edge_ready = sem("edge_ready")
    big_ready = sem("big_ready")
    mask_init = sem("mask_init")
    slot_copy = sem("slot_copy")
    scat = [sem(f"scat{k}") for k in range(COPIES)]
    mask_in = [sem(f"mask_in{k}") for k in range(2)]
    mask_half = sem("mask_half")
    mask_ok = sem("mask_ok")
    ld_f = sem("ld_f")
    wf_ok = sem("wf_ok")
    bias_ok = sem("bias_ok")
    sp_passed, pool_passed, dve_passed = sem("sp_passed"), sem("pool_passed"), sem("dve_passed")
    links = [0]

    def link(ins):
        links[0] += 1
        ins.then_inc(chain, 1)
        nc.vector.wait_ge(chain, links[0])

    def relink():
        nc.vector.sem_clear(chain)
        links[0] = 0

    def rsqrt(n, mv=mv, nwt=nwt, nwi=nwi, parts=(0, 1, 2)):
        v, y, t = nwt[:, 0, 0:n], nwt[:, 1, 0:n], nwt[:, 2, 0:n]
        g = nwi[:, 0:n].bitcast(F32)
        if 0 in parts:
            link(nc.vector.tensor_scalar(v, mv[:, 0:n, 1], 1e-5, None, ALU.add))
            link(nc.vector.tensor_scalar(nwi[:, 0:n], v.bitcast(I32), 1, None, ALU.logical_shift_right))
            link(nc.vector.tensor_scalar(nwi[:, 0:n], nwi[:, 0:n], -1.0, float(0x5F3759DF), ALU.mult, ALU.add))
        for k in parts:
            g = g if k == 0 else y
            link(nc.vector.tensor_tensor(t, g, g, ALU.mult))
            link(nc.vector.tensor_tensor(t, t, v, ALU.mult))
            link(nc.vector.tensor_scalar(t, t, -0.5, 1.5, ALU.mult, ALU.add))
            link(nc.vector.tensor_tensor(y, g, t, ALU.mult))

    class Attention:

        NORM_STEPS = 5 + QT

        def __init__(self, n, src, dst, wqkv, wout, kw, local):
            self.n, self.src, self.dst, self.wqkv, self.wout = n, src, dst, wqkv, wout
            self.kw, self.local = kw, local
            self.nb = (kw + BANK - 1) // BANK
            self.kc = kw // P
            self.xh = xhs[n]
            self.depth, self.lag = (4, 0) if local else (2, 0)
            self.over = 10
            self.msc, self.prob = (msc0, prob0) if local else (msc, prob)
            self.pT = pT0 if local else pT
            c = lambda s: sem(f"{s}{n}")
            self.x_in = c("x_in")
            self.x_norm = c("x_norm")
            self.hT_ps = c("hT_ps")
            self.hT_act = c("hT_act")
            self.hT_dve = c("hT_dve")
            self.res_ok = c("res_ok")
            self.proj_ps = c("proj_ps")
            self.proj_hi = c("proj_hi")
            self.proj_out = c("proj_out")
            self.k_staged = c("k_staged")
            self.q_staged = [c("q_staged_a"), c("q_staged_b")]
            self.qk = c("qk")
            self.masked = c("masked")
            self.exp = c("exp")
            self.p_ps = c("p_ps")
            self.p_act = c("p_act")
            self.p_dve = c("p_dve")
            self.r_exp = c("r_exp")
            self.pv = c("pv")
            self.r_act = c("r_act")
            self.o_norm = c("o_norm")
            self.wo_ps = c("wo_ps")
            self.wo_out = c("wo_out")
            self.stored = c("stored")
            self.mask_set = c("mask_set")

        def steps(self, g, s):
            return g * 16 + s

        def set_tile(self, tp):
            self.tp_of = tp

        def freed(self, g, s):
            back = s + 1 - self.depth
            return g * 16 + (back if back >= 0 or self.prev else 0)

        def later(self, g, s, prev, rest, of=lambda pair: None):
            r = s - self.lag
            if prev and r < self.over:
                of(-1)
                rest(g - 1, r + 16)
            of(0)
            if r >= 0:
                rest(g, r)

        def chunk(self, g, s, j):
            m = self.nb * s + j
            return m % 2, g * (8 * self.nb) + m // 2

        def key_tile(self, tp, u):
            return min(max(2 * tp + u - 1, 0), QT - WT) if self.local else 0

        def kind(self, tp, u):
            return {0: 0, QT - 1: 2}.get(2 * tp + u, 1)

        def loop(self, eng, b, prelude, pair, tail):
            prelude(b)
            pair(b * 4, 0, False)
            if self.local:
                for tp in range(1, QT // 2):
                    pair(b * 4 + tp, tp, True)
            else:
                with eng.Fori(1, QT // 2) as tp:
                    pair(b * 4 + tp, tp, True)
            tail(b * 4 + 4)

        def load(self, sp, b):
            sp.dma_start(xb[:, :, :], tiles(self.src)[:, bass.ds(b * QT, QT), :]).then_inc(self.x_in, 16)

        def sp(self, sp, between=lambda: None):
            sp.sem_inc(self.stored, 16)
            dst = tiles(self.dst)

            def stage_k(b):
                if self.local:
                    sp.wait_ge(bias_ok, 3)
                sp.wait_ge(self.proj_out, b * 12 + 4)
                sp.sem_inc(sp_passed, 1)
                sp.wait_ge(self.qk, b * 64 + 1)
                sp.sem_inc(sp_passed, 1)
                for r, half in enumerate((k_hi, k_hi, k_lo)):
                    for j in range(4):
                        sp.dma_start(kst[32 * r:32 * r + 32, :, :].rearrange("p (c j) n -> p c j n", j=4)[:, :, j, :]
                                     .bitcast(F32), half[32 * j:32 * j + 32, :, :].bitcast(F32)).then_inc(self.k_staged, 16)

            def stage(g, tp, u):
                sp.wait_ge(self.qk, (g * 16 + 8 * (u - 1) if u else g * 16 - 8 if not isinstance(tp, int) or tp else g * 16) + 1)
                sp.sem_inc(sp_passed, 1)
                t = tp * 2 + u
                for r, half in enumerate((q_hi, q_lo, q_hi)):
                    for j in range(4):
                        sp.dma_start(
                            qst[32 * r:32 * r + 32, u, :, :].rearrange("p (c j) n -> p c j n", j=4)[:, :, j, :]
                            .bitcast(F32), half[32 * j:32 * j + 32, :, bass.ds(t * P, P)].bitcast(F32)).then_inc(self.q_staged[u], 16)

            def stage_pair(g, tp):
                for r, half in enumerate((q_hi, q_lo, q_hi)):
                    for j in range(4):
                        sp.dma_start(
                            q_pair[tp % 2][32 * r:32 * r + 32, :, :].rearrange("p (c j) n -> p c j n", j=4)[:, :, j, :]
                            .bitcast(F32), half[32 * j:32 * j + 32, :, tp * 2 * P:(tp + 1) * 2 * P].bitcast(F32))\
                          .then_inc(self.q_staged[tp % 2], 16)

            def store(g, tp, u):
                sp.wait_ge(self.wo_out, g * 2 + (u + 1) + 1)
                sp.sem_inc(sp_passed, 1)
                sp.dma_start(dst[:, bass.ds(g * 2 + u, 1), :], res[:, bass.ds(tp * 2 + u, 1), :])\
                  .then_inc(self.stored, 16)

            def batch(b, more):
                stage_k(b)
                sp.wait_ge(self.proj_out, b * 12 + 8)
                sp.sem_inc(sp_passed, 1)
                if self.local:
                    stage_pair(b * 4, 0)
                    sp.wait_ge(self.k_staged, b * STAGE + STAGE)
                    sp.sem_inc(sp_passed, 1)
                    stage_pair(b * 4 + 1, 1)
                else:
                    for u in range(2):
                        stage(b * 4, 0, u)
                if more:
                    sp.wait_ge(self.res_ok, b + 2)
                    sp.sem_inc(sp_passed, 1)
                    self.load(sp, b + 1)
                if self.local:
                    for tp in range(QT // 2):
                        if tp + 2 < QT // 2:
                            sp.wait_ge(self.qk, b * 64 + (16 * tp + 17))
                            sp.sem_inc(sp_passed, 1)
                            stage_pair(b * 4 + (tp + 2), tp + 2)
                        for u in range(2):
                            store(b * 4 + tp, tp, u)
                else:
                    with sp.Fori(1, QT // 2) as tp:
                        for u in range(2):
                            stage(b * 4 + tp, tp, u)
                            store(b * 4 + tp - 1, tp - 1, u)
                    for u in range(2):
                        store(b * 4 + 3, QT // 2 - 1, u)

            with sp.Fori(0, BATCH - 1) as b:
                batch(b, True)
            between()
            batch(BATCH - 1, False)

        def pe(self, pe):
            pe.sem_inc(self.qk, 1)
            pe.sem_inc(self.p_ps, 1)
            pe.sem_inc(self.pv, 1)

            def prelude(b):
                for hf in range(2):
                    pe.wait_ge(self.x_norm, b * QT + 4 * hf + 4)
                    if hf == 1:
                        pe.wait_ge(self.wo_out, b * QT + 1)
                    for c in range(KC):
                        bank = 4 + 2 * hf + c
                        for t in range(4):
                            ins = nc.tensor.transpose(ps[:, bank, t * P:(t + 1) * P],
                                                      self.xh[:, 4 * hf + t, c * P:(c + 1) * P], ident[:, :])
                        ins.then_inc(self.hT_ps, 1)
                pe.wait_ge(self.hT_act, b * 2 + 2)
                pe.wait_ge(self.hT_dve, b * 2 + 2)
                job = 0
                for part in (1, 0):
                    for c in range(KC):
                        for hf in range(2):
                            if job >= 4:
                                pe.wait_ge(self.proj_out, b * 12 + (job - 3))
                            for k in range(KC):
                                ins = nc.tensor.matmul(ps[:, job % 4, :],
                                                       self.wqkv[:, k, part * C + c * P:part * C + (c + 1) * P],
                                                       hT[:, k, hf * BANK:(hf + 1) * BANK],
                                                       start=(k == 0), stop=(k == KC - 1))
                            ins.then_inc(self.proj_ps, 1)
                            job += 1
                for t2 in range(QT // 2):
                    pe.wait_ge(self.proj_out, b * 12 + (job - 3))
                    for u in range(2):
                        t = 2 * t2 + u
                        for k in range(KC):
                            ins = nc.tensor.matmul(ps[:, job % 4, u * C:(u + 1) * C], hT[:, k, t * P:(t + 1) * P],
                                                   self.wqkv[:, k, 2 * C:3 * C], start=(k == 0), stop=(k == KC - 1))
                    ins.then_inc(self.proj_ps, 1)
                    job += 1
                pe.wait_ge(self.proj_out, b * 12 + 12)
                pe.wait_ge(self.k_staged, b * STAGE + STAGE)

            def scores(g, tp, s):
                u, h = divmod(s, HEADS)
                if h == 0 and not self.local:
                    pe.wait_ge(self.q_staged[u], g * STAGE + STAGE)
                if s == 0 and self.local:
                    pe.wait_ge(self.q_staged[tp % 2], self.b * (2 * STAGE) + STAGE * (tp // 2 + 1))
                rows = PARTS * HD
                q = q_pair[tp % 2][0:rows, h, u * P:(u + 1) * P] if self.local else qst[0:rows, u, h, :]
                pe.wait_ge(self.masked, self.freed(g, s) + 1)
                k0 = self.key_tile(tp, u) * P
                for i in range(self.nb):
                    w = min(BANK, self.kw - i * BANK)
                    ins = nc.tensor.matmul(ps[:, (self.nb * s) % 4 + i, 0:w], q,
                                           kst[0:rows, h, k0 + i * BANK:k0 + i * BANK + w], start=True, stop=True)
                ins.then_inc(self.qk, 1)

            def turn(g, s):
                pe.wait_ge(self.exp, self.steps(g, s + 1) + 1)
                for j in range(self.nb):
                    odd, m = self.chunk(g, s, j)
                    pe.wait_ge(self.p_dve if odd else self.p_act, m + 1)
                    n = min(4, self.kc - 4 * j)
                    for i in range(n):
                        k = 4 * j + i
                        ins = nc.tensor.transpose(ps[:, 4 + odd, i * P:(i + 1) * P],
                                                  self.prob[:, s % self.depth, k * P:(k + 1) * P], ident[:, :])
                    ins.then_inc(self.p_ps, 1)

            def values(g, u, c, part):
                s = 8 * u + 4 * c + 3
                for j in range(self.nb):
                    odd, m = self.chunk(g, s, j)
                    pe.wait_ge(self.p_dve if odd else self.p_act, m + 2)
                if self.nb == 1:
                    odd, m = self.chunk(g, s - 1, 0)
                    pe.wait_ge(self.p_dve if odd else self.p_act, m + 2)
                if c == 1 and part == 0:
                    pe.wait_ge(self.wo_out, g * 2 + u + 1)
                if c == 0 and part == 0:
                    pe.wait_ge(self.o_norm, g * 4 + (2 * u + 1))
                for k in range(self.kc * part // 4, self.kc * (part + 1) // 4):
                    for j in range(4):
                        h = 4 * c + j
                        v = vt[:, self.key_tile(self.tp_of, u) + k, 32 * h:32 * h + 32]
                        nc.tensor.matmul(ps[32 * j:32 * j + 32, 6 + c, 0:P], v,
                                         self.pT[:, h, k * P:(k + 1) * P], start=(k == 0), stop=(k == self.kc - 1))
                if part < 3:
                    return
                pe.wait_ge(self.r_exp, g * 4 + (2 * u + c + 1))
                nc.tensor.transpose(ps[:, 6 + c, P:2 * P], rexp[:, c, :], ident[:, :]).then_inc(self.pv, 1)

            def project(g, u):
                pe.wait_ge(self.o_norm, g * 4 + (2 * u + 4))
                for c in range(KC):
                    ins = nc.tensor.matmul(ps[:, 7, 2 * P:4 * P], oTn[:, u, c, :], self.wout[:, c, :],
                                           start=(c == 0), stop=(c == KC - 1))
                ins.then_inc(self.wo_ps, 1)

            def rest(g, s):
                if s - 2 in range(16):
                    turn(g, s - 2)
                for u in range(2):
                    if s == 8 * u + 16:
                        project(g, u)
                for u in range(2):
                    for c in range(2):
                        if s - (8 * u + 4 * c) in range(6, 10):
                            values(g, u, c, s - (8 * u + 4 * c) - 6)

            def pair(g, tp, prev):
                self.prev = prev
                for s in range(16):
                    scores(g, tp, s)
                    self.later(g, s, prev, rest, lambda n: self.set_tile(tp + n))

            def tail(g):
                self.tp_of = QT // 2 - 1
                for s in range(-self.lag, self.over):
                    rest(g - 1, s + 16)

            with pe.Fori(0, BATCH) as b:
                self.b = b
                self.loop(pe, b, prelude, pair, tail)

        def act(self, act):
            act.sem_inc(self.exp, 1)
            act.sem_inc(self.p_act, 1)

            def prelude(b):
                for hf in range(2):
                    act.wait_ge(self.hT_ps, b * 4 + 2 * hf + 1)
                    o, i = hT[:, 0, hf * BANK:(hf + 1) * BANK], ps[:, 4 + 2 * hf, :]
                    if self.local:
                        ins = nc.scalar.activation(o, i, ACT.Identity, scale=colv("n1w", 0), bias=colv("n1b", 0))
                    else:
                        ins = nc.scalar.activation(o, i, ACT.Copy)
                    ins.then_inc(self.hT_act, 1)
                job = 0
                for name, hi in (("kb", k_hi), ("qb", q_hi)):
                    for c in range(KC):
                        for hf in range(2):
                            act.wait_ge(self.proj_ps, b * 12 + (job + 1))
                            nc.scalar.activation(hi[:, c, hf * BANK:(hf + 1) * BANK], ps[:, job % 4, :], ACT.Identity,
                                                 bias=colv(f"{name}{self.n}", c)).then_inc(self.proj_hi, 1)
                            job += 1

            def softmax(g, s):
                act.wait_ge(self.masked, self.steps(g, s + 1) + 1)
                self.p_ps_turned(act, g, s)
                u, h = divmod(s, HEADS)
                d = s % self.depth
                nc.scalar.activation(self.prob[:, d, 0:self.kw], self.msc[:, d, 0:self.kw], ACT.Exp,
                                     scale=-1.0, bias=nmax[:, d:d + 1],
                                     accum_out=rsum[:, u, h:h + 1]).then_inc(self.exp, 1)

            def rest(g, s):
                if s - 2 in range(16):
                    for j in range(self.nb):
                        odd, m = self.chunk(g, s - 2, j)
                        if not odd:
                            self.copy_out(act, g, s - 2, j)
                for u in range(2):
                    for c in range(2):
                        if s == 8 * u + 4 * c + 10:
                            act.wait_ge(self.pv, g * 4 + (2 * u + c + 1) + 1)
                            nc.scalar.activation(rT[:, c, :], ps[:, 6 + c, P:2 * P], ACT.Copy)\
                              .then_inc(self.r_act, 1)

            def pair(g, tp, prev):
                self.prev = prev
                for s in range(16):
                    self.later(g, s, prev, rest)
                    softmax(g, s)

            def tail(g):
                for s in range(-self.lag, self.over):
                    rest(g - 1, s + 16)

            with act.Fori(0, BATCH) as b:
                self.loop(act, b, prelude, pair, tail)

        def p_ps_turned(self, act, g, s):
            back = s - self.depth
            if back >= 0:
                act.wait_ge(self.p_ps, g * (16 * self.nb) + self.nb * (back + 1) + 1)
            elif self.prev:
                act.wait_ge(self.p_ps, g * (16 * self.nb) - self.nb * (-back - 1) + 1)

        def copy_out(self, eng, g, s, j):
            odd, m = self.chunk(g, s, j)
            u, h = divmod(s, HEADS)
            w = min(BANK, self.kw - j * BANK)
            eng.wait_ge(self.p_ps, g * (16 * self.nb) + (self.nb * s + j + 1) + 1)
            eng.wait_ge(self.pv, (g * 4 + (2 * u + h // 4 - 1) if 2 * u + h // 4 >= 1 else g * 4 - 1 if self.prev else g * 4) + 1)
            o, i = self.pT[:, h, j * BANK:j * BANK + w], ps[:, 4 + odd, 0:w]
            if odd:
                nc.vector.tensor_copy(o, i).then_inc(self.p_dve, 1)
            else:
                nc.scalar.activation(o, i, ACT.Copy).then_inc(self.p_act, 1)

        def pool(self, pool):
            def pair(g, tp, prev):
                for u in range(2):
                    if prev:
                        pool.wait_ge(self.masked, g * 16 + (8 * u - 8) + 1)
                        pool.sem_inc(pool_passed, 1)
                    nc.gpsimd.tensor_copy(mask_tile[:, u, :], mask[:, bass.ds(tp * 2 + u, 1), :].rearrange("p o n -> p (o n)"))\
                      .then_inc(self.mask_set, 1)

            pair(0, 0, False)
            with pool.Fori(1, QT // 2) as tp:
                pair(tp, tp, True)
            with pool.Fori(1, BATCH) as b:
                with pool.Fori(0, QT // 2) as tp:
                    pair(b * 4 + tp, tp, True)

        def normal(self, dve, b, s):
            if s >= self.NORM_STEPS:
                return
            relink()
            if s < 2:
                if s == 0:
                    dve.wait_ge(self.x_in, b * 16 + 16)
                for t in range(4 * s, 4 * s + 4):
                    ins = nc.vector.bn_stats(stats[:, t, :], xb[:, t, :])
                link(ins)
                for t in range(4 * s, 4 * s + 4):
                    ins = nc.vector.bn_aggr(mv[:, t, :], stats[:, t, :])
                link(ins)
            elif s < 5:
                rsqrt(QT, parts=(s - 2,))
            else:
                t = s - 5
                nc.vector.tensor_scalar(self.xh[:, t, :], xb[:, t, :], mv[:, t, 0:1], nwt[:, 1, t:t + 1],
                                        ALU.subtract, ALU.mult).then_inc(self.x_norm, 1)

        def dve(self, dve):
            dve.sem_inc(self.masked, 1)
            dve.sem_inc(self.o_norm, 2)
            dve.sem_inc(self.p_dve, 1)
            dve.sem_inc(self.res_ok, 1)
            dve.sem_inc(self.wo_out, 1)
            n = self.n

            def prelude(b):
                for hf in range(2):
                    dve.wait_ge(self.hT_ps, b * 4 + 2 * hf + 2)
                    o, i = hT[:, 1, hf * BANK:(hf + 1) * BANK], ps[:, 5 + 2 * hf, :]
                    if self.local:
                        ins = nc.vector.tensor_scalar(o, i, colv("n1w", 1), colv("n1b", 1), ALU.mult, ALU.add)
                    else:
                        ins = nc.vector.tensor_copy(o, i)
                    ins.then_inc(self.hT_dve, 1)
                job = 0
                for name, hi, lo in (("kb", k_hi, k_lo), ("qb", q_hi, q_lo)):
                    for c in range(KC):
                        for hf in range(2):
                            dve.wait_ge(self.proj_hi, b * 8 + (job + 1))
                            w = slice(hf * BANK, (hf + 1) * BANK)
                            nc.vector.scalar_tensor_tensor(lo[:, c, w], ps[:, job % 4, :], colv(f"{name}{n}", c),
                                                           hi[:, c, w].bitcast(F32), ALU.add, ALU.subtract)\
                              .then_inc(self.proj_out, 1)
                            job += 1
                dve.wait_ge(self.stored, b * (16 * QT) + 16)
                r = rowv("pb0" if self.local else "ob1").rearrange("p (o c) -> p o c", o=1).broadcast_to([P, QT, C])
                nc.vector.tensor_tensor(res[:, :, :], xb[:, :, :] if self.local else self.xh[:, :, :], r, ALU.add)\
                  .then_inc(self.res_ok, 1)
                if self.local:
                    dve.wait_ge(mask_init, 16)
                vb = rowv(f"vb{n}").rearrange("p (o c) -> p o c", o=1).broadcast_to([P, 2, C])
                for t2 in range(QT // 2):
                    dve.wait_ge(self.proj_ps, b * 12 + (job + 1))
                    nc.vector.tensor_tensor(vt[:, 2 * t2:2 * t2 + 2, :],
                                            ps[:, job % 4, :].rearrange("p (u c) -> p u c", u=2), vb, ALU.add)\
                      .then_inc(self.proj_out, 1)
                    job += 1

            def add_mask(g, tp, s):
                u, h = divmod(s, HEADS)
                dve.wait_ge(self.qk, self.steps(g, s + 1) + 1)
                dve.wait_ge(self.exp, self.freed(g, s) + 1)
                dve.sem_inc(dve_passed, 1)
                if self.local and tp == 0 and s == 0:
                    dve.wait_ge(bias_ok, 3)
                if self.local:
                    extra = bias[:, self.kind(tp, u), h, :]
                else:
                    extra = mask_tile[:, u, :]
                    if h == 0:
                        dve.wait_ge(self.mask_set, g * 2 + (u + 1))
                        dve.sem_inc(dve_passed, 1)
                sc = ps[:, (self.nb * s) % 4:(self.nb * s) % 4 + self.nb, :].rearrange("p a n -> p (a n)")[:, 0:self.kw]
                d = s % self.depth
                nc.vector.tensor_tensor_reduce(out=self.msc[:, d, 0:self.kw], in0=sc, in1=extra, scale=1.0,
                                               scalar=BIG, op0=ALU.add, op1=ALU.min,
                                               accum_out=nmax[:, d:d + 1]).then_inc(self.masked, 1)

            def rest(g, s):
                if s - 2 in range(16):
                    for j in range(self.nb):
                        odd, m = self.chunk(g, s - 2, j)
                        if odd:
                            self.copy_out(dve, g, s - 2, j)
                for u in range(2):
                    for c in range(2):
                        if s == 8 * u + 4 * c + 5:
                            relink()
                            dve.wait_ge(self.exp, self.steps(g, 8 * u + 4 * c + 4) + 1)
                            link(nc.vector.reciprocal(rinv[:, :], rsum[:, u, 4 * c:4 * c + 4]))
                            nc.vector.tensor_copy(rexp[:, c, :].rearrange("p (h d) -> p h d", h=4),
                                                  rinv[:, :].rearrange("p (h o) -> p h o", o=1).broadcast_to([P, 4, HD]))\
                              .then_inc(self.r_exp, 1)
                        if s == 8 * u + 4 * c + 11:
                            dve.wait_ge(self.r_act, g * 4 + (2 * u + c + 1))
                            nc.vector.tensor_tensor(oTn[:, u, c, :], ps[:, 6 + c, 0:P], rT[:, c, :], ALU.mult)\
                              .then_inc(self.o_norm, 1)
                    if s == 8 * u + 17:
                        dve.wait_ge(self.wo_ps, g * 2 + (u + 1))
                        t = self.tp_of * 2 + u
                        r = res[:, bass.ds(t, 1), :].rearrange("p o c -> p (o c)")
                        nc.vector.tensor_tensor(r, ps[:, 7, 2 * P:4 * P], r, ALU.add).then_inc(self.wo_out, 1)

            def pair(g, tp, prev, following=None):
                self.prev = prev
                for s in range(16):
                    add_mask(g, tp, s)
                    self.later(g, s, prev, rest, lambda n: self.set_tile(tp + n))
                    if following is not None:
                        self.normal(dve, following, s)

            def tail(g):
                self.tp_of = QT // 2 - 1
                for s in range(-self.lag, self.over):
                    rest(g - 1, s + 16)

            def batch(b, more):
                following = b + 1 if more else None
                last = QT // 2 - 1
                prelude(b)
                pair(b * 4, 0, False)
                if self.local:
                    for tp in range(1, last):
                        pair(b * 4 + tp, tp, True)
                else:
                    with dve.Fori(1, last) as tp:
                        pair(b * 4 + tp, tp, True)
                pair(b * 4 + last, last, True, following)
                tail(b * 4 + 4)

            with dve.Fori(0, BATCH - 1) as b:
                batch(b, True)
            batch(BATCH - 1, False)

    att0 = Attention(0, x, x1_d, wq0, wp0, WK, True)
    att1 = Attention(1, x2_d, y_d, wq1, wo1, N, False)

    xm = sb("xm", [P, 2, 4, C], F32, at=at_q)
    xmh = sb("xmh", [P, 4, C], F32, at=at_q + 8192)
    mT = sb("mT", [P, KC, BANK], F32, at=at_q + 12288)
    gel = sb("gel", [P, HCH, BANK], F32, at=at_att)
    gel_hi = sb("gel_hi", [P, HCH, BANK], F32R, at=at_k)
    gel_lo = sb("gel_lo", [P, HCH, BANK], F32R, at=at_att)
    mT_hi = sb("mT_hi", [P, KC, BANK], F32R, at=at_k + 16384)
    mT_lo = sb("mT_lo", [P, KC, BANK], F32R, at=at_q + 12288)
    wf1_hi = sb("wf1_hi", [P, KC, HID], F32R, at=at_att + 16384)
    wf2_hi = sb("wf2_hi", [P, HCH, C], F32R, at=at_att + 24576)
    wf1_lo = sb("wf1_lo", [P, KC, HID], F32R, at=at_wf1)
    wf2_lo = sb("wf2_lo", [P, HCH, C], F32R, at=at_wf1 + 8192)
    x2t = sb("x2t", [P, 2, 4, C], F32, at=at_q + 16384)
    m_in = [sem("m_in_a"), sem("m_in_b")]
    wq1_in = sem("wq1_in")
    m_norm = sem("m_norm")
    m_turn = sem("m_turn")
    m_act = sem("m_act")
    m_dve = sem("m_dve")
    m_used = sem("m_used")
    m_hi = sem("m_hi")
    m_lo = sem("m_lo")
    g_hi = sem("g_hi")
    g_lo = sem("g_lo")
    wf_hi = sem("wf_hi")
    wf_lo = sem("wf_lo")
    f1_ps = sem("f1_ps")
    f1_out = sem("f1_out")
    f2_ps = sem("f2_ps")
    f2_out = sem("f2_out")
    m_stored = [sem("m_stored_a"), sem("m_stored_b")]
    GROUPS = TILES // 4

    def mlp_loop(eng, group, between=lambda: None):
        with eng.Fori(0, GROUPS // 2 - 1) as i:
            for u in range(2):
                group(i * 2 + u, i, u, True)
        between()
        for u in range(2):
            group(GROUPS - 2 + u, GROUPS // 2 - 1, u, u == 0)

    def mlp_sp(sp):
        for c in m_stored:
            sp.sem_inc(c, 16)
        x1, x2 = tiles(x1_d), tiles(x2_d)
        sp.wait_ge(att0.stored, 16 * TILES + 16)
        sp.sem_inc(sp_passed, 1)

        def load(g, i, u):
            sp.dma_start(xm[:, u, :, :], x1[:, bass.ds(g * 4, 4), :]).then_inc(m_in[u], 16)

        def group(g, i, u, more):
            if not isinstance(g, int):
                sp.wait_ge(m_used, g + 1)
                sp.sem_inc(sp_passed, 1)
                load(g + 2, i, u)
            zero_sp(sp, g)
            sp.wait_ge(f2_out, g * 4 + 5)
            sp.sem_inc(sp_passed, 1)
            sp.dma_start(x2[:, bass.ds(g * 4, 4), :], x2t[:, u, :, :]).then_inc(m_stored[u], 16)

        def following():
            for c in m_stored:
                sp.wait_ge(c, 16 * (GROUPS // 2 - 1) + 16)
            att1.load(sp, 0)

        load(0, 0, 0)
        load(1, 0, 1)
        sp.dma_start(wq1[:, :, :], w_qkv1.rearrange("(k p) n -> p k n", p=P)).then_inc(wq1_in, 16)
        mlp_loop(sp, group, following)

    def mlp_pe(pe):
        def turn(g):
            pe.wait_ge(m_norm, g + 1)
            for c in range(KC):
                for t in range(4):
                    ins = nc.tensor.transpose(ps[:, 6 + c, t * P:(t + 1) * P], xmh[:, t, c * P:(c + 1) * P], ident[:, :])
                ins.then_inc(m_turn, 1)

        def group(g, i, u, more):
            pe.wait_ge(m_lo, g + 1)
            for h in range(HCH):
                pe.wait_ge(f1_out, (g * HCH + (h - 3) if h >= 3 else g * HCH) + 1)
                cols = slice(h * P, (h + 1) * P)
                parts = [(w, m, k) for k in range(KC) for w, m in ((wf1_hi, mT_hi), (wf1_hi, mT_lo), (wf1_lo, mT_hi))]
                for n, (w, m, k) in enumerate(parts):
                    ins = nc.tensor.matmul(ps[:, h % 4, :], w[:, k, cols], m[:, k, :],
                                           start=(n == 0), stop=(n == len(parts) - 1))
                ins.then_inc(f1_ps, 1)
            if more:
                turn(g + 1)
            pe.wait_ge(g_lo, g * HCH + HCH)
            for t in range(4):
                pe.wait_ge(f2_out, (g * 4 + (t - 1) if t else g * 4) + 1)
                parts = [(q, w, h) for h in range(HCH) for q, w in ((gel_hi, wf2_hi), (gel_hi, wf2_lo), (gel_lo, wf2_hi))]
                for n, (q, w, h) in enumerate(parts):
                    ins = nc.tensor.matmul(ps[:, 4 + t % 2, 0:C], q[:, h, t * P:(t + 1) * P], w[:, h, :],
                                           start=(n == 0), stop=(n == len(parts) - 1))
                ins.then_inc(f2_ps, 1)

        turn(0)
        pe.wait_ge(wf_lo, 2)
        mlp_loop(pe, group)
        pe.wait_ge(f2_out, GROUPS * 4 + 1)

    def mlp_act(act):
        act.sem_inc(f1_out, 1)

        def bring(g):
            act.wait_ge(m_turn, g * 2 + 1)
            nc.scalar.activation(mT[:, 0, :], ps[:, 6, :], ACT.Identity, scale=colv("n2w", 0), bias=colv("n2b", 0))\
              .then_inc(m_act, 1)
            act.wait_ge(m_act, g + 1)
            act.wait_ge(m_dve, g + 1)
            nc.scalar.activation(mT_hi[:, :, :], mT[:, :, :], ACT.Copy).then_inc(m_hi, 1)

        def high(g, h):
            act.wait_ge(f1_out, g * HCH + (h + 1) + 1)
            nc.scalar.activation(gel_hi[:, h, :], gel[:, h, :], ACT.Copy).then_inc(g_hi, 1)

        def group(g, i, u, more):
            act.wait_ge(f2_out, g * 4 + 1)
            for h in range(HCH):
                act.wait_ge(f1_ps, g * HCH + (h + 1))
                nc.scalar.activation(gel[:, h, :], ps[:, h % 4, :], ACT.Gelu, bias=colv("fb", h)).then_inc(f1_out, 1)
                if h:
                    high(g, h - 1)
            high(g, HCH - 1)
            if more:
                bring(g + 1)

        act.wait_ge(wf_ok, 1)
        nc.scalar.activation(wf1_hi[:, :, :], wf1[:, :, :], ACT.Copy).then_inc(wf_hi, 1)
        nc.scalar.activation(wf2_hi[:, :, :], wf2[:, :, :], ACT.Copy).then_inc(wf_hi, 1)
        bring(0)
        mlp_loop(act, group)

    def mlp_dve(dve):
        dve.sem_inc(f2_out, 1)
        f2b = rowv("f2b").rearrange("p (o c) -> p o c", o=1).broadcast_to([P, 4, C])

        def normal(g, i, u):
            relink()
            dve.wait_ge(m_in[u], i * 16 + 16)
            for t in range(4):
                ins = nc.vector.bn_stats(stats[:, t, :], xm[:, u, t, :])
            link(ins)
            for t in range(4):
                ins = nc.vector.bn_aggr(mv[:, t, :], stats[:, t, :])
            link(ins)
            rsqrt(4)
            for t in range(4):
                ins = nc.vector.tensor_scalar(xmh[:, t, :], xm[:, u, t, :], mv[:, t, 0:1], nwt[:, 1, t:t + 1],
                                              ALU.subtract, ALU.mult)
            ins.then_inc(m_norm, 1)
            dve.wait_ge(m_stored[u], i * 16 + 16)
            nc.vector.tensor_tensor(x2t[:, u, :, :], xm[:, u, :, :], f2b, ALU.add).then_inc(m_used, 1)

        def turned(g, i, u):
            relink()
            dve.wait_ge(m_turn, g * 2 + 2)
            nc.vector.tensor_scalar(mT[:, 1, :], ps[:, 7, :], colv("n2w", 1), colv("n2b", 1), ALU.mult, ALU.add)\
              .then_inc(m_dve, 1)
            dve.wait_ge(m_hi, g + 1)
            nc.vector.tensor_tensor(mT_lo[:, :, :], mT[:, :, :], mT_hi[:, :, :].bitcast(F32), ALU.subtract).then_inc(m_lo, 1)

        def group(g, i, u, more):
            if more:
                normal(g + 1, i + u, 1 - u)
            for h in range(HCH):
                dve.wait_ge(g_hi, g * HCH + (h + 1))
                nc.vector.tensor_tensor(gel_lo[:, h, :], gel[:, h, :], gel_hi[:, h, :].bitcast(F32), ALU.subtract)\
                  .then_inc(g_lo, 1)
            if more:
                turned(g + 1, i + u, 1 - u)
            dve.wait_ge(m_used, g + 1)
            final = isinstance(g, int) and g == GROUPS - 1
            for t in range(4):
                if final:
                    for s in range(4 * t, min(4 * t + 4, att1.NORM_STEPS)):
                        att1.normal(dve, 0, s)
                dve.wait_ge(f2_ps, g * 4 + (t + 1))
                ins = nc.vector.tensor_tensor(x2t[:, u, t, :], ps[:, 4 + t % 2, 0:C], x2t[:, u, t, :], ALU.add)
                ins.then_inc(f2_out, 1)

        relink()
        dve.wait_ge(ld_f, 64)
        scale_rows(dve, "g2", wf2, "f2b", HCH).then_inc(wf_ok, 1)
        dve.wait_ge(wf_ok, 1)
        normal(0, 0, 0)
        for n, (lo, w, hi) in enumerate(((wf1_lo, wf1, wf1_hi), (wf2_lo, wf2, wf2_hi))):
            dve.wait_ge(wf_hi, n + 1)
            nc.vector.tensor_tensor(lo[:, :, :], w[:, :, :], hi[:, :, :].bitcast(F32), ALU.subtract).then_inc(wf_lo, 1)
        turned(0, 0, 0)
        dve.wait_ge(wq1_in, 16)
        relink()
        link(nc.vector.tensor_scalar(wq1[:, :, 0:C], wq1[:, :, 0:C], -SCALE, None, ALU.mult))
        mlp_loop(dve, group)

    def prep_sp(sp):
        att0.load(sp, 0)
        edge_view = edges.rearrange("a (p n) -> a p n", p=P)
        sp.dma_start(e_src[:, :], edge_view[0]).then_inc(edge_ld, 16)
        sp.dma_start(e_dst[:, :], edge_view[1]).then_inc(edge_ld, 16)
        for dst, src in ((col[:, :], cols), (wq0[:, :, :], w_qkv0.rearrange("(k p) n -> p k n", p=P)),
                         (wp0[:, :, :], w_proj0.rearrange("(k p) n -> p k n", p=P))):
            sp.dma_start(dst, src).then_inc(ld, 16)
        sp.dma_start(row[:, :].rearrange("p (r c) -> p r c", c=C), rows.rearrange("(o r) c -> o r c", o=1).broadcast_to([P, len(NROW), C]))\
          .then_inc(ld, 16)
        sp.dma_start(wmask[:, :, :], window_mask).then_inc(ld_b, 16)
        sp.wait_ge(prep_p, 3)
        for i in range(ROWS):
            sp.dma_start(toep[32 * i:32 * i + 32, i + 2:i + 15, :, :].rearrange("p a h c -> p (a h c)"), rpb_toeplitz)\
              .then_inc(ld_b, 16)
        sp.wait_ge(big_ready, 1)
        sp.dma_start(mask_d.rearrange("(p k n) o -> p k (n o)", p=P, n=2048),
                     big[:, :].rearrange("p (o n) -> p o n", o=1).broadcast_to([P, 16, 2048])).then_inc(mask_init, 16)

    def later_weights(sp):
        for dst, src in ((wf1, w_fc1), (wf2, w_fc2), (wo1, w_o1), (wr, w_router)):
            sp.dma_start(dst[:, :, :], src.rearrange("(k p) n -> p k n", p=P)).then_inc(ld_f, 16)

    def zero_sp(sp, g):
        n = XT // GROUPS
        sp.dma_start(tiles(xs_d)[:, bass.ds(g * n, n), :],
                     zeros[:, :].rearrange("p (o c) -> p o c", o=1).broadcast_to([P, n, C])).then_inc(xs_zero, 16)

    def prep_pool(pool):
        nc.gpsimd.memset(ident[:, :], 0.0).then_inc(prep_p, 1)
        nc.gpsimd.memset(zeros[:, :], 0.0).then_inc(prep_p, 1)
        nc.gpsimd.memset(toep[:, :, :, :], 0.0).then_inc(prep_p, 1)
        pool.wait_ge(prep_p, 1)
        nc.gpsimd.affine_select(out=ident[:, :], in_=ident[:, :], compare_op=ALU.not_equal, fill=1.0,
                                base=0, pattern=[[-1, P]], channel_multiplier=1).then_inc(prep_p, 1)

    def scatter_pool(pool):
        pool.wait_ge(edge_ready, 1)
        pool.wait_ge(mask_init, 16)
        half = EBATCH // 2
        zero = zeros[:, :].bitcast(BF16)[:, 0:1]
        def columns(i):
            for x in range(EBATCH):
                if x in (0, 4):
                    a = 0 if x == 0 else half
                    nc.gpsimd.tensor_copy(edge_slot[:, a:a + half], edge_at[:, bass.ds(i * EBATCH + a, half)])\
                      .then_inc(slot_copy, 1)
                if x in (0, half):
                    pool.wait_ge(slot_copy, i * 2 + (1 if x == 0 else 2))
                    pool.sem_inc(pool_passed, 1)
                k = x % COPIES
                if x >= COPIES or not isinstance(i, int):
                    pool.wait_ge(scat[k], i * (EBATCH // COPIES * 16) + 16 * (x // COPIES))
                    pool.sem_inc(pool_passed, 1)
                pool.indirect_dma_start(mask_d, bass.IndirectOffsetOnAxis(edge_slot[:, x:x + 1], 0), zero, None,
                                        bounds_check=COPIES * CELLS - 1, oob_is_err=False).then_inc(scat[k], 16)

        columns(0)
        with pool.Fori(1, ECOL // EBATCH) as i:
            columns(i)

    def scale_rows(dve, nme, w, b, n):
        link(nc.vector.scalar_tensor_tensor(rowv(nme), rowv(nme), -1.0, rowv(nme), ALU.mult, ALU.max))
        g = rowv(nme).rearrange("p (o c) -> p o c", o=1).broadcast_to([P, n, C])
        nc.vector.tensor_tensor(rowv(b), rowv(b), rowv(nme), ALU.mult)
        return nc.vector.tensor_tensor(w[:, :, :], w[:, :, :], g, ALU.mult)

    def prep_dve(dve):
        nc.vector.memset(big[:, :], NO_EDGE).then_inc(big_ready, 1)
        relink()
        dve.wait_ge(edge_ld, 32)
        link(nc.vector.tensor_scalar(e_tmp[:, :], e_dst[:, :], float(N), None, ALU.is_ge))
        link(nc.vector.scalar_tensor_tensor(e_tmp[:, :], e_src[:, :], float(N), e_tmp[:, :], ALU.is_ge, ALU.max))
        link(nc.vector.scalar_tensor_tensor(e_src[:, :], e_src[:, :], float(N), e_dst[:, :], ALU.mult, ALU.add))
        link(nc.vector.scalar_tensor_tensor(edge_at[:, :], e_tmp[:, :], float(1 << 23), e_src[:, :], ALU.mult, ALU.add))
        for k in range(1, COPIES):
            v = edge_at[:, :].rearrange("p (n k) -> p n k", k=COPIES)[:, :, k]
            link(nc.vector.tensor_scalar(v, v, float(k * CELLS), None, ALU.add))
        nc.vector.memset(nwi[:, :], 0).then_inc(edge_ready, 1)
        dve.wait_ge(ld, 16 * 4)
        link(nc.vector.tensor_scalar(wq0[:, :, 0:C], wq0[:, :, 0:C], -SCALE, None, ALU.mult))
        for nme in ("qb0", "qb1"):
            link(nc.vector.tensor_scalar(col[:, cat[nme]:cat[nme] + KC], col[:, cat[nme]:cat[nme] + KC], -SCALE, None, ALU.mult))
        link(scale_rows(dve, "g1", wp0, "pb0", KC))
        nc.vector.memset(nwt[:, :, :], 0.0).then_inc(prep_v, 1)
        dve.wait_ge(prep_v, 1)

    def bias_pool(pool):
        pool.wait_ge(ld_b, 16 + 16 * ROWS)
        for kind, first in enumerate((8, 4, 0)):
            nc.gpsimd.tensor_tensor(
                bias[:, kind, :, :].rearrange("p h (r c) -> p h r c", c=SIDE),
                wmask[:, kind, :].rearrange("p (o r c) -> p o r c", o=1, c=SIDE).broadcast_to([P, HEADS, WT * ROWS, SIDE]),
                toep[:, first:first + WT * ROWS, :, :].rearrange("p r h c -> p h r c"), ALU.subtract)\
              .then_inc(bias_ok, 1)

    def mask_pool(pool):
        masks = mask_d.rearrange("(k t p n) o -> t p k (n o)", k=COPIES, t=QT, p=P)
        for c in scat:
            pool.wait_ge(c, 16 * (ECOL // COPIES))
        pool.wait_ge(att0.stored, 16 * TILES + 16)

        def load(t, u):
            pool.dma_start(mcopy[:, u, :, :], masks[t]).then_inc(mask_in[u], 16)

        load(0, 0)
        for t in range(QT):
            u = t % 2
            if t + 1 < QT:
                if t:
                    pool.wait_ge(mask_ok, t)
                load(t + 1, 1 - u)
            pool.wait_ge(mask_in[u], 16 * (t // 2 + 1))
            nc.gpsimd.tensor_tensor(mcopy[:, u, 0:2, :], mcopy[:, u, 0:2, :], mcopy[:, u, 2:4, :], ALU.mult)\
              .then_inc(mask_half, 1)
            pool.wait_ge(mask_half, t + 1)
            nc.gpsimd.tensor_tensor(mask[:, t, :], mcopy[:, u, 0, :], mcopy[:, u, 1, :], ALU.mult).then_inc(mask_ok, 1)
        pool.wait_ge(mask_ok, QT)

    at_z = at_w0 + 20480
    moe_at = {"at": at_w0}

    def mb(name, shape, dt=F32, at=None):
        n = 4 * int(np.prod(shape[1:]))
        if at is None:
            at = moe_at["at"]
            moe_at["at"] = (at + n + 31) // 32 * 32
        return sb(name, shape, dt, at=at)

    gate = mb("gate", [P, 2, TILES])
    pos = mb("pos", [P, TILES, 2], I32)
    te = mb("te", [P, BLOCKS], I32)
    at_work = moe_at["at"]
    rc = mb("route", [P, EXPERTS + 2 * P + BLOCKS])
    st32 = mb("stats32", [P, TILES, 6])
    mv32 = mb("mv32", [P, TILES, 2])
    mvz = mb("mvz", [P, TILES, 2])
    nwt32 = mb("nwt32", [P, 3, TILES])
    nwi32 = mb("nwi32", [P, TILES], I32)
    at_zT = moe_at["at"]
    zT = mb("zT", [P, 2, KC, BANK])
    te_ge = mb("te_ge", [P, BLOCKS, EXPERTS], at=at_zT)
    te_f = mb("te_f", [P, BLOCKS], at=at_zT + 2304)
    acc_a = mb("acc_a", [P, TILES, EXPERTS], at=at_zT + 2304 + 512)
    acc_b = mb("acc_b", [P, TILES, EXPERTS], at=at_zT + 2304 + 512 + 1024)
    lg = mb("lg", [P, TILES, EXPERTS])
    pr = mb("pr", [P, TILES, EXPERTS])
    oh = mb("oh", [P, 2, TILES, EXPERTS])
    tot = mb("tot", [P, TILES, EXPERTS])
    m1 = mb("m1", [P, TILES])
    rsm = mb("rsm", [P, TILES])
    topp = mb("topp", [P, 2, TILES])
    posf = mb("posf", [P, 2, TILES])
    cnt = mb("cnt", [P, 4, EXPERTS])
    cnt_i = mb("cnt_i", [P, EXPERTS], I32)
    assert moe_at["at"] <= at_z
    zall = sb("zall", [P, TILES, C], F32, at=at_z)
    at_w13 = at_z + 32768
    W13 = sb("W13", [P, EXPERTS, KC, 2 * FF], F32, at=at_w13)
    at_w2 = at_w13 + EXPERTS * KC * 2 * FF * 4
    W2 = sb("W2", [P, EXPERTS, FCH, C], F32, at=at_w2)
    zs2 = sb("zs2", [P, 2, 4, C], F32, at=at_w13 + 6 * KC * 2 * FF * 4)
    t2b = sb("t2b", [P, TILES, C], F32, at=at_w2 + 2 * FCH * C * 4)
    assert at_w2 + EXPERTS * FCH * C * 4 <= nc.sbuf_usable_end
    G1 = TILES // 4
    xs_zero = sem("xs_zero")
    rc_in = sem("rc_in")
    y_in = [sem(f"y_in{q}") for q in range(CHUNKS)]
    x2_in = [sem(f"x2_in{q}") for q in range(CHUNKS)]
    t2_ok = sem("t2_ok")
    t2_stored = sem("t2_stored")
    w13_in = sem("w13_in")
    w2_in = sem("w2_in")
    x2b_ok = sem("x2b_ok")
    z_ok = sem("z_ok")
    z_turn = sem("z_turn")
    z_act = sem("z_act")
    z_copy = sem("z_copy")
    z_dve = sem("z_dve")
    lg_ps = sem("lg_ps")
    lg_ok = sem("lg_ok")
    lg_exp = sem("lg_exp")
    oh_ok = sem("oh_ok")
    rank_ps = sem("rank_ps")
    routed = sem("routed")

    def m1_sp(sp):
        sp.wait_ge(att1.stored, 16 * TILES + 16)
        sp.sem_inc(sp_passed, 1)
        sp.dma_start(rc[:, :], route_const).then_inc(rc_in, 16)
        ty, tx = tiles(y_d), tiles(x2_d)
        for dst, src, done in ((zall, ty, y_in), (t2b, tx, x2_in)):
            for q in range(CHUNKS):
                w = slice(q * QT, (q + 1) * QT)
                sp.dma_start(dst[:, w, :], src[:, w, :]).then_inc(done[q], 16)
        for e in range(0, EXPERTS - 2, 2):
            load_w13(sp, e)
        load_w2(sp, 0)
        sp.wait_ge(t2_ok, G1)
        sp.sem_inc(sp_passed, 1)
        sp.dma_start(tiles(t2_d), t2b[:, :, :]).then_inc(t2_stored, 16)
        sp.wait_ge(t2_stored, 16)
        sp.wait_ge(z_ok, G1)
        for e in range(2, EXPERTS, 2):
            load_w2(sp, e)
        sp.wait_ge(z_turn, 2 * G1 + 1)
        sp.wait_ge(z_copy, G1 + 2)
        load_w13(sp, EXPERTS - 2)

    def load_w13(sp, e):
        sp.dma_start(W13[:, e:e + 2, :, :].rearrange("p e k n -> p (e k) n"),
                     w13[e:e + 2].rearrange("e (k p) n -> p (e k) n", p=P)).then_inc(w13_in, 16)

    def load_w2(sp, e):
        sp.dma_start(W2[0:FCW, e:e + 2, :, :].rearrange("p e k n -> p (e k) n"),
                     w2[e:e + 2].rearrange("e (k p) n -> p (e k) n", p=FCW)).then_inc(w2_in, 16)

    def m1_pool(pool):
        bet = rowv("bet").rearrange("p (o c) -> p o c", o=1).broadcast_to([P, QT, C])
        for q in range(CHUNKS):
            pool.wait_ge(x2_in[q], 16)
            v = t2b[:, q * QT:(q + 1) * QT, :]
            nc.gpsimd.tensor_tensor(v, v, bet, ALU.add).then_inc(x2b_ok, 1)

    def m1_pe(pe):
        pe.sem_inc(z_turn, 1)

        def turn(g, u):
            pe.wait_ge(z_ok, g + 1)
            pe.wait_ge(z_act, g + 1)
            pe.wait_ge(z_dve, g + 1)
            for c in range(KC):
                for t in range(4):
                    ins = nc.tensor.transpose(ps[:, 2 * u + c, t * P:(t + 1) * P],
                                              zs2[:, u, t, c * P:(c + 1) * P], ident[:, :])
                ins.then_inc(z_turn, 1)

        def route(g, u):
            pe.wait_ge(z_act, g + 3)
            pe.wait_ge(z_dve, g + 3)
            for t in range(4):
                for k in range(KC):
                    ins = nc.tensor.matmul(ps[:, 5, bass.ds(g * 4 * EXPERTS + t * EXPERTS, EXPERTS)],
                                           zT[:, u, k, t * P:(t + 1) * P], wr[:, k, :],
                                           start=(k == 0), stop=(k == KC - 1))
            ins.then_inc(lg_ps, 1)

        turn(0, 0)
        with pe.Fori(0, G1 // 2 - 1) as i:
            for u in range(2):
                turn(i * 2 + (u + 1), 1 - u)
                route(i * 2 + u, u)
        turn(G1 - 1, 1)
        for u in range(2):
            route(G1 - 2 + u, u)
        pe.wait_ge(oh_ok, 1)
        chosen = pr[:, :, :].rearrange("p t e -> p (t e)")
        nc.tensor.matmul(ps[:, 4, 0:TILES * EXPERTS], rc[:, EXPERTS:EXPERTS + P], chosen, start=True, stop=True)
        nc.tensor.matmul(ps[:, 4, TILES * EXPERTS:2 * TILES * EXPERTS], rc[:, EXPERTS + P:EXPERTS + 2 * P], chosen,
                         start=True, stop=True).then_inc(rank_ps, 1)

    def m1_act(act):
        act.sem_inc(z_act, 2)
        act.sem_inc(z_copy, 2)
        with act.Fori(0, G1 // 2) as i:
            for u in range(2):
                act.wait_ge(z_ok, i * 2 + (u + 1))
                nc.scalar.activation(zall[:, bass.ds(i * 8 + u * 4, 4), :], zs2[:, u, :, :], ACT.Copy)\
                  .then_inc(z_copy, 1)
                act.wait_ge(z_turn, i * 4 + (2 * u + 1) + 1)
                nc.scalar.activation(zT[:, u, 0, :], ps[:, 2 * u, :], ACT.Copy).then_inc(z_act, 1)
        act.wait_ge(lg_ok, 1)
        nc.scalar.activation(pr[:, :, :], lg[:, :, :], ACT.Exp).then_inc(lg_exp, 1)

    def over(ap, n):
        return ap.rearrange("p (a o) -> p a o", o=1).broadcast_to([P, ap.shape[1], n])

    def m1_dve(dve):
        dve.sem_inc(z_dve, 2)
        gam = rowv("gam")

        def tile_of(buf, g):
            return [buf[:, bass.ds(g * 4 + t, 1), :].rearrange("p o c -> p (o c)") for t in range(4)]

        relink()
        for q in range(CHUNKS):
            dve.wait_ge(y_in[q], 16)
            for t in range(q * QT, (q + 1) * QT):
                ins = nc.vector.bn_stats(st32[:, t, :], zall[:, t, :])
            link(ins)
            for t in range(q * QT, (q + 1) * QT):
                ins = nc.vector.bn_aggr(mv32[:, t, :], st32[:, t, :])
            link(ins)
        rsqrt(TILES, mv32, nwt32, nwi32)
        with dve.Fori(0, CHUNKS) as i:
            for u in range(2):
                g = i * 2 + u
                relink()
                dve.wait_ge(x2b_ok, i + 1)
                zs, ts = tile_of(zall, g), tile_of(t2b, g)
                for t in range(4):
                    ins = nc.vector.scalar_tensor_tensor(zs[t], zs[t], mv32[:, bass.ds(g * 4 + t, 1), 0], gam,
                                                         ALU.subtract, ALU.mult)
                link(ins)
                for t in range(4):
                    ins = nc.vector.scalar_tensor_tensor(ts[t], zs[t], nwt32[:, 1, bass.ds(g * 4 + t, 1)], ts[t],
                                                         ALU.mult, ALU.add)
                ins.then_inc(t2_ok, 1)
                dve.wait_ge(t2_ok, g + 1)
                dve.sem_inc(dve_passed, 1)
                for t in range(4):
                    ins = nc.vector.bn_stats(st32[:, t, :], ts[t])
                link(ins)
                for t in range(4):
                    ins = nc.vector.bn_aggr(mv[:, t, :], st32[:, t, :])
                link(ins)
                link(nc.vector.tensor_copy(mvz[:, bass.ds(g * 4, 4), :], mv[:, 0:4, :]))
        relink()
        rsqrt(TILES, mvz, nwt32, nwi32)

        def normal(g, u, again):
            ts = tile_of(t2b, g)
            if again:
                dve.wait_ge(z_turn, g * 2 - 1)
                dve.wait_ge(z_copy, g + 1)
            for t in range(4):
                ins = nc.vector.tensor_scalar(zs2[:, u, t, :], ts[t], mvz[:, bass.ds(g * 4 + t, 1), 0],
                                              nwt32[:, 1, bass.ds(g * 4 + t, 1)], ALU.subtract, ALU.mult)
            ins.then_inc(z_ok, 1)

        def bring(g, u):
            dve.wait_ge(z_turn, g * 2 + 3)
            nc.vector.tensor_copy(zT[:, u, 1, :], ps[:, 2 * u + 1, :]).then_inc(z_dve, 1)

        for u in range(2):
            normal(u, u, False)
        with dve.Fori(0, G1 // 2 - 1) as i:
            for u in range(2):
                bring(i * 2 + u, u)
                normal(i * 2 + (u + 2), u, True)
        for u in range(2):
            bring(G1 - 2 + u, u)
        relink()
        dve.wait_ge(lg_ps, G1)
        dve.wait_ge(rc_in, 16)
        nop = EXPERTS
        flat = ps[:, 5, 0:TILES * EXPERTS].rearrange("p (t e) -> p t e", e=EXPERTS)
        link(nc.vector.tensor_reduce(m1[:, :], flat, AX.X, ALU.max))
        nc.vector.tensor_tensor(lg[:, :, :], flat, over(m1[:, :], nop), ALU.subtract).then_inc(lg_ok, 1)
        dve.wait_ge(lg_exp, 1)
        link(nc.vector.tensor_reduce(rsm[:, :], pr[:, :, :], AX.X, ALU.add))
        link(nc.vector.reciprocal(rsm[:, :], rsm[:, :]))
        link(nc.vector.tensor_tensor(pr[:, :, :], pr[:, :, :], over(rsm[:, :], nop), ALU.mult))
        ids = rc[:, 0:EXPERTS].rearrange("p (o e) -> p o e", o=1).broadcast_to([P, TILES, EXPERTS])
        for k in range(2):
            link(nc.vector.tensor_reduce(topp[:, k, :], pr[:, :, :], AX.X, ALU.max))
            link(nc.vector.tensor_tensor(oh[:, k, :, :], pr[:, :, :], over(topp[:, k, :], nop), ALU.is_equal))
            link(nc.vector.tensor_tensor(oh[:, k, :, :], oh[:, k, :, :], ids, ALU.mult))
            link(nc.vector.tensor_reduce(m1[:, :], oh[:, k, :, :], AX.X, ALU.min))
            link(nc.vector.tensor_tensor(oh[:, k, :, :], ids, over(m1[:, :], nop), ALU.is_equal))
            if k == 0:
                link(nc.vector.scalar_tensor_tensor(pr[:, :, :], oh[:, 0, :, :], -2.0, pr[:, :, :], ALU.mult, ALU.add))
        nc.vector.tensor_tensor(pr[:, :, :], oh[:, 0, :, :], oh[:, 1, :, :], ALU.add).then_inc(oh_ok, 1)
        link(nc.vector.tensor_tensor(rsm[:, :], topp[:, 0, :], topp[:, 1, :], ALU.add))
        link(nc.vector.tensor_scalar(rsm[:, :], rsm[:, :], 1e-9, None, ALU.add))
        link(nc.vector.reciprocal(rsm[:, :], rsm[:, :]))
        for k in range(2):
            link(nc.vector.tensor_tensor(gate[:, k, :], topp[:, k, :], rsm[:, :], ALU.mult))
        dve.wait_ge(rank_ps, 1)
        totals = ps[:, 4, TILES * EXPERTS:2 * TILES * EXPERTS].rearrange("p (t e) -> p t e", e=EXPERTS)
        link(nc.vector.tensor_copy(tot[:, :, :], totals))
        src, a, b = tot, acc_a, acc_b
        d = 1
        while d < TILES:
            nc.vector.tensor_copy(a[:, 0:d, :], src[:, 0:d, :])
            link(nc.vector.tensor_tensor(a[:, d:, :], src[:, d:, :], src[:, 0:TILES - d, :], ALU.add))
            src, a, b = a, b, a
            d *= 2
        inc = src
        link(nc.vector.tensor_scalar(cnt_i[:, :], inc[:, TILES - 1, :], float(BLOCK - 1), None, ALU.add))
        link(nc.vector.tensor_scalar(cnt_i[:, :], cnt_i[:, :], BLOCK.bit_length() - 1, None, ALU.logical_shift_right))
        link(nc.vector.tensor_copy(cnt[:, 0, :], cnt_i[:, :]))
        s, d = 0, 1
        while d < EXPERTS:
            nc.vector.tensor_copy(cnt[:, s + 1, 0:d], cnt[:, s, 0:d])
            link(nc.vector.tensor_tensor(cnt[:, s + 1, d:], cnt[:, s, d:], cnt[:, s, 0:EXPERTS - d], ALU.add))
            s += 1
            d *= 2
        ends = cnt[:, s, :]
        nums = rc[:, EXPERTS + 2 * P:].rearrange("p (j o) -> p j o", o=1).broadcast_to([P, BLOCKS, EXPERTS])
        link(nc.vector.tensor_tensor(te_ge[:, :, :], nums,
                                     ends.rearrange("p (o e) -> p o e", o=1).broadcast_to([P, BLOCKS, EXPERTS]), ALU.is_ge))
        link(nc.vector.tensor_reduce(te_f[:, :], te_ge[:, :, :], AX.X, ALU.add))
        link(nc.vector.tensor_scalar(te[:, :], te_f[:, :], float(EXPERTS - 1), None, ALU.min))
        link(nc.vector.tensor_tensor(cnt[:, 1, :], ends, cnt[:, 0, :], ALU.subtract))
        link(nc.vector.tensor_scalar(cnt[:, 1, :], cnt[:, 1, :], float(BLOCK), None, ALU.mult))
        link(nc.vector.tensor_tensor(inc[:, :, :], inc[:, :, :], tot[:, :, :], ALU.subtract))
        link(nc.vector.tensor_tensor(inc[:, :, :], inc[:, :, :], ps[:, 4, 0:TILES * EXPERTS].rearrange("p (t e) -> p t e", e=EXPERTS), ALU.add))
        link(nc.vector.tensor_tensor(inc[:, :, :], inc[:, :, :], cnt[:, 1, :].rearrange("p (o e) -> p o e", o=1).broadcast_to([P, TILES, EXPERTS]), ALU.add))
        for k in range(2):
            link(nc.vector.tensor_tensor(oh[:, k, :, :], oh[:, k, :, :], inc[:, :, :], ALU.mult))
            link(nc.vector.tensor_reduce(posf[:, k, :], oh[:, k, :, :], AX.X, ALU.add))
            ins = nc.vector.tensor_copy(pos[:, :, k], posf[:, k, :])
            link(ins)
        nc.vector.memset(st32[:, 0, :], 0.0).then_inc(routed, 1)

    moe_at["at"] = at_row
    xs = mb("xs", [P, 2, C])
    xs_hi = mb("xs_hi", [P, KC, BLOCK], F32R)
    xs_lo = mb("xs_lo", [P, KC, BLOCK], F32R)
    sil = mb("sil", [P, 2, HALF])
    yo = mb("yo", [P, 2, C])
    assert moe_at["at"] <= row_end
    moe_at["at"] = at_work
    w13_hi = [mb(f"w13_hi{h}", [P, KC, 2, HALF], F32R) for h in range(2)]
    w13_lo = [mb(f"w13_lo{h}", [P, KC, 2, HALF], F32R) for h in range(2)]
    w2_hi = mb("w2_hi", [P, FCH, C], F32R)
    w2_lo = mb("w2_lo", [P, FCH, C], F32R)
    hm = mb("hm", [P, 2, FF])
    hT_hi = mb("hmT_hi", [P, 2, FCH, P], F32R)
    hT_lo = mb("hmT_lo", [P, 2, FCH, P], F32R)
    assert moe_at["at"] <= at_w13
    ya = sb("ya", [P, 2, 4, 2, C], F32, at=at_w13)
    tc = sb("tc", [P, 2, 4, C], F32, at=at_w13 + 16384)
    oc = sb("oc", [P, 2, 4, C], F32, at=at_w13 + 24576)

    sent = sem("sent")
    xs_in = sem("xs_in")
    xs_turn = sem("xs_turn")
    x_hi_ok = sem("x_hi_ok")
    x_lo_ok = sem("x_lo_ok")
    w_hi_ok = sem("w_hi_ok")
    w_lo_ok = sem("w_lo_ok")
    w2_hi_ok = sem("w2_hi_ok")
    w2_lo_ok = sem("w2_lo_ok")
    h_ps = sem("h_ps")
    silu_ok = sem("silu_ok")
    hm_ok = sem("hm_ok")
    hm_turn = sem("hm_turn")
    hT_hi_ok = sem("hT_hi_ok")
    hT_lo_ok = sem("hT_lo_ok")
    y_ps = sem("y_ps")
    y_out = sem("y_out")
    y_stored = [sem("y_stored_a"), sem("y_stored_b")]

    def dispatch_pool(pool):
        pool.wait_ge(xs_zero, 16 * GROUPS)
        pool.wait_ge(routed, 1)
        pool.wait_ge(z_copy, G1 + 2)
        for t in range(TILES):
            for k in range(2):
                pool.indirect_dma_start(xs_d, bass.IndirectOffsetOnAxis(pos[:, t, k:k + 1], 0), zall[:, t, :], None,
                                        bounds_check=MT * P - 1, oob_is_err=False).then_inc(sent, 16)

    Y_BANK = (7, 4)

    def moe_loop(eng, block):
        block(0, True, False)
        with eng.Fori(1, BLOCKS - 1) as j:
            block(j, False, False)
        block(BLOCKS - 1, False, True)

    def expert(eng, j):
        return eng.value_load(te[0:1, bass.ds(j, 1)], min_val=0, max_val=EXPERTS - 1)

    def w13_of(e, hf):
        both = W13[:, bass.ds(e, 1), :, :].rearrange("p o k (m f) -> p (o k) m f", m=2)
        return both[:, :, :, hf * HALF:hf * HALF + HALVES[hf]]

    def chunk_rows(c):
        return min(FCW, FF - c * FCW)

    def moe_sp(sp):
        for c in y_stored:
            sp.sem_inc(c, 16)
        xt, yt = tiles(xs_d), tiles(y2_d)
        sp.wait_ge(sent, 16 * SLOTS // P)

        def load(j):
            sp.dma_start(xs[:, :, :], xt[:, bass.ds(j * 2, 2), :]).then_inc(xs_in, 16)

        def store(j):
            for t in range(2):
                sp.wait_ge(y_out, j * 2 + (t + 2))
                sp.sem_inc(sp_passed, 1)
                sp.dma_start(yt[:, bass.ds(j * 2 + t, 1), :], yo[:, t, :].rearrange("p (o c) -> p o c", o=1))\
                  .then_inc(y_stored[t], 16)

        def block(j, first, last):
            if not last:
                sp.wait_ge(xs_turn, j + 1)
                sp.sem_inc(sp_passed, 1)
                load(j + 1)
            if not first:
                store(j - 1)

        load(0)
        moe_loop(sp, block)
        store(BLOCKS - 1)

    def moe_pe(pe):
        pe.sem_inc(y_ps, 1)

        def turn_x(j):
            pe.wait_ge(xs_in, j * 16 + 16)
            pe.wait_ge(y_out, j * 2 - 3 if not isinstance(j, int) or j > 1 else 1)
            for t in range(2):
                for k in range(KC):
                    ins = nc.tensor.transpose(ps[:, 4, k * BLOCK + t * P:k * BLOCK + (t + 1) * P],
                                              xs[:, t, k * P:(k + 1) * P], ident[:, :])
            ins.then_inc(xs_turn, 1)

        def hidden(j, hf, t):
            n = 2 * hf + t
            if t == 0:
                pe.wait_ge(w_lo_ok, j * 2 + (hf + 1))
            pe.wait_ge(hm_ok, j * 4 + (n + 1))
            rows = slice(t * P, (t + 1) * P)
            parts = [(x, w, k) for k in range(KC)
                     for x, w in ((xs_hi, w13_hi[hf]), (xs_hi, w13_lo[hf]), (xs_lo, w13_hi[hf]))]
            for m in range(2):
                for i, (x, w, k) in enumerate(parts):
                    ins = nc.tensor.matmul(ps[:, 2 * t + m, 0:HALVES[hf]], x[:, k, rows], w[:, k, m, 0:HALVES[hf]],
                                           start=(i == 0), stop=(i == len(parts) - 1))
            ins.then_inc(h_ps, 1)

        def turn_h(j, t):
            pe.wait_ge(hT_lo_ok, j * 2 + (t + 1))
            pe.wait_ge(hm_ok, j * 4 + (t + 5))
            for c in range(FCH):
                w = chunk_rows(c)
                ins = nc.tensor.transpose(ps[0:w, 5 + c // 4, (c % 4) * P:(c % 4 + 1) * P],
                                          hm[:, t, c * FCW:c * FCW + w], ident[:, :])
            ins.then_inc(hm_turn, 1)

        def down(j, t, last=False):
            pe.wait_ge(hT_lo_ok, j * 2 + (t + 2))
            pe.wait_ge(w2_lo_ok, j + 1)
            if t == 1:
                pe.wait_ge(x_lo_ok, j + 3 if not last else j + 1)
            parts = [(h, w, c) for c in range(FCH) for h, w in ((hT_hi, w2_hi), (hT_hi, w2_lo), (hT_lo, w2_hi))]
            for i, (h, w, c) in enumerate(parts):
                r = chunk_rows(c)
                ins = nc.tensor.matmul(ps[:, Y_BANK[t], 0:C], h[0:r, t, c, :], w[0:r, c, :],
                                       start=(i == 0), stop=(i == len(parts) - 1))
            ins.then_inc(y_ps, 1)

        def block(j, first, last):
            pe.wait_ge(x_lo_ok, j + 1)
            for hf in range(2):
                for t in range(2):
                    hidden(j, hf, t)
            if not last:
                turn_x(j + 1)
            for t in range(2):
                if not first:
                    down(j - 1, t, last)
                turn_h(j, t)

        turn_x(0)
        moe_loop(pe, block)
        for t in range(2):
            down(BLOCKS - 1, t, True)

    def moe_act(act):
        def high_w(e, hf):
            nc.scalar.activation(w13_hi[hf][:, :, :, 0:HALVES[hf]], w13_of(e, hf), ACT.Copy).then_inc(w_hi_ok, 1)

        def high_x(j):
            act.wait_ge(xs_turn, j + 1)
            nc.scalar.activation(xs_hi[:, :, :].rearrange("p k n -> p (k n)"), ps[:, 4, :], ACT.Copy).then_inc(x_hi_ok, 1)

        def gate_half(j, hf, t):
            n = 2 * hf + t
            act.wait_ge(h_ps, j * 4 + (n + 1))
            act.wait_ge(hm_ok, j * 4 + (n + 1))
            nc.scalar.activation(sil[:, t, 0:HALVES[hf]], ps[:, 2 * t, 0:HALVES[hf]], ACT.Silu).then_inc(silu_ok, 1)

        def high_h(j, t):
            act.wait_ge(hm_turn, j * 2 + (t + 1))
            r = chunk_rows(FCH - 1)
            nc.scalar.activation(hT_hi[0:FCW, t, 0:4, :].rearrange("p k n -> p (k n)"), ps[0:FCW, 5, :], ACT.Copy)
            nc.scalar.activation(hT_hi[0:FCW, t, 4, :], ps[0:FCW, 6, 0:P], ACT.Copy)
            nc.scalar.activation(hT_hi[0:r, t, 5, :], ps[0:r, 6, P:2 * P], ACT.Copy).then_inc(hT_hi_ok, 1)

        def high_w2(j):
            d = expert(act, j)
            act.wait_ge(w2_in, 16 * EXPERTS // 2)
            act.wait_ge(y_ps, j * 2 + 1)
            nc.scalar.activation(w2_hi[0:FCW, :, :], W2[0:FCW, bass.ds(d, 1), :, :].rearrange("p o c n -> p (o c) n"),
                                 ACT.Copy).then_inc(w2_hi_ok, 1)

        def block(j, first, last):
            if not first:
                high_w2(j - 1)
            for t in range(2):
                gate_half(j, 0, t)
            if not last:
                e = expert(act, j + 1)
                high_w(e, 0)
            for t in range(2):
                gate_half(j, 1, t)
            if not last:
                high_x(j + 1)
            high_h(j, 0)
            if not last:
                high_w(e, 1)
            high_h(j, 1)

        act.wait_ge(w13_in, 16 * EXPERTS // 2)
        act.wait_ge(routed, 1)
        e = expert(act, 0)
        for hf in range(2):
            high_w(e, hf)
        high_x(0)
        moe_loop(act, block)
        high_w2(BLOCKS - 1)

    def moe_dve(dve):
        dve.sem_inc(hm_ok, 2)
        dve.sem_inc(hT_lo_ok, 1)
        dve.sem_inc(y_out, 1)

        def low_w(e, j, hf):
            dve.wait_ge(w_hi_ok, j * 2 + (hf + 1))
            n = HALVES[hf]
            nc.vector.tensor_tensor(w13_lo[hf][:, :, :, 0:n], w13_of(e, hf), w13_hi[hf][:, :, :, 0:n].bitcast(F32),
                                    ALU.subtract).then_inc(w_lo_ok, 1)

        def low_x(j):
            dve.wait_ge(x_hi_ok, j + 1)
            nc.vector.tensor_tensor(xs_lo[:, :, :].rearrange("p k n -> p (k n)"), ps[:, 4, :],
                                    xs_hi[:, :, :].rearrange("p k n -> p (k n)").bitcast(F32), ALU.subtract)\
              .then_inc(x_lo_ok, 1)

        def times(j, hf, t, first):
            dve.wait_ge(silu_ok, j * 4 + (2 * hf + t + 1))
            if hf == 0 and not first:
                dve.wait_ge(hm_turn, j * 2 + (t - 1))
            n = HALVES[hf]
            nc.vector.tensor_tensor(hm[:, t, hf * HALF:hf * HALF + n], sil[:, t, 0:n], ps[:, 2 * t + 1, 0:n], ALU.mult).then_inc(hm_ok, 1)

        def low_h(j, t):
            dve.wait_ge(hT_hi_ok, j * 2 + (t + 1))
            r = chunk_rows(FCH - 1)
            nc.vector.tensor_tensor(hT_lo[0:FCW, t, 0:4, :].rearrange("p k n -> p (k n)"), ps[0:FCW, 5, :],
                                    hT_hi[0:FCW, t, 0:4, :].rearrange("p k n -> p (k n)").bitcast(F32), ALU.subtract)
            nc.vector.tensor_tensor(hT_lo[0:FCW, t, 4, :], ps[0:FCW, 6, 0:P], hT_hi[0:FCW, t, 4, :].bitcast(F32),
                                    ALU.subtract)
            nc.vector.tensor_tensor(hT_lo[0:r, t, 5, :], ps[0:r, 6, P:2 * P], hT_hi[0:r, t, 5, :].bitcast(F32),
                                    ALU.subtract).then_inc(hT_lo_ok, 1)

        def bring_y(j, t):
            dve.wait_ge(y_ps, j * 2 + (t + 2))
            dve.wait_ge(y_stored[t], j * 16 + 16)
            nc.vector.tensor_copy(yo[:, t, :], ps[:, Y_BANK[t], 0:C]).then_inc(y_out, 1)

        def low_w2(j):
            d = expert(dve, j)
            dve.wait_ge(w2_hi_ok, j + 1)
            nc.vector.tensor_tensor(w2_lo[0:FCW, :, :], W2[0:FCW, bass.ds(d, 1), :, :].rearrange("p o c n -> p (o c) n"),
                                    w2_hi[0:FCW, :, :].bitcast(F32), ALU.subtract).then_inc(w2_lo_ok, 1)

        def block(j, first, last):
            for t in range(2):
                times(j, 0, t, first)
            if not first:
                low_w2(j - 1)
            for t in range(2):
                times(j, 1, t, first)
            if not last:
                low_x(j + 1)
                e = expert(dve, j + 1)
                low_w(e, j + 1, 0)
            if not first:
                bring_y(j - 1, 0)
            low_h(j, 0)
            if not first:
                bring_y(j - 1, 1)
            if not last:
                low_w(e, j + 1, 1)
            low_h(j, 1)

        e = expert(dve, 0)
        low_w(e, 0, 0)
        dve.wait_ge(sent, 16 * SLOTS // P)
        low_w(e, 0, 1)
        low_x(0)
        moe_loop(dve, block)
        low_w2(BLOCKS - 1)
        for t in range(2):
            bring_y(BLOCKS - 1, t)

    back = [sem("back_a"), sem("back_b")]
    tc_in = [sem("tc_in_a"), sem("tc_in_b")]
    mixed = sem("mixed")
    out_stored = [sem("out_stored_a"), sem("out_stored_b")]

    def combine_pool(pool):
        for c in y_stored:
            pool.wait_ge(c, 16 * BLOCKS + 16)
        pool.wait_ge(y_ps, MT + 1)

        for g in range(G1):
            if g >= 2:
                pool.wait_ge(mixed, g)
            for t in range(4):
                for k in range(2):
                    pool.indirect_dma_start(ya[:, g % 2, t, k, :], None, y2_d,
                                            bass.IndirectOffsetOnAxis(pos[:, g * 4 + t, k:k + 1], 0),
                                            bounds_check=MT * P - 1, oob_is_err=False).then_inc(back[g % 2], 16)

    def combine_sp(sp):
        for c in out_stored:
            sp.sem_inc(c, 16)
        sp.wait_ge(y_ps, MT + 1)
        t2, o = tiles(t2_d), tiles(out.rearrange("b h w c -> (b h w) c"))

        def load(g, u):
            sp.dma_start(tc[:, u, :, :], t2[:, bass.ds(g * 4, 4), :]).then_inc(tc_in[u], 16)

        load(0, 0)
        load(1, 1)

        def store(g, u):
            sp.wait_ge(mixed, g + 2)
            sp.sem_inc(sp_passed, 1)
            sp.dma_start(o[:, bass.ds(g * 4, 4), :], oc[:, u, :, :]).then_inc(out_stored[u], 16)

        with sp.Fori(0, G1 // 2 - 1) as i:
            for u in range(2):
                store(i * 2 + u, u)
                load(i * 2 + (u + 2), u)
        for u in range(2):
            store(G1 - 2 + u, u)
        for c in out_stored:
            sp.wait_ge(c, 16 * G1 // 2 + 16)

    def combine_dve(dve):
        dve.sem_inc(mixed, 1)
        with dve.Fori(0, G1 // 2) as i:
            for u in range(2):
                relink()
                dve.wait_ge(tc_in[u], i * 16 + 16)
                dve.wait_ge(back[u], i * 128 + 128)
                dve.wait_ge(out_stored[u], i * 16 + 16)
                for k in range(2):
                    for t in range(4):
                        ins = nc.vector.scalar_tensor_tensor(
                            oc[:, u, t, :], ya[:, u, t, k, :], gate[:, k, bass.ds(i * 8 + u * 4 + t, 1)],
                            (tc if k == 0 else oc)[:, u, t, :], ALU.mult, ALU.add)
                    if k == 0:
                        link(ins)
                ins.then_inc(mixed, 1)

    block = ctx.enter_context(nc.Block())

    @block.sync
    def _(sp):
        prep_sp(sp)
        att0.sp(sp, lambda: later_weights(sp))
        mlp_sp(sp)
        for c in m_stored:
            sp.wait_ge(c, 16 * GROUPS // 2 + 16)
        att1.sp(sp)
        m1_sp(sp)
        moe_sp(sp)
        combine_sp(sp)

    @block.gpsimd
    def _(pool):
        prep_pool(pool)
        bias_pool(pool)
        scatter_pool(pool)
        mask_pool(pool)
        att1.pool(pool)
        m1_pool(pool)
        dispatch_pool(pool)
        combine_pool(pool)

    @block.tensor
    def _(pe):
        pe.wait_ge(prep_p, 4)
        pe.wait_ge(prep_v, 1)
        att0.pe(pe)
        mlp_pe(pe)
        att1.pe(pe)
        m1_pe(pe)
        moe_pe(pe)

    @block.scalar
    def _(act):
        act.wait_ge(prep_v, 1)
        att0.act(act)
        mlp_act(act)
        att1.act(act)
        m1_act(act)
        moe_act(act)

    @block.vector
    def _(dve):
        prep_dve(dve)
        for s in range(att0.NORM_STEPS):
            att0.normal(dve, 0, s)
        att0.dve(dve)
        mlp_dve(dve)
        att1.dve(dve)
        m1_dve(dve)
        moe_dve(dve)
        combine_dve(dve)


def layout(inputs):
    f = {k: np.asarray(v) for k, v in inputs.items()}
    two = lambda v: v.reshape(-1, P).T
    cols = np.concatenate([two(f["L0_conv_norm1_w"]), two(f["L0_conv_norm1_b"]), two(f["L0_conv_norm2_w"]),
                           two(f["L0_conv_norm2_b"]), two(f["L0_conv_qkv_b"][0:C]), two(f["L0_conv_qkv_b"][C:2 * C]),
                           two(f["L0_conv_fc1_b"]), two(f["L1_attn_bq"]), two(f["L1_attn_bk"])], axis=1)
    rows = np.stack([f["L0_conv_qkv_b"][2 * C:], f["L0_conv_proj_b"], f["L0_conv_gamma_1"][4], f["L0_conv_fc2_b"],
                     f["L0_conv_gamma_2"][4], f["L1_attn_bv"], f["L1_attn_bo"], f["L1_attn_gamma"], f["L1_attn_beta"]])
    rpb = np.pad(f["L0_conv_rpb"].transpose(1, 0, 2), ((0, 0), (0, 0), (SIDE, SIDE - 1)))
    toeplitz = np.stack([rpb[:, :, 38 - j:70 - j] for j in range(SIDE)]).reshape(SIDE, -1)
    shut = np.full((3, ROWS, SIDE, WT * ROWS, SIDE), BIG, np.float32)
    for kind, (row0, key0) in enumerate(((0, 0), (2 * ROWS, ROWS), (SIDE - ROWS, SIDE - WT * ROWS))):
        for i in range(ROWS):
            for j in range(SIDE):
                a = min(max(row0 + i - KWIN // 2, 0), SIDE - KWIN) - key0
                b = min(max(j - KWIN // 2, 0), SIDE - KWIN)
                shut[kind, i, j, a:a + KWIN, b:b + KWIN] = 0.0
    shut = shut.reshape(3, P, WK).transpose(1, 0, 2)
    w13 = np.concatenate([f["L1_ffn_w1"], f["L1_ffn_w3"]], axis=1).transpose(0, 2, 1)
    route_const = np.zeros((P, EXPERTS + 2 * P + BLOCKS), np.float32)
    route_const[:, 0:EXPERTS] = np.arange(EXPERTS) - EXPERTS
    route_const[:, EXPERTS:EXPERTS + P] = np.triu(np.ones((P, P)), 1)
    route_const[:, EXPERTS + P:EXPERTS + 2 * P] = 1.0
    route_const[:, EXPERTS + 2 * P:] = np.arange(BLOCKS)
    return {
        "x": f["x"].reshape(TOK, C), "rpb_toeplitz": toeplitz, "window_mask": shut, "cols": cols, "rows": rows,
        "w_qkv0": f["L0_conv_qkv_w"].T, "w_proj0": f["L0_conv_proj_w"].T, "w_fc1": f["L0_conv_fc1_w"].T,
        "w_fc2": f["L0_conv_fc2_w"].T,
        "w_qkv1": np.concatenate([f["L1_attn_Wq"], f["L1_attn_Wk"], f["L1_attn_Wv"]], axis=1),
        "w_o1": f["L1_attn_Wo"], "w_router": f["L1_ffn_router_w"].T, "edges": f["L1_attn_edge_index"],
        "w13": w13, "w2": np.pad(f["L1_ffn_w2"].transpose(0, 2, 1), ((0, 0), (0, FCH * FCW - FF), (0, 0))),
        "route_const": route_const,
    }


def kernel(**inputs):
    import concourse.bacc as bacc
    from concourse.bass_utils import run_bass_kernel_spmd

    arrays = {name: np.ascontiguousarray(a) for name, a in layout(inputs).items()}
    nc = bacc.Bacc("TRN2", target_bir_lowering=False, num_devices=1)
    args = [nc.dram_tensor(f"in_{name}_dram", a.shape, mybir.dt.from_np(a.dtype), kind="ExternalInput").ap()
            for name, a in arrays.items()]
    out = nc.dram_tensor("out_0_dram", (BATCH, SIDE, SIDE, C), F32, kind="ExternalOutput").ap()
    build_program(nc, *args, out)
    if not nc.is_finalized():
        nc.finalize()
    r = run_bass_kernel_spmd(nc, [{f"in_{name}_dram": a for name, a in arrays.items()}], core_ids=[0])
    return r.results[0]["out_0_dram"]
```
